# Optimizing a Trainium2 kernel written in Bass

```python
import numpy as np
import jax
import jax.numpy as jnp

def _softmax(x, axis=-1):
    return jax.nn.softmax(x, axis=axis)

def _gelu(x):
    return jax.nn.gelu(x, approximate=True)

def _silu(x):
    return jax.nn.silu(x)

def _sigmoid(x):
    return jax.nn.sigmoid(x)

def _layernorm(x, axis=-1, eps=1e-05):
    m = jnp.mean(x, axis=axis, keepdims=True)
    v = jnp.var(x, axis=axis, keepdims=True)
    return (x - m) / jnp.sqrt(v + eps)

def _scatter_add(tgt, idx, src, axis=0):
    return tgt.at[idx].add(src)

def _segment_sum(src, seg, n):
    return jax.ops.segment_sum(src, seg, n)
kernel_name = 'mk_xattn_ffn_d2_seqx_r8_6feb72'

def setup_inputs(seed: int=0):
    np.random.seed(seed)
    _w = jnp.asarray

    def _rec_inputs():
        import jax
        import jax.numpy as jnp
        _rk = jax.random.key(seed)
        x = 7.22e-05 + 1 * jax.random.normal(jax.random.fold_in(_rk, 1), (2, 512, 128), jnp.float32)
        _lenS = 512 - jax.random.randint(jax.random.fold_in(_rk, 7), (2,), 0, max(1, 512 // 4) + 1, jnp.int32)
        _lenS2 = 77 - jax.random.randint(jax.random.fold_in(_rk, 8), (2,), 0, max(1, 77 // 4) + 1, jnp.int32)
        _ctx_1024P = jax.random.normal(jax.random.fold_in(_rk, 11), (2, 16, 128), jnp.float32)
        _ctx_1024c = jax.random.dirichlet(jax.random.fold_in(_rk, 511), 0.3 * jnp.ones((16,), jnp.float32), (2, 77))
        _ctx_1024t = jnp.einsum('bsk,bkd->bsd', _ctx_1024c, _ctx_1024P)
        _ctx_1024t = _ctx_1024t * jax.lax.rsqrt(jnp.mean(jnp.square(_ctx_1024t)) + 1e-12) * 0.953939
        ctx_1024 = 4.13588e-05 + 0.999923 * (_ctx_1024t + 0.3 * jax.random.normal(jax.random.fold_in(_rk, 611), (2, 77, 128), jnp.float32))
        return (x, ctx_1024)
    x, ctx_1024 = _rec_inputs()

    def _L0_xattn_setup():
        import jax, jax.numpy as jnp
        import numpy as np
        B, N, E = (4, 256, 128)
        H = 16
        D = E
        HD = D // H
        key = jax.random.key(seed)
        ks = jax.random.split(key, 11)
        s = 0.02
        return {'q': jax.random.normal(ks[0], (B, N, E), jnp.float32), 'k': jax.random.normal(ks[1], (B, N, E), jnp.float32), 'v': jax.random.normal(ks[2], (B, N, E), jnp.float32), 'Wq': jax.random.normal(ks[3], (E, D), jnp.float32) * s, 'bq': jnp.zeros((D,), jnp.float32), 'Wk': jax.random.normal(ks[4], (E, D), jnp.float32) * s, 'bk': jnp.zeros((D,), jnp.float32), 'Wv': jax.random.normal(ks[5], (E, D), jnp.float32) * s, 'bv': jnp.zeros((D,), jnp.float32), 'Wo': jax.random.normal(ks[6], (D, E), jnp.float32) * s, 'bo': jnp.zeros((E,), jnp.float32)}
    _L0_xattn_all = _L0_xattn_setup()
    _L0_xattn_in = {k: v for k, v in _L0_xattn_all.items() if k in ('Wq', 'bq', 'Wk', 'bk', 'Wv', 'bv', 'Wo', 'bo')}
    del _L0_xattn_all

    def _L0_ffn_setup():
        import jax, jax.numpy as jnp
        import numpy as np
        B, T, D, E, H, K = (4, 256, 128, 8, 256, 2)
        key = jax.random.key(seed)
        k0, k1, k2, k3 = jax.random.split(key, 4)
        x = jax.random.normal(k0, (B, T, D), dtype=jnp.float32)
        router_w = jax.random.normal(k1, (E, D), dtype=jnp.float32) * D ** (-0.5)
        w1 = jax.random.normal(k2, (E, D, H), dtype=jnp.float32) * D ** (-0.5)
        w2 = jax.random.normal(k3, (E, H, D), dtype=jnp.float32) * H ** (-0.5)
        return {'x': x, 'router_w': router_w, 'w1': w1, 'w2': w2}
    _L0_ffn_all = _L0_ffn_setup()
    _L0_ffn_in = {k: v for k, v in _L0_ffn_all.items() if k in ('router_w', 'w1', 'w2')}
    del _L0_ffn_all

    def _L1_xattn_setup():
        import jax, jax.numpy as jnp
        import numpy as np
        NUM_HEADS = 16
        D_MODEL = 128
        LN_EPS = 1e-05
        key = jax.random.key(seed)
        ks = jax.random.split(key, 10)
        B, S, D = (2, 256, D_MODEL)
        s = 1.0 / np.sqrt(D)
        return {'encoded': jax.random.normal(ks[0], (B, S, D), jnp.float32), 'decoded': jax.random.normal(ks[1], (B, S, D), jnp.float32), 'Wq': jax.random.normal(ks[2], (D, D), jnp.float32) * s, 'bq': jax.random.normal(ks[3], (D,), jnp.float32) * s, 'Wk': jax.random.normal(ks[4], (D, D), jnp.float32) * s, 'bk': jax.random.normal(ks[5], (D,), jnp.float32) * s, 'Wv': jax.random.normal(ks[6], (D, D), jnp.float32) * s, 'bv': jax.random.normal(ks[7], (D,), jnp.float32) * s, 'gamma': jnp.ones((D,), jnp.float32), 'beta': jnp.zeros((D,), jnp.float32)}
    _L1_xattn_all = _L1_xattn_setup()
    _L1_xattn_in = {k: v for k, v in _L1_xattn_all.items() if k in ('Wq', 'bq', 'Wk', 'bk', 'Wv', 'bv', 'gamma', 'beta')}
    del _L1_xattn_all

    def _L1_ffn_setup():
        import jax, jax.numpy as jnp
        import numpy as np
        D = 128
        H = 16
        DH = D // H
        DC = D // 4
        HID = 256
        G = 2
        EPG = 4
        E = G * EPG
        TOPK = 2
        EPS = 1e-06
        B, T = (2, 256)

        def _rope_sincos(t, dh):
            inv_freq = 1.0 / 10000.0 ** (jnp.arange(0, dh, 2, dtype=jnp.float32) / dh)
            ang = jnp.arange(t, dtype=jnp.float32)[:, None] * inv_freq[None, :]
            return (jnp.sin(ang), jnp.cos(ang))

        def _apply_rope(x, sin, cos):
            x1 = x[..., ::2]
            x2 = x[..., 1::2]
            r = jnp.stack([x1 * cos - x2 * sin, x1 * sin + x2 * cos], axis=-1)
            return r.reshape(x.shape)

        def _swiglu(x):
            a, b = jnp.split(x, 2, axis=-1)
            return jax.nn.silu(a) * b

        def _rmsnorm(x, w):
            return x * jax.lax.rsqrt(jnp.mean(x * x, axis=-1, keepdims=True) + EPS) * w
        key = jax.random.key(seed)
        ks = jax.random.split(key, 14)
        s = 0.02
        return {'src': jax.random.normal(ks[0], (B, T, D), jnp.float32), 'Wq': jax.random.normal(ks[1], (D, D), jnp.float32) * s, 'Wk_c': jax.random.normal(ks[2], (D, DC), jnp.float32) * s, 'Wv_c': jax.random.normal(ks[3], (D, DC), jnp.float32) * s, 'Wk': jax.random.normal(ks[4], (DC, D), jnp.float32) * s, 'Wv': jax.random.normal(ks[5], (DC, D), jnp.float32) * s, 'Wo': jax.random.normal(ks[6], (D, D), jnp.float32) * s, 'W_shared_in': jax.random.normal(ks[7], (D, 2 * HID), jnp.float32) * s, 'W_shared_out': jax.random.normal(ks[8], (HID, D), jnp.float32) * s, 'W1_shared': jax.random.normal(ks[9], (D, 2 * HID), jnp.float32) * s, 'W2_experts': jax.random.normal(ks[10], (E, HID, D), jnp.float32) * s, 'Wg_gate': jax.random.normal(ks[11], (D, G), jnp.float32) * s, 'We_gate': jax.random.normal(ks[12], (D, E), jnp.float32) * s, 'group_bias': jnp.zeros((G,), jnp.float32), 'expert_bias': jnp.zeros((E,), jnp.float32), 'norm1_w': jnp.ones((D,), jnp.float32), 'norm2_w': jnp.ones((D,), jnp.float32)}
    _L1_ffn_all = _L1_ffn_setup()
    _L1_ffn_in = {k: v for k, v in _L1_ffn_all.items() if k in ('Wq', 'Wk_c', 'Wv_c', 'Wk', 'Wv', 'Wo', 'W_shared_in', 'W_shared_out', 'W1_shared', 'W2_experts', 'Wg_gate', 'We_gate', 'group_bias', 'expert_bias', 'norm1_w', 'norm2_w')}
    del _L1_ffn_all
    return {'x': x, 'ctx_1024': ctx_1024, 'L0_xattn_Wq': _L0_xattn_in['Wq'], 'L0_xattn_bq': _L0_xattn_in['bq'], 'L0_xattn_Wk': _L0_xattn_in['Wk'], 'L0_xattn_bk': _L0_xattn_in['bk'], 'L0_xattn_Wv': _L0_xattn_in['Wv'], 'L0_xattn_bv': _L0_xattn_in['bv'], 'L0_xattn_Wo': _L0_xattn_in['Wo'], 'L0_xattn_bo': _L0_xattn_in['bo'], 'L0_ffn_router_w': _L0_ffn_in['router_w'], 'L0_ffn_w1': _L0_ffn_in['w1'], 'L0_ffn_w2': _L0_ffn_in['w2'], 'L1_xattn_Wq': _L1_xattn_in['Wq'], 'L1_xattn_bq': _L1_xattn_in['bq'], 'L1_xattn_Wk': _L1_xattn_in['Wk'], 'L1_xattn_bk': _L1_xattn_in['bk'], 'L1_xattn_Wv': _L1_xattn_in['Wv'], 'L1_xattn_bv': _L1_xattn_in['bv'], 'L1_xattn_gamma': _L1_xattn_in['gamma'], 'L1_xattn_beta': _L1_xattn_in['beta'], 'L1_ffn_Wq': _L1_ffn_in['Wq'], 'L1_ffn_Wk_c': _L1_ffn_in['Wk_c'], 'L1_ffn_Wv_c': _L1_ffn_in['Wv_c'], 'L1_ffn_Wk': _L1_ffn_in['Wk'], 'L1_ffn_Wv': _L1_ffn_in['Wv'], 'L1_ffn_Wo': _L1_ffn_in['Wo'], 'L1_ffn_W_shared_in': _L1_ffn_in['W_shared_in'], 'L1_ffn_W_shared_out': _L1_ffn_in['W_shared_out'], 'L1_ffn_W1_shared': _L1_ffn_in['W1_shared'], 'L1_ffn_W2_experts': _L1_ffn_in['W2_experts'], 'L1_ffn_Wg_gate': _L1_ffn_in['Wg_gate'], 'L1_ffn_We_gate': _L1_ffn_in['We_gate'], 'L1_ffn_group_bias': _L1_ffn_in['group_bias'], 'L1_ffn_expert_bias': _L1_ffn_in['expert_bias'], 'L1_ffn_norm1_w': _L1_ffn_in['norm1_w'], 'L1_ffn_norm2_w': _L1_ffn_in['norm2_w']}

def reference(x, ctx_1024, L0_xattn_Wq, L0_xattn_bq, L0_xattn_Wk, L0_xattn_bk, L0_xattn_Wv, L0_xattn_bv, L0_xattn_Wo, L0_xattn_bo, L0_ffn_router_w, L0_ffn_w1, L0_ffn_w2, L1_xattn_Wq, L1_xattn_bq, L1_xattn_Wk, L1_xattn_bk, L1_xattn_Wv, L1_xattn_bv, L1_xattn_gamma, L1_xattn_beta, L1_ffn_Wq, L1_ffn_Wk_c, L1_ffn_Wv_c, L1_ffn_Wk, L1_ffn_Wv, L1_ffn_Wo, L1_ffn_W_shared_in, L1_ffn_W_shared_out, L1_ffn_W1_shared, L1_ffn_W2_experts, L1_ffn_Wg_gate, L1_ffn_We_gate, L1_ffn_group_bias, L1_ffn_expert_bias, L1_ffn_norm1_w, L1_ffn_norm2_w):
    import jax
    import jax.numpy as jnp

    def _L0_xattn_ref(q, k, v, Wq, bq, Wk, bk, Wv, bv, Wo, bo):
        import jax, jax.numpy as jnp
        import numpy as np
        B, N, E = (4, 256, 128)
        H = 16
        D = E
        HD = D // H
        qp = q @ Wq + bq
        kp = k @ Wk + bk
        vp = v @ Wv + bv

        def split(x):
            b, n, _ = x.shape
            return x.reshape(b, n, H, HD).transpose(0, 2, 1, 3)
        qh, kh, vh = (split(qp), split(kp), split(vp))
        scale = 1.0 / jnp.sqrt(jnp.asarray(HD, qh.dtype))
        attn = jnp.einsum('bhqd,bhkd->bhqk', qh, kh) * scale
        attn = jax.nn.softmax(attn, axis=-1)
        out = jnp.einsum('bhqk,bhkd->bhqd', attn, vh)
        b, h, n, hd = out.shape
        out = out.transpose(0, 2, 1, 3).reshape(b, n, h * hd)
        return out @ Wo + bo

    def _L0_ffn_ref(x, router_w, w1, w2):
        import jax, jax.numpy as jnp
        import numpy as np
        B, T, D, E, H, K = (4, 256, 128, 8, 256, 2)
        Bb, Tt, Dd = x.shape
        N = Bb * Tt
        logits = jnp.einsum('btd,ed->bte', x, router_w)
        top_vals, top_idx = jax.lax.top_k(logits, K)
        top_w = jax.nn.softmax(top_vals, axis=-1)
        xf = x.reshape(N, Dd)
        h = jnp.einsum('nd,edh->enh', xf, w1)
        h = jnp.square(jax.nn.relu(h))
        y = jnp.einsum('enh,ehd->end', h, w2)
        idx_f = top_idx.reshape(N, K)
        w_f = top_w.reshape(N, K)
        y_sel = y[idx_f, jnp.arange(N)[:, None]]
        out = jnp.einsum('nk,nkd->nd', w_f, y_sel)
        return out.reshape(Bb, Tt, Dd)

    def _L1_xattn_ref(encoded, decoded, Wq, bq, Wk, bk, Wv, bv, gamma, beta):
        import jax, jax.numpy as jnp
        import numpy as np
        NUM_HEADS = 16
        D_MODEL = 128
        LN_EPS = 1e-05
        B, Sq, D = decoded.shape
        H = NUM_HEADS
        dh = D // H
        q = decoded @ Wq.T + bq
        k = encoded @ Wk.T + bk
        v = encoded @ Wv.T + bv
        q = q.reshape(B, Sq, H, dh).transpose(0, 2, 1, 3)
        k = k.reshape(B, -1, H, dh).transpose(0, 2, 1, 3)
        v = v.reshape(B, -1, H, dh).transpose(0, 2, 1, 3)
        qk = jnp.einsum('bhqd,bhkd->bhqk', q, k)
        qk = jnp.where(jnp.isnan(qk), -jnp.inf, qk)
        attn = jax.nn.softmax(qk, axis=-1)
        attn = jnp.where(jnp.isnan(attn), 0.0, attn)
        v = jnp.where(jnp.isnan(v), 0.0, v)
        z = jnp.einsum('bhqk,bhkd->bhqd', attn, v)
        z = z.reshape(B, Sq, D)
        x = z + decoded
        mu = jnp.mean(x, axis=-1, keepdims=True)
        var = jnp.var(x, axis=-1, keepdims=True)
        return (x - mu) * jax.lax.rsqrt(var + LN_EPS) * gamma + beta

    def _L1_ffn_ref(src, Wq, Wk_c, Wv_c, Wk, Wv, Wo, W_shared_in, W_shared_out, W1_shared, W2_experts, Wg_gate, We_gate, group_bias, expert_bias, norm1_w, norm2_w):
        import jax, jax.numpy as jnp
        import numpy as np
        D = 128
        H = 16
        DH = D // H
        DC = D // 4
        HID = 256
        G = 2
        EPG = 4
        E = G * EPG
        TOPK = 2
        EPS = 1e-06
        B, T = (2, 256)

        def _rope_sincos(t, dh):
            inv_freq = 1.0 / 10000.0 ** (jnp.arange(0, dh, 2, dtype=jnp.float32) / dh)
            ang = jnp.arange(t, dtype=jnp.float32)[:, None] * inv_freq[None, :]
            return (jnp.sin(ang), jnp.cos(ang))

        def _apply_rope(x, sin, cos):
            x1 = x[..., ::2]
            x2 = x[..., 1::2]
            r = jnp.stack([x1 * cos - x2 * sin, x1 * sin + x2 * cos], axis=-1)
            return r.reshape(x.shape)

        def _swiglu(x):
            a, b = jnp.split(x, 2, axis=-1)
            return jax.nn.silu(a) * b

        def _rmsnorm(x, w):
            return x * jax.lax.rsqrt(jnp.mean(x * x, axis=-1, keepdims=True) + EPS) * w
        Bb, Tt, C = src.shape
        q = (src @ Wq).reshape(Bb, Tt, H, DH).transpose(0, 2, 1, 3)
        k = (src @ Wk_c @ Wk).reshape(Bb, Tt, H, DH).transpose(0, 2, 1, 3)
        v = (src @ Wv_c @ Wv).reshape(Bb, Tt, H, DH).transpose(0, 2, 1, 3)
        sin, cos = _rope_sincos(Tt, DH)
        q = _apply_rope(q, sin, cos)
        k = _apply_rope(k, sin, cos)
        attn = jnp.einsum('bhqd,bhkd->bhqk', q, k) / np.sqrt(DH).astype(np.float32)
        attn = jax.nn.softmax(attn, axis=-1)
        sa = jnp.einsum('bhqk,bhkd->bhqd', attn, v)
        sa = sa.transpose(0, 2, 1, 3).reshape(Bb, Tt, C) @ Wo
        x = _rmsnorm(src + sa, norm1_w)
        S = Bb * Tt
        flat = x.reshape(S, C)
        shared = _swiglu(flat @ W_shared_in) @ W_shared_out
        g_probs = jax.nn.softmax(flat @ Wg_gate + group_bias, -1)
        g_idx = jnp.argmax(g_probs, axis=-1)
        e_logits = flat @ We_gate + expert_bias
        e_group = jnp.arange(E) // EPG
        in_group = e_group[None, :] == g_idx[:, None]
        e_probs = jax.nn.softmax(jnp.where(in_group, e_logits, -jnp.inf), -1)
        g_prob = jnp.take_along_axis(g_probs, g_idx[:, None], axis=1)
        p_expert = e_probs * g_prob
        topv, topi = jax.lax.top_k(p_expert, TOPK)
        w = jnp.zeros((S, E), flat.dtype).at[jnp.arange(S)[:, None], topi].set(topv)
        h = _swiglu(flat @ W1_shared)
        routed = jnp.zeros_like(shared)
        for e in range(E):
            routed = routed + h @ W2_experts[e] * w[:, e:e + 1]
        out = x + (shared + routed).reshape(Bb, Tt, C)
        return _rmsnorm(out, norm2_w)
    x = x + _L0_xattn_ref(_layernorm(x, axis=-1), ctx_1024, ctx_1024, L0_xattn_Wq, L0_xattn_bq, L0_xattn_Wk, L0_xattn_bk, L0_xattn_Wv, L0_xattn_bv, L0_xattn_Wo, L0_xattn_bo)
    x = x + _L0_ffn_ref(_layernorm(x, axis=-1), L0_ffn_router_w, L0_ffn_w1, L0_ffn_w2)
    x = x + _L1_xattn_ref(ctx_1024, _layernorm(x, axis=-1), L1_xattn_Wq, L1_xattn_bq, L1_xattn_Wk, L1_xattn_bk, L1_xattn_Wv, L1_xattn_bv, L1_xattn_gamma, L1_xattn_beta)
    x = x + _L1_ffn_ref(_layernorm(x, axis=-1), L1_ffn_Wq, L1_ffn_Wk_c, L1_ffn_Wv_c, L1_ffn_Wk, L1_ffn_Wv, L1_ffn_Wo, L1_ffn_W_shared_in, L1_ffn_W_shared_out, L1_ffn_W1_shared, L1_ffn_W2_experts, L1_ffn_Wg_gate, L1_ffn_We_gate, L1_ffn_group_bias, L1_ffn_expert_bias, L1_ffn_norm1_w, L1_ffn_norm2_w)
    return x

_drawn_inputs = setup_inputs


def setup_inputs(seed=0):
    import zlib

    import numpy as np

    out = dict(_drawn_inputs(seed))
    spreads = {'L0_xattn_bq': (0.0, 0.8),
     'L0_xattn_bk': (0.0, 0.8),
     'L0_xattn_bv': (0.0, 0.1),
     'L0_xattn_bo': (0.0, 0.1),
     'L1_xattn_gamma': (1.0, 0.2),
     'L1_xattn_beta': (0.0, 0.1),
     'L1_ffn_group_bias': (0.0, 0.8),
     'L1_ffn_expert_bias': (0.0, 0.8),
     'L1_ffn_norm1_w': (1.0, 0.2),
     'L1_ffn_norm2_w': (1.0, 0.2)}
    factors = {'L0_xattn_Wq': 2.828,
     'L0_xattn_Wk': 2.829,
     'L1_xattn_bk': 8.0,
     'L1_ffn_Wq': 8.0,
     'L1_ffn_Wk_c': 8.0,
     'L1_ffn_Wv_c': 8.0,
     'L1_ffn_Wk': 8.0,
     'L1_ffn_Wv': 8.0,
     'L1_ffn_Wo': 8.0,
     'L1_ffn_W_shared_in': 8.0,
     'L1_ffn_W_shared_out': 8.0,
     'L1_ffn_W1_shared': 8.0,
     'L1_ffn_W2_experts': 8.0,
     'L1_ffn_Wg_gate': 8.0,
     'L1_ffn_We_gate': 8.0}
    for name, (base, spread) in spreads.items():
        noise = np.random.default_rng([zlib.crc32(name.encode()), seed]).standard_normal(out[name].shape)
        drawn = base * np.exp(spread * noise) if base else spread * noise
        out[name] = jnp.asarray(drawn.astype(out[name].dtype))
    for name, factor in factors.items():
        out[name] = (out[name] * factor).astype(out[name].dtype)
    return out
```

```python
from contextlib import ExitStack

import numpy as np

import concourse.bass as bass
from concourse import mybir

F32 = mybir.dt.float32
BF16 = mybir.dt.bfloat16
ALU = mybir.AluOpType
ACT = mybir.ActivationFunctionType
AX = mybir.AxisListType

P = 128
B = 2
T = 4
N = T * P
H = 16
DH = P // H
C = 77
CP = 80
E = 8
HID = 256
GR = 4
HG = H // GR
HP = H // 2
NGRP = B * GR
VW = 32
LN_EPS, RMS_EPS = 1e-5, 1e-6
BIG = 3.0e38

SLOTS = 6
Q_PART = (0, 0, 1, 1, 0, 2)
K_PART = (0, 1, 0, 1, 2, 0)
HROWS = SLOTS * DH
MROW = 2 * HROWS

ROWS = ("bq0", "bk0", "bv0", "bo0", "bq1", "bk1", "bv1", "gamma", "beta", "norm1", "norm2", "gates")
NKT = (1, 1, T)
SCALE = (DH ** -0.5, 1.0, DH ** -0.5)


def make_schedule():
    s = []

    def attention(layer, hooks):
        nkt = NKT[layer]
        lag = 1 if nkt > 1 else 2

        def maxima(i, part):
            if i < NGRP:
                s.append(("SMAX", layer, i, part))
                if part == nkt - 1:
                    s.append(("MCH", layer, i))

        for i in (0, 1):
            for part in range(nkt):
                maxima(i, part)
        s.append(("MTR", layer, 0))
        last = None
        for i in range(NGRP):
            for kt in range(nkt):
                s.append(("ST", layer, i, kt))
                maxima(i + 2, kt)
                if last:
                    s.append(("PV",) + last)
                last = (layer, i, kt)
                if kt == 0 and i + 1 < NGRP:
                    s.append(("MTR", layer, i + 1))
                if kt == min(1, nkt - 1) and i >= lag:
                    s.append(("OTR", layer, i - lag))
            s.extend(hooks.get(i, ()))
        s.append(("PV",) + last)
        for i in range(NGRP - lag, NGRP):
            s.append(("OTR", layer, i))

    def ffn0(b, hooks):
        s.append(("FH", b, 0))
        for e in range(E):
            if e + 1 < E:
                s.append(("FH", b, e + 1))
            s.append(("FY", b, e))
            s.extend(hooks.get(e, ()))

    qprep = lambda l, b: [("QP", l, b), ("SPLITQ", l, b)]
    qtr = lambda l, b: [("QT", l, b, 0), ("QT", l, b, 1)]

    s += [("NORM", "n0", 0), ("NORM", "n0", 1), ("CKV", 0), ("SPLITC", 0)]
    for b in range(B):
        s += [("XT", "n0", b)] + qprep(0, b)
    s += [("KTC", 0, 0), ("KTC", 0, 1)] + qtr(0, 0) + qtr(0, 1)
    attention(0, {6: [("XT", "z0", 0)], 7: [("OP", 0, 0), ("NORM", "n1", 0)]})
    s += [("XT", "n1", 0), ("RT", 0), ("RTE", 0)]
    ffn0(0, {0: [("XT", "z0", 1)], 1: [("OP", 0, 1), ("NORM", "n1", 1)], 3: [("XT", "n1", 1)],
             4: [("RT", 1)], 5: [("RTE", 1)], 6: [("CKV", 1), ("SPLITC", 1)]})
    ffn0(1, {0: [("NORM", "n2", 0), ("KTC", 1, 0), ("KTC", 1, 1)], 1: [("XT", "n2", 0)], 2: qprep(1, 0), 5: qtr(1, 0)})
    s += [("NORM", "n2", 1)]
    attention(1, {0: [("XT", "n2", 1)] + qprep(1, 1), 1: qtr(1, 1),
                  6: [("Z1", 0), ("NORM", "n3", 0), ("FIN1", 0), ("NORM", "n4", 0)], 7: [("XT", "n4", 0)]})
    kvprep = lambda b: [("KVC", b), ("QP", 2, b), ("KV", b), ("SPLITK", b), ("SPLITQ", 2, b)]
    kvtr = lambda b: [("KT", b, t) for t in range(T)] + qtr(2, b)
    s += kvprep(0) + [("Z1", 1), ("NORM", "n3", 1), ("FIN1", 1), ("NORM", "n4", 1)] + kvtr(0)
    attention(2, {0: [("XT", "n4", 1)] + kvprep(1), 1: kvtr(1),
                  5: [("XT", "z2", 0)], 6: [("OP", 2, 0), ("NORM", "r1", 0)], 7: [("XT", "fl", 0), ("GT", 0)]})
    s += [("GTE", 0), ("GH", 0, 0), ("XT", "z2", 1), ("GH", 0, 1), ("OP", 2, 1), ("NORM", "r1", 1), ("SO", 0)]
    beside = {0: [("XT", "fl", 1)], 1: [("GT", 1)], 2: [("GTE", 1)], 3: [("GH", 1, 0), ("GH", 1, 1)]}
    for b in range(B):
        if b:
            s += [("SO", b)]
        for t in range(T):
            s += [("RO", b, t, 0), ("RO", b, t, 1)]
            if b == 0:
                s += beside[t]
        s += [("NORM", "r2", b), ("OUT", b)]
    return s


def psum_uses(step):
    kind = step[0]
    if kind == "SMAX":
        return ["scores"] * 2
    if kind == "ST":
        return ["probs"] * HG
    if kind in ("QT", "KT", "KTC", "KV", "FH"):
        return ["scores"]
    if kind == "GH":
        return ["scores"] * 2
    if kind in ("FY", "SO", "RO"):
        return ["probs"]
    if kind == "OTR" and step[1] == 1:
        return []
    if kind in ("XT", "QP", "CKV", "OP", "RT", "GT", "KVC", "MTR", "OTR"):
        return ["misc"]
    return []


class Unit:

    def __init__(self, name, buffers, new_sem, schedule):
        self.full_sems = [new_sem(f"{name}{i}_full") for i in range(buffers)]
        self.read_sems = [new_sem(f"{name}{i}_read") for i in range(buffers)]
        self.n = buffers
        self.turn = {}
        for step in schedule:
            for k, unit in enumerate(psum_uses(step)):
                if unit == name:
                    self.turn[step, k] = len(self.turn)

    def buf(self, step, k=0):
        return self.turn[step, k] % self.n

    def reused(self, step, k=0):
        return self.turn[step, k] >= self.n

    def free(self, step, k=0):
        t = self.turn[step, k]
        return self.read_sems[t % self.n], t // self.n

    def full(self, step, k=0):
        t = self.turn[step, k]
        return self.full_sems[t % self.n], t // self.n + 1

    def read(self, step, k=0):
        t = self.turn[step, k]
        return self.read_sems[t % self.n], t // self.n + 1

    def full_sem(self, step, k=0):
        return self.full_sems[self.buf(step, k)]

    def read_sem(self, step, k=0):
        return self.read_sems[self.buf(step, k)]


def build(nc, d_x, d_wa, d_consts, d_rows, d_f0, d_f0y, d_wb, d_f1, d_out):
    schedule = make_schedule()
    ctx = ExitStack()
    with ctx:
        def sb(name, shape, dt=F32):
            return ctx.enter_context(nc.sbuf_tensor(name, shape, dt))

        def psum(name, shape, dt=F32):
            return ctx.enter_context(nc.psum_tensor(name, shape, dt))

        def sem(name):
            return ctx.enter_context(nc.semaphore(name))

        wa = sb("wa", [P, 4 * P + B * C])
        wq0, wkv0, wo0 = wa[:, 0:P], wa[:, P:3 * P], wa[:, 3 * P:4 * P]
        ctxT = wa[:, 4 * P:4 * P + B * C].rearrange("p (b c) -> p b c", b=B)
        consts = sb("consts", [P, P + 2 * T * P + E + T])
        ident = consts[:, 0:P]
        cosf = consts[:, P:P + N]
        sinf = consts[:, P + N:P + 2 * N]
        rev = consts[:, P + 2 * N:P + 2 * N + E]
        minus_half = consts[:, P + 2 * N + E:P + 2 * N + E + T]
        rows = sb("rows", [P, len(ROWS) * P])
        row = {name: rows[:, i * P:(i + 1) * P] for i, name in enumerate(ROWS)}
        f0 = sb("f0", [P, E + E * HID])
        rw = f0[:, 0:E]
        w1 = f0[:, E:E + E * HID].rearrange("p (e c h) -> p e c h", e=E, c=2)
        f0y = sb("f0y", [P, E * 2 * P])
        w2 = f0y[:, :].rearrange("p (e c d) -> p e c d", e=E, c=2)
        wb = sb("wb", [P, 8 * P])
        wq1, wkv1 = wb[:, 0:P], wb[:, P:3 * P]
        wq2, wkvc, wkv2, wo2 = wb[:, 3 * P:4 * P], wb[:, 4 * P:5 * P], wb[:, 5 * P:7 * P], wb[:, 7 * P:8 * P]
        GW = 2 + E
        f1 = sb("f1", [P, 2 * 2 * HID + 2 * P + 2 * E * P + GW])
        win = f1[:, 0:4 * HID].rearrange("p (w m h) -> p w m h", w=2, m=4)
        wso = f1[:, 4 * HID:4 * HID + 2 * P].rearrange("p (c d) -> p c d", c=2)
        w2x = f1[:, 4 * HID + 2 * P:4 * HID + 2 * P + 2 * E * P].rearrange("p (c f n) -> p c f n", c=2, f=2)
        wgate = f1[:, 4 * HID + 2 * P + 2 * E * P:]
        wq = (wq0, wq1, wq2)
        wkvx = (wkv0, wkv1)
        identb = sb("identb", [P, P], BF16)

        def pair(name, shape, dt=F32):
            return [sb(f"{name}{b}", shape, dt) for b in range(B)]

        X = pair("X", [P, T, P])
        XN = pair("XN", [P, T, P])
        XT = pair("XT", [P, N])
        Z = pair("Z", [P, T, P])
        ACC = pair("ACC", [P, T, P])
        QF = [ACC[b][:, :, :].rearrange("p t d -> p (t d)") for b in range(B)]
        KF = [f0[:, E + b * N:E + (b + 1) * N] for b in range(B)]
        RS = [Z[b][:, :, :].rearrange("p t d -> p (t d)") for b in range(B)]
        qcat = pair("qcat", [P, T, HP, P], BF16)
        qT = pair("qT", [P, HP, N], BF16)
        kcat = sb("kcat", [P, T, H, P], BF16)
        kT = pair("kT", [P, H, N], BF16)
        kTc = [pair(f"kTc{l}", [P, H, CP], BF16) for l in range(2)]
        V = pair("V", [P, T, H, VW])
        Vc = [pair(f"Vc{l}", [P, H, VW]) for l in range(2)]
        mx = [sb(f"mx{i}", [P, T, HG]) for i in range(2)]
        mrs = [sb(f"mrs{i}", [P, T, HG]) for i in range(2)]
        mcat = [sb(f"mcat{i}", [P, T, 2, P], BF16) for i in range(2)]
        pT = [sb(f"pT{i}", [P, HG, N]) for i in range(2)]
        oT = [sb(f"oT{i}", [P, N]) for i in range(2)]
        kf = oT[0][:, 0:B * P].rearrange("p (b d) -> p b d", b=B)
        rinv = [sb(f"rinv{i}", [P, T, HG]) for i in range(2)]
        kflat = [kT[b][:, :, :].bitcast(F32).rearrange("p h n -> p (h n)") for b in range(B)]
        relu = [kflat[1][:, 2 * N * i:2 * N * (i + 1)] for i in range(2)]
        h2 = [kflat[0][:, 2 * N * i:2 * N * (i + 1)].rearrange("p (c n) -> p c n", c=2) for i in range(2)]
        gh = h2
        bn = pair("bn", [P, T, 6])
        mv = pair("mv", [P, T, 2])
        var = pair("var", [P, T])
        rstd = pair("rstd", [P, T])
        gl = pair("gl", [P, T, GW])
        gx = pair("gx", [P, T, GW])
        gex = pair("gex", [P, T, GW])
        g1 = pair("g1", [P, T, E])
        g2 = pair("g2", [P, T, E])
        oh1 = pair("oh1", [P, T, E])
        oh2 = pair("oh2", [P, T, E])
        gv = pair("gv", [P, 8, T])
        gw = pair("gw", [P, T, E])

        scores_ps = [psum(f"scores_ps{i}", [P, 2, 512]) for i in range(2)]
        probs_ps = [psum(f"probs_ps{i}", [P, 512]) for i in range(2)]
        misc_ps = psum("misc_ps", [P, 512])
        out_ps = psum("out_ps", [P, 512])
        scores = Unit("scores", 2, sem, schedule)
        probs = Unit("probs", 2, sem, schedule)
        misc = Unit("misc", 1, sem, schedule)

        kinds = {"NORM": "normed", "SPLITQ": "query_parts", "SPLITC": "context_parts", "SPLITK": "key_parts",
                 "MCH": "max_parts", "FH": "hidden", "RT": "router_diffs", "RTE": "router_exps",
                 "GT": "gate_diffs", "GTE": "gate_exps", "OP": "projected", "KV": "values",
                 "Z1": "z_added", "PV": "pv", "NORMSTATS": "stats", "RSTD": "rstds",
                 "OUTV": "out_rows", "PVREAD": "out_ps_read", "QROT": "queries"}
        done = {k: sem(f"{n}_done") for k, n in kinds.items()}
        base = {"NORMSTATS": "NORM", "RSTD": "NORM", "OUTV": "OUT", "QROT": "QP"}
        seen, nth = {}, {}
        for step in schedule:
            seen[step[0]] = seen.get(step[0], 0) + 1
            nth[step] = seen[step[0]]

        def after(kind, *args):
            if kind == "PVREAD":
                layer, i = args
                return done[kind], layer * NGRP + i + 1
            return done[kind], nth[(base.get(kind, kind),) + args]

        loaded = {n: sem(f"{n}_loaded") for n in ("x0", "x1", "wa", "consts", "rows", "f0", "f0y", "wb", "f1")}
        stored = [sem(f"stored{b}") for b in range(B)]
        zeroed = sem("zeroed")
        consts_cast = sem("consts_cast")
        dve_chain = sem("dve_chain")
        pool_chain = sem("pool_chain")
        ZERO = {"qcat0": 1, "kcat": 2, "Vc": 3, "pT": 4, "mcat": 5, "qcat1": 6, "V": 7}

        source = {"n0": XN, "n1": XN, "n2": XN, "n4": XN, "fl": XN, "z0": Z, "z2": Z}

        def slot(cat, first, pairs, s, parts=P):
            wide = 2 * P if cat is kcat else P
            step = P + HROWS if cat is kcat else HROWS
            size = int(np.prod(cat.shape[1:]))
            return bass.AP(cat, first * wide + DH * s, [[size, parts], [wide, pairs], [step, 2], [1, DH]])

        def flat_heads(t, parts=P):
            return t.rearrange("p (n e d) -> p n e d", e=2, d=DH)

        def flat(t):
            return t[:, :, :].rearrange("p t d -> p (t d)")

        def over_tiles(r, n=T):
            return r.unsqueeze(1).broadcast_to([P, n, r.shape[1]])

        block = ctx.enter_context(nc.Block())

        @block.sync
        def _(sp):
            sp.dma_start(X[0][:, :, :], d_x[0]).then_inc(loaded["x0"], 16)
            sp.dma_start(wa[:, :], d_wa).then_inc(loaded["wa"], 16)
            sp.dma_start(X[1][:, :, :], d_x[1]).then_inc(loaded["x1"], 16)
            sp.dma_start(f0[:, :], d_f0).then_inc(loaded["f0"], 16)
            sp.dma_start(f0y[:, :], d_f0y).then_inc(loaded["f0y"], 16)
            sp.dma_start(wb[:, :], d_wb).then_inc(loaded["wb"], 16)
            sp.dma_start(f1[:, :], d_f1).then_inc(loaded["f1"], 16)
            for b in range(B):
                sp.wait_ge(*after("OUTV", b))
                sp.dma_start(d_out[b], ACC[b][:, :, :]).then_inc(stored[b], 16)
            for b in range(B):
                sp.wait_ge(stored[b], 16)

        @block.gpsimd
        def _(pool):
            U32 = mybir.dt.uint32
            pool.memset(qcat[0][:, :, :, :].bitcast(U32), 0).then_inc(zeroed, 1)
            pool.memset(kcat[:, :, :, :].bitcast(U32), 0).then_inc(zeroed, 1)
            for l in range(2):
                for b in range(B):
                    last = pool.memset(Vc[l][b][:, :, :], 0.0)
            last.then_inc(zeroed, 1)
            pool.memset(pT[0][:, :, :], 0.0)
            pool.memset(pT[1][:, :, :], 0.0).then_inc(zeroed, 1)
            pool.memset(mcat[0][:, :, :, :].bitcast(U32), 0)
            pool.memset(mcat[1][:, :, :, :].bitcast(U32), 0).then_inc(zeroed, 1)
            chain = 0
            pool.wait_ge(loaded["consts"], 16)

            def NORM(kind, b):
                pool.wait_ge(*after("NORMSTATS", kind, b))
                pool.tensor_tensor(rstd[b][:, :], var[b][:, :], minus_half, ALU.pow).then_inc(done["RSTD"], 1)

            for n, step in enumerate(schedule):
                if n == 4:
                    pool.memset(qcat[1][:, :, :, :].bitcast(U32), 0).then_inc(zeroed, 1)
                    pool.memset(V[0][:, :, :, :], 0.0)
                    pool.memset(V[1][:, :, :, :], 0.0).then_inc(zeroed, 1)
                if step[0] == "NORM":
                    NORM(*step[1:])

        @block.tensor
        def _(pe):
            def mm(out, lhsT, rhs, start=True, stop=True):
                return nc.tensor.matmul(out, lhsT, rhs, start=start, stop=stop)

            def XTstep(step, kind, b):
                if kind[0] == "z":
                    pe.wait_ge(*misc.read(("OTR", int(kind[1]), b * GR + GR - 1)))
                else:
                    pe.wait_ge(*after("NORM", {"fl": "r1"}.get(kind, kind), b))
                if misc.reused(step):
                    pe.wait_ge(*misc.free(step))
                for t in range(T):
                    last = nc.tensor.transpose(misc_ps[:, t * P:(t + 1) * P], source[kind][b][:, t, :], ident)
                last.then_inc(misc.full_sem(step), 1)

            def project(step, b, w, width, xt_step):
                pe.wait_ge(*misc.read(xt_step))
                pe.wait_ge(*misc.free(step))
                for t in range(T):
                    last = mm(misc_ps[:, t * width:(t + 1) * width], XT[b][:, t * P:(t + 1) * P], w)
                last.then_inc(misc.full_sem(step), 1)

            def QP(step, layer, b):
                if layer:
                    pe.wait_ge(loaded["wb"], 16)
                else:
                    pe.wait_ge(loaded["wa"], 16)
                project(step, b, wq[layer], P, ("XT", ("n0", "n2", "n4")[layer], b))

            def OP(step, layer, b):
                project(step, b, wo0 if layer == 0 else wo2, P, ("XT", "z0" if layer == 0 else "z2", b))

            def RT(step, b):
                if b == 0:
                    pe.wait_ge(loaded["f0"], 16)
                project(step, b, rw, E, ("XT", "n1", b))

            def GT(step, b):
                if b == 0:
                    pe.wait_ge(loaded["f1"], 16)
                project(step, b, wgate, GW, ("XT", "fl", b))

            def CKV(step, layer):
                pe.wait_ge(loaded["wb" if layer else "wa"], 16)
                if misc.reused(step):
                    pe.wait_ge(*misc.free(step))
                for b in range(B):
                    last = mm(misc_ps[0:C, b * 2 * P:(b + 1) * 2 * P], ctxT[:, b, :], wkvx[layer])
                last.then_inc(misc.full_sem(step), 1)

            def KVC(step, b):
                pe.wait_ge(*misc.read(("XT", "n4", b)))
                pe.wait_ge(*misc.free(step))
                mm(misc_ps[:, :], wkvc, XT[b][:, :]).then_inc(misc.full_sem(step), 1)

            def KV(step, b):
                pe.wait_ge(*misc.read(("KVC", b)))
                pe.wait_ge(*scores.free(step))
                ps = scores_ps[scores.buf(step)]
                for t in range(T):
                    last = mm(ps[:, t // 2, (t % 2) * 256:(t % 2) * 256 + 256], relu[b][:, t * P:(t + 1) * P], wkv2)
                last.then_inc(scores.full_sem(step), 1)

            def KTC(step, layer, b):
                pe.wait_ge(*after("SPLITC", layer))
                if scores.reused(step):
                    pe.wait_ge(*scores.free(step))
                ps = scores_ps[scores.buf(step)][:, :, :].bitcast(BF16)
                for h in range(H):
                    o = (h % 8) * CP
                    last = nc.tensor.transpose(ps[:, h // 8, o:o + C], kcat[0:C, 2 * layer + b, h, :], identb[0:C, 0:C])
                last.then_inc(scores.full_sem(step), 1)

            def KT(step, b, t):
                pe.wait_ge(*after("SPLITK", b))
                pe.wait_ge(*scores.free(step))
                ps = scores_ps[scores.buf(step)][:, :, :].bitcast(BF16)
                for h in range(H):
                    o = (h % 8) * P
                    last = nc.tensor.transpose(ps[:, h // 8, o:o + P], kcat[:, t, h, :], identb[:, :])
                last.then_inc(scores.full_sem(step), 1)

            def QT(step, layer, b, u):
                pe.wait_ge(*after("SPLITQ", layer, b))
                if scores.reused(step):
                    pe.wait_ge(*scores.free(step))
                ps = scores_ps[scores.buf(step)][:, :, :].bitcast(BF16)
                for t in range(2):
                    for p in range(HP):
                        last = nc.tensor.transpose(ps[:, t, p * P:(p + 1) * P], qcat[b][:, 2 * u + t, p, :], identb[:, :])
                last.then_inc(scores.full_sem(step), 1)

            def SMAX(step, layer, i, part):
                b, g = divmod(i, GR)
                if i % GR == 0 and part == 0:
                    for u in range(2):
                        pe.wait_ge(*scores.read(("QT", layer, b, u)))
                    for k in range(T if layer == 2 else 1):
                        pe.wait_ge(*scores.read(("KT", b, k) if layer == 2 else ("KTC", layer, b)))
                for u in range(2):
                    pe.wait_ge(*scores.free(step, u))
                    ps = scores_ps[scores.buf(step, u)]
                    for k in range(2):
                        if layer == 2:
                            pr = 2 * g + u
                            last = mm(ps[:, k, :], qT[b][:, pr, part * P:(part + 1) * P], kT[b][:, 2 * pr + k, :])
                        else:
                            t = 2 * u + k
                            for pr in range(2):
                                a = 2 * g + pr
                                last = mm(ps[:, k, pr * 2 * C:(pr + 1) * 2 * C], qT[b][:, a, t * P:(t + 1) * P],
                                          kTc[layer][b][:, 2 * a:2 * a + 2, 0:C])
                    last.then_inc(scores.full_sem(step, u), 1)

            def MTR(step, layer, i):
                pe.wait_ge(*after("MCH", layer, i))
                pe.wait_ge(*misc.free(step))
                ps = misc_ps[:, :].bitcast(BF16)
                for pr in range(2):
                    for t in range(T):
                        o = (pr * T + t) * P
                        last = nc.tensor.transpose(ps[:, o:o + P], mcat[i % 2][:, t, pr, :], identb[:, :])
                last.then_inc(misc.full_sem(step), 1)

            def ST(step, layer, i, kt):
                b, g = divmod(i, GR)
                if kt == 0:
                    pe.wait_ge(*misc.read(("MTR", layer, i)))
                for j in range(HG):
                    h = HG * g + j
                    if probs.reused(step, j):
                        pe.wait_ge(*probs.free(step, j))
                    ps = probs_ps[probs.buf(step, j)]
                    if layer == 2:
                        out, keys = ps[:, :], kT[b][:, h, kt * P:(kt + 1) * P]
                    else:
                        out, keys = ps[0:C, :], kTc[layer][b][:, h, 0:C]
                    mm(out, keys, qT[b][:, h // 2, :]).then_inc(probs.full_sem(step, j), 1)

            def PV(step, layer, i, kt):
                b, g = divmod(i, GR)
                if layer == 2 and i % GR == 0 and kt == 0:
                    pe.wait_ge(*after("KV", b))
                if kt == 0 and (layer or i):
                    pe.wait_ge(done["PVREAD"], layer * NGRP + i)
                st = ("ST", layer, i, kt)
                for j in range(HG):
                    pe.wait_ge(*probs.read(st, j))
                    h = HG * g + j
                    vals = V[b][:, kt, h, :] if layer == 2 else Vc[layer][b][:, h, :]
                    last = mm(out_ps[j * VW:(j + 1) * VW, :], vals, pT[(nth[step] - 1) % 2][:, j, :],
                              start=(kt == 0), stop=(kt == NKT[layer] - 1))
                last.then_inc(done["PV"], 1)

            def OTR(step, layer, i):
                if layer == 1:
                    return
                pe.wait_ge(*after("PVREAD", layer, i))
                pe.wait_ge(*misc.free(step))
                for t in range(T):
                    last = nc.tensor.transpose(misc_ps[:, t * P:(t + 1) * P], oT[i % 2][:, t * P:(t + 1) * P], ident)
                last.then_inc(misc.full_sem(step), 1)

            def FH(step, b, e):
                if e == 0:
                    pe.wait_ge(*misc.read(("XT", "n1", b)))
                pe.wait_ge(*scores.free(step))
                ps = scores_ps[scores.buf(step)]
                for c in range(2):
                    last = mm(ps[:, c, :], w1[:, e, c, :], XT[b][:, :])
                last.then_inc(scores.full_sem(step), 1)

            def FY(step, b, e):
                if b == 0 and e == 0:
                    pe.wait_ge(loaded["f0y"], 16)
                pe.wait_ge(*after("FH", b, e))
                pe.wait_ge(*probs.free(step))
                ps = probs_ps[probs.buf(step)]
                for t in range(T):
                    for c in range(2):
                        last = mm(ps[:, t * P:(t + 1) * P], h2[e % 2][:, c, t * P:(t + 1) * P], w2[:, e, c, :],
                                  start=(c == 0), stop=(c == 1))
                last.then_inc(probs.full_sem(step), 1)

            def GH(step, b, w):
                if w == 0:
                    pe.wait_ge(*misc.read(("XT", "fl", b)))
                for half in range(2):
                    pe.wait_ge(*scores.free(step, half))
                    ps = scores_ps[scores.buf(step, half)]
                    for c in range(2):
                        last = mm(ps[:, c, :], win[:, w, 2 * half + c, :], XT[b][:, :])
                    last.then_inc(scores.full_sem(step, half), 1)

            def SO(step, b):
                pe.wait_ge(*scores.read(("GH", b, 0), 1))
                pe.wait_ge(*probs.free(step))
                ps = probs_ps[probs.buf(step)]
                for t in range(T):
                    for c in range(2):
                        last = mm(ps[:, t * P:(t + 1) * P], gh[0][:, c, t * P:(t + 1) * P], wso[:, c, :],
                                  start=(c == 0), stop=(c == 1))
                last.then_inc(probs.full_sem(step), 1)

            def RO(step, b, t, half):
                if t == 0 and half == 0:
                    pe.wait_ge(*scores.read(("GH", b, 1), 1))
                pe.wait_ge(*probs.free(step))
                ps = probs_ps[probs.buf(step)]
                for c in range(2):
                    last = mm(ps[:, :], gh[1][:, c, t * P:(t + 1) * P], w2x[:, c, half, :],
                              start=(c == 0), stop=(c == 1))
                last.then_inc(probs.full_sem(step), 1)

            parts = {"XT": XTstep, "QP": QP, "OP": OP, "RT": RT, "GT": GT, "CKV": CKV, "KVC": KVC, "KV": KV,
                     "KTC": KTC, "KT": KT, "QT": QT, "SMAX": SMAX, "MTR": MTR, "ST": ST, "PV": PV, "OTR": OTR,
                     "FH": FH, "FY": FY, "GH": GH, "SO": SO, "RO": RO}
            pe.wait_ge(loaded["consts"], 16)
            pe.wait_ge(consts_cast, 1)
            for step in schedule:
                if step[0] in parts:
                    parts[step[0]](step, *step[1:])

        @block.scalar
        def _(act):
            act.dma_start(consts[:, :], d_consts).then_inc(loaded["consts"], 16)
            act.dma_start(rows[:, :], d_rows.partition_broadcast(P)).then_inc(loaded["rows"], 16)

            def XTstep(step, kind, b):
                act.wait_ge(*misc.full(step))
                nc.scalar.copy(XT[b][:, :], misc_ps[:, :]).then_inc(misc.read_sem(step), 1)

            def KVC(step, b):
                act.wait_ge(*misc.full(step))
                nc.scalar.copy(relu[b][:, 0:N], misc_ps[:, :]).then_inc(misc.read_sem(step), 1)

            def KTC(step, layer, b):
                act.wait_ge(*scores.full(step))
                src = scores_ps[scores.buf(step)][:, :, :].bitcast(BF16)[:, :, 0:8 * CP]
                src = src.rearrange("p a (h c) -> p a h c", c=CP)[:, :, :, 0:C]
                dst = kTc[layer][b][:, :, :].rearrange("p (a h) c -> p a h c", a=2)[:, :, :, 0:C]
                nc.scalar.copy(dst, src).then_inc(scores.read_sem(step), 1)

            def KT(step, b, t):
                if t % 2:
                    return
                act.wait_ge(*scores.full(step))
                src = scores_ps[scores.buf(step)][:, :, :].bitcast(BF16)
                src = src.rearrange("p a (h c) -> p (a h) c", c=P)
                nc.scalar.copy(kT[b][:, :, t * P:(t + 1) * P], src).then_inc(scores.read_sem(step), 1)

            def QT(step, layer, b, u):
                if u:
                    return
                act.wait_ge(*scores.full(step))
                src = scores_ps[scores.buf(step)][:, :, :].bitcast(BF16).rearrange("p t (a c) -> p t a c", c=P)
                dst = qT[b][:, :, 2 * u * P:2 * (u + 1) * P].rearrange("p a (t c) -> p t a c", t=2)
                nc.scalar.copy(dst, src).then_inc(scores.read_sem(step), 1)

            def MTR(step, layer, i):
                b, g = divmod(i, GR)
                act.wait_ge(*misc.full(step))
                src = misc_ps[MROW:MROW + 6, :].bitcast(BF16).rearrange("p (a n) -> p a n", a=2)
                nc.scalar.copy(qT[b][MROW:MROW + 6, 2 * g:2 * g + 2, :], src).then_inc(misc.read_sem(step), 1)

            def ST(step, layer, i, kt):
                rows_ = P if layer == 2 else C
                n = nth[step] - 1
                if n >= 2:
                    act.wait_ge(done["PV"], n - 1)
                for j in range(HG):
                    act.wait_ge(*probs.full(step, j))
                    nc.scalar.activation(pT[n % 2][0:rows_, j, :], probs_ps[probs.buf(step, j)][0:rows_, :], ACT.Exp,
                                         scale=SCALE[layer]).then_inc(probs.read_sem(step, j), 1)

            def PV(step, layer, i, kt):
                if kt < NKT[layer] - 1 or layer == 1:
                    return
                act.wait_ge(*after("PV", layer, i, kt))
                if i >= 2:
                    act.wait_ge(*misc.full(("OTR", layer, i - 2)))
                nc.scalar.copy(oT[i % 2][:, :], out_ps[:, :]).then_inc(done["PVREAD"], 1)

            def RTE(step, b):
                act.wait_ge(*after("RT", b))
                nc.scalar.activation(gex[b][:, :, 0:1], gx[b][:, :, 0:1], ACT.Exp).then_inc(done["RTE"], 1)

            def GTE(step, b):
                act.wait_ge(*after("GT", b))
                nc.scalar.activation(gex[b][:, :, :], gx[b][:, :, :], ACT.Exp).then_inc(done["GTE"], 1)

            def FH(step, b, e):
                n = nth[step] - 1
                if n >= 2:
                    act.wait_ge(done["FH"], n - 1)
                act.wait_ge(*scores.full(step))
                src = scores_ps[scores.buf(step)][:, :, :].rearrange("p c n -> p (c n)")
                nc.scalar.activation(relu[n % 2], src, ACT.Relu).then_inc(scores.read_sem(step), 1)

            def GH(step, b, w):
                n = nth[step] - 1
                if n >= 2:
                    prev = [s for s in schedule if s[0] == "GH"][n - 2]
                    act.wait_ge(*scores.read(prev, 1))
                act.wait_ge(*scores.full(step, 0))
                src = scores_ps[scores.buf(step, 0)][:, :, :].rearrange("p c n -> p (c n)")
                nc.scalar.activation(relu[n % 2], src, ACT.Silu).then_inc(scores.read_sem(step, 0), 1)

            parts = {"XT": XTstep, "KVC": KVC, "KTC": KTC, "KT": KT, "QT": QT, "MTR": MTR, "ST": ST, "PV": PV,
                     "RTE": RTE, "GTE": GTE, "FH": FH, "GH": GH}
            act.wait_ge(zeroed, ZERO["pT"])
            for step in schedule:
                if step[0] in parts:
                    parts[step[0]](step, *step[1:])

        @block.vector
        def _(dve):
            V_ = nc.vector
            chain = [0]

            def link(ins):
                chain[0] += 1
                ins.then_inc(dve_chain, 1)
                dve.wait_ge(dve_chain, chain[0])

            def tt(out, a, c, op):
                return V_.tensor_tensor(out, a, c, op)

            def NORM(step, kind, b):
                src, dst = {"n0": (X, XN), "n1": (X, XN), "n2": (X, XN), "n4": (X, XN), "n3": (ACC, ACC),
                            "r1": (ACC, XN), "r2": (ACC, ACC)}[kind]
                if kind == "n0":
                    dve.wait_ge(loaded[f"x{b}"], 16)
                for t in range(T):
                    link_last = V_.bn_stats(bn[b][:, t, :], src[b][:, t, :])
                link(link_last)
                for t in range(T):
                    link_last = V_.bn_aggr(mv[b][:, t, :], bn[b][:, t, :])
                link(link_last)
                mean, v = mv[b][:, :, 0], mv[b][:, :, 1]
                if kind[0] == "n":
                    V_.tensor_scalar(var[b][:, :], v, LN_EPS, None, ALU.add).then_inc(done["NORMSTATS"], 1)
                else:
                    link(tt(var[b][:, :], mean, mean, ALU.mult))
                    V_.scalar_tensor_tensor(out=var[b][:, :], in0=var[b][:, :], scalar=RMS_EPS, in1=v,
                                            op0=ALU.add, op1=ALU.add).then_inc(done["NORMSTATS"], 1)
                dve.wait_ge(*after("RSTD", kind, b))
                for t in range(T):
                    if kind[0] == "n":
                        ins = V_.tensor_scalar(dst[b][:, t, :], src[b][:, t, :], mv[b][:, t, 0:1],
                                               rstd[b][:, t:t + 1], ALU.subtract, ALU.mult)
                    else:
                        ins = V_.tensor_scalar(dst[b][:, t, :], src[b][:, t, :], rstd[b][:, t:t + 1], None, ALU.mult)
                if kind == "r1":
                    link(ins)
                    ins = tt(dst[b][:, :, :], dst[b][:, :, :], over_tiles(row["norm1"]), ALU.mult)
                ins.then_inc(done["NORM"], 1)

            def CKV(step, layer):
                dve.wait_ge(*misc.full(step))
                if layer == 0:
                    dve.wait_ge(loaded["rows"], 16)
                    dve.wait_ge(zeroed, ZERO["Vc"])
                src = misc_ps[0:C, :].rearrange("p (b w d) -> p b w d", b=B, w=2)
                bk, bv = row[f"bk{layer}"][0:C, :], row[f"bv{layer}"][0:C, :]
                for b in range(B):
                    v = Vc[layer][b]
                    V_.memset(v[0:C, :, DH:DH + 1], 1.0)
                    tt(v[0:C, :, 0:DH], src[:, b, 1, :].rearrange("p (h d) -> p h d", d=DH),
                       bv.rearrange("p (h d) -> p h d", d=DH), ALU.add)
                    last = tt(kf[0:C, b, :], src[:, b, 0, :], bk, ALU.add)
                last.then_inc(misc.read_sem(step), 1)

            def split(cat, first, pairs, values, rest, part_of, parts=P):
                def dst(s):
                    return slot(cat, first, pairs, s, parts)
                s0, s1, s2 = (part_of.index(k) for k in range(3))
                link(V_.tensor_copy(dst(s0), flat_heads(values)))
                link(tt(flat_heads(rest), flat_heads(values), dst(s0), ALU.subtract))
                link(V_.tensor_copy(dst(s1), flat_heads(rest)))
                for s, k in enumerate(part_of):
                    if k < 2 and s != (s0, s1)[k]:
                        V_.tensor_copy(dst(s), dst((s0, s1)[k]))
                return tt(dst(s2), flat_heads(rest), dst(s1), ALU.subtract)

            def SPLITC(step, layer):
                dve.wait_ge(*misc.read(("CKV", layer)))
                if layer == 0:
                    dve.wait_ge(zeroed, ZERO["kcat"])
                    for e in range(2):
                        heads = kcat[:, :, :, :].rearrange("p t (a e) c -> p (t a) e c", e=2)
                        V_.memset(heads[:, :, e, MROW + 3 * e:MROW + 3 * e + 3], 1.0)
                flatk = oT[0][0:C, 0:B * P]
                flatr = oT[1][0:C, 0:B * P]
                split(kcat, 2 * layer * HP, B * HP, flatk, flatr, K_PART, C).then_inc(done["SPLITC"], 1)

            def rotate(src, out, tmp):
                sv = src.rearrange("p t (i two) -> p t i two", two=2)
                tv = tmp.rearrange("p (t i two) -> p t i two", t=T, two=2)
                nv = sinf.rearrange("p (t i two) -> p t i two", t=T, two=2)
                tt(out.rearrange("p (t d) -> p t d", t=T), src, cosf.rearrange("p (t d) -> p t d", t=T), ALU.mult)
                tt(tv[:, :, :, 0], sv[:, :, :, 1], nv[:, :, :, 0], ALU.mult)
                return tt(tv[:, :, :, 1], sv[:, :, :, 0], nv[:, :, :, 1], ALU.mult)

            def QP(step, layer, b):
                dve.wait_ge(*misc.full(step))
                src = misc_ps[:, :].rearrange("p (t d) -> p t d", t=T)
                if layer < 2:
                    tt(QF[b].rearrange("p (t d) -> p t d", t=T), src, over_tiles(row[f"bq{layer}"]),
                       ALU.add).then_inc(misc.read_sem(step), 1)
                    dve.wait_ge(*misc.read(step))
                else:
                    rotate(src, QF[b], RS[b]).then_inc(misc.read_sem(step), 1)
                    dve.wait_ge(*misc.read(step))
                    link(tt(QF[b], QF[b], RS[b], ALU.add))

            def SPLITQ(step, layer, b):
                if layer == 0:
                    dve.wait_ge(zeroed, ZERO[f"qcat{b}"])
                split(qcat[b], 0, T * HP, QF[b], RS[b], Q_PART).then_inc(done["SPLITQ"], 1)

            def KV(step, b):
                dve.wait_ge(*scores.full(step))
                if b == 0:
                    dve.wait_ge(zeroed, ZERO["V"])
                src = scores_ps[scores.buf(step)][:, :, :].rearrange("p a (t w d) -> p (a t) w d", t=2, w=2)
                V_.memset(V[b][:, :, :, DH:DH + 1], 1.0)
                V_.tensor_copy(V[b][:, :, :, 0:DH], src[:, :, 1, :].rearrange("p t (h d) -> p t h d", d=DH)
                               ).then_inc(done["KV"], 1)
                rotate(src[:, :, 0, :], KF[b], RS[b]).then_inc(scores.read_sem(step), 1)
                dve.wait_ge(*scores.read(step))
                link(tt(KF[b], KF[b], RS[b], ALU.add))

            def SPLITK(step, b):
                if b:
                    for t in range(T):
                        dve.wait_ge(*scores.full(("KT", 0, t)))
                split(kcat, 0, T * HP, KF[b], RS[b], K_PART).then_inc(done["SPLITK"], 1)

            def KT(step, b, t):
                if t % 2 == 0:
                    return
                dve.wait_ge(*scores.full(step))
                src = scores_ps[scores.buf(step)][:, :, :].bitcast(BF16).rearrange("p a (h c) -> p (a h) c", c=P)
                V_.tensor_copy(kT[b][:, :, t * P:(t + 1) * P], src).then_inc(scores.read_sem(step), 1)

            def QT(step, layer, b, u):
                if u == 0:
                    return
                dve.wait_ge(*scores.full(step))
                src = scores_ps[scores.buf(step)][:, :, :].bitcast(BF16).rearrange("p t (a c) -> p t a c", c=P)
                dst = qT[b][:, :, 2 * u * P:2 * (u + 1) * P].rearrange("p a (t c) -> p t a c", t=2)
                V_.tensor_copy(dst, src).then_inc(scores.read_sem(step), 1)

            def SMAX(step, layer, i, part):
                for u in range(2):
                    dve.wait_ge(*scores.full(step, u))
                    ps = scores_ps[scores.buf(step, u)]
                    if layer == 2:
                        src, dst = ps[:, :, :], mx[i % 2][:, part, 2 * u:2 * u + 2]
                    else:
                        src = ps[:, :, 0:HG * C].rearrange("p t (h c) -> p t h c", c=C)
                        dst = mx[i % 2][:, 2 * u:2 * u + 2, :]
                    V_.tensor_reduce(dst, src, AX.X, ALU.max).then_inc(scores.read_sem(step, u), 1)

            def MCH(step, layer, i):
                k = i % 2
                if layer == 0 and i == 0:
                    dve.wait_ge(zeroed, ZERO["mcat"])
                if layer or i >= 2:
                    old = ("MTR", layer, i - 2) if i >= 2 else ("MTR", layer - 1, NGRP - 2 + i)
                    dve.wait_ge(*misc.full(old))
                for u in range(2):
                    dve.wait_ge(*scores.read(("SMAX", layer, i, NKT[layer] - 1), u))
                m = mx[k][:, :, :].rearrange("p t (a e) -> p (t a) e", e=2)
                r = mrs[k][:, :, :].rearrange("p t (a e) -> p (t a) e", e=2)
                c = mcat[k][:, :, :, MROW:MROW + 6].rearrange("p t a (e r) -> p (t a) e r", e=2)
                link(V_.tensor_scalar(c[:, :, :, 0], m, -1.0, None, ALU.mult))
                link(V_.scalar_tensor_tensor(out=r, in0=m, scalar=-1.0, in1=c[:, :, :, 0], op0=ALU.mult, op1=ALU.subtract))
                link(V_.tensor_copy(c[:, :, :, 1], r))
                tt(c[:, :, :, 2], r, c[:, :, :, 1], ALU.subtract).then_inc(done["MCH"], 1)

            def PV(step, layer, i, kt):
                if layer != 1:
                    return
                dve.wait_ge(*after("PV", layer, i, kt))
                V_.transpose(oT[i % 2][:, :].rearrange("p (c r) -> p c r", c=N // VW),
                             out_ps[:, :].rearrange("p (m c) -> p c m", c=N // VW)).then_inc(done["PVREAD"], 1)

            def OTR(step, layer, i):
                b, g = divmod(i, GR)
                if layer == 1:
                    dve.wait_ge(*after("PVREAD", layer, i))
                    src = oT[i % 2][:, :].rearrange("p (c r) -> p c r", c=N // VW)
                    inv = rinv[i % 2][:, :, :].rearrange("p t j -> p (t j)")
                    link(V_.reciprocal(inv, src[:, :, DH]))
                    dst = Z[b][:, g, :].rearrange("p (c d) -> p c d", d=DH)
                    link(tt(dst, src[:, :, 0:DH], inv.unsqueeze(2).broadcast_to([P, N // VW, DH]), ALU.mult))
                    return
                dve.wait_ge(*misc.full(step))
                src = misc_ps[:, :].rearrange("p (t j c) -> p t j c", t=T, j=HG)
                link(V_.reciprocal(rinv[i % 2][:, :, :], src[:, :, :, DH]))
                dst = Z[b][:, :, g * HG * DH:(g + 1) * HG * DH].rearrange("p t (j d) -> p t j d", d=DH)
                tt(dst, src[:, :, :, 0:DH], rinv[i % 2][:, :, :].unsqueeze(3).broadcast_to([P, T, HG, DH]),
                   ALU.mult).then_inc(misc.read_sem(step), 1)

            def OP(step, layer, b):
                dve.wait_ge(*misc.full(step))
                src = misc_ps[:, :].rearrange("p (t d) -> p t d", t=T)
                if layer == 0:
                    tt(X[b][:, :, :], X[b][:, :, :], src, ALU.add).then_inc(misc.read_sem(step), 1)
                    dve.wait_ge(*misc.read(step))
                    link(tt(X[b][:, :, :], X[b][:, :, :], over_tiles(row["bo0"]), ALU.add))
                else:
                    tt(ACC[b][:, :, :], XN[b][:, :, :], src, ALU.add).then_inc(misc.read_sem(step), 1)
                    dve.wait_ge(*misc.read(step))

            def Z1(step, b):
                link(tt(ACC[b][:, :, :], Z[b][:, :, :], XN[b][:, :, :], ALU.add))

            def FIN1(step, b):
                dve.wait_ge(*after("NORM", "n3", b))
                link(tt(ACC[b][:, :, :], ACC[b][:, :, :], over_tiles(row["gamma"]), ALU.mult))
                link(tt(ACC[b][:, :, :], ACC[b][:, :, :], over_tiles(row["beta"]), ALU.add))
                link(tt(X[b][:, :, :], X[b][:, :, :], ACC[b][:, :, :], ALU.add))

            def first_max(b, src, oh, top, k):
                eq, best = g2[b], gv[b][:, k, :]
                link(V_.tensor_reduce(top, src, AX.X, ALU.max))
                link(tt(eq[:, :, :], src, top.unsqueeze(2).broadcast_to([P, T, E]), ALU.is_equal))
                link(tt(eq[:, :, :], eq[:, :, :], over_tiles(rev), ALU.mult))
                link(V_.tensor_reduce(best, eq[:, :, :], AX.X, ALU.max))
                link(tt(oh[:, :, :], over_tiles(rev), best.unsqueeze(2).broadcast_to([P, T, E]), ALU.is_equal))

            def per_expert(v):
                return v.unsqueeze(2).broadcast_to([P, T, E])

            def RT(step, b):
                dve.wait_ge(*misc.full(step))
                lg = gl[b][:, :, 0:E]
                V_.tensor_copy(lg, misc_ps[:, 0:T * E].rearrange("p (t e) -> p t e", t=T)).then_inc(misc.read_sem(step), 1)
                dve.wait_ge(*misc.read(step))
                first_max(b, lg, oh1[b], gv[b][:, 0, :], 7)
                link(V_.scalar_tensor_tensor(out=g1[b][:, :, :], in0=oh1[b][:, :, :], scalar=-BIG, in1=lg,
                                             op0=ALU.mult, op1=ALU.add))
                first_max(b, g1[b][:, :, :], oh2[b], gv[b][:, 1, :], 6)
                tt(gx[b][:, :, 0], gv[b][:, 1, :], gv[b][:, 0, :], ALU.subtract).then_inc(done["RT"], 1)

            def RTE(step, b):
                dve.wait_ge(*after("RTE", b))
                e2, w1_, w2_ = gex[b][:, :, 0], gv[b][:, 2, :], gv[b][:, 3, :]
                link(V_.tensor_scalar(w2_, e2, 1.0, None, ALU.add))
                link(V_.reciprocal(w1_, w2_))
                link(tt(w2_, e2, w1_, ALU.mult))
                tt(oh1[b][:, :, :], oh1[b][:, :, :], per_expert(w1_), ALU.mult)
                link(tt(oh2[b][:, :, :], oh2[b][:, :, :], per_expert(w2_), ALU.mult))
                link(tt(gw[b][:, :, :], oh1[b][:, :, :], oh2[b][:, :, :], ALU.add))

            def GT(step, b):
                dve.wait_ge(*misc.full(step))
                tt(gl[b][:, :, :], misc_ps[:, 0:T * GW].rearrange("p (t e) -> p t e", t=T),
                   over_tiles(row["gates"][:, 0:GW]), ALU.add).then_inc(misc.read_sem(step), 1)
                dve.wait_ge(*misc.read(step))
                lg = gl[b][:, :, 2:GW].rearrange("p t (g e) -> p t g e", g=2)
                gmax, emax = gv[b][:, 0, :], g1[b][:, :, 0:2]
                V_.tensor_reduce(gmax, gl[b][:, :, 0:2], AX.X, ALU.max)
                link(V_.tensor_reduce(emax, lg, AX.X, ALU.max))
                tt(gx[b][:, :, 0:2], gl[b][:, :, 0:2], gmax.unsqueeze(2).broadcast_to([P, T, 2]), ALU.subtract)
                tt(gx[b][:, :, 2:GW].rearrange("p t (g e) -> p t g e", g=2), lg,
                   emax.unsqueeze(3).broadcast_to([P, T, 2, E // 2]), ALU.subtract).then_inc(done["GT"], 1)

            def GTE(step, b):
                dve.wait_ge(*after("GTE", b))
                eg = gex[b][:, :, 0:2]
                sel, ex = g1[b][:, :, 0:2], gex[b][:, :, 2:GW]
                gsum, esum, inv = gv[b][:, 1, :], gv[b][:, 2, :], gv[b][:, 3, :]
                V_.tensor_reduce(gsum, eg, AX.X, ALU.add)
                tt(sel[:, :, 1], eg[:, :, 1], eg[:, :, 0], ALU.is_gt)
                link(tt(sel[:, :, 0], eg[:, :, 0], eg[:, :, 1], ALU.is_ge))
                ex4 = ex.rearrange("p t (g e) -> p t g e", g=2)
                link(tt(ex4, ex4, sel.unsqueeze(3).broadcast_to([P, T, 2, E // 2]), ALU.mult))
                link(V_.tensor_reduce(esum, ex, AX.X, ALU.add))
                link(tt(inv, gsum, esum, ALU.mult))
                link(V_.reciprocal(inv, inv))
                first_max(b, ex, oh1[b], gv[b][:, 4, :], 7)
                link(V_.scalar_tensor_tensor(out=g1[b][:, :, :], in0=oh1[b][:, :, :], scalar=-BIG, in1=ex,
                                             op0=ALU.mult, op1=ALU.add))
                first_max(b, g1[b][:, :, :], oh2[b], gv[b][:, 5, :], 6)
                link(tt(oh1[b][:, :, :], oh1[b][:, :, :], oh2[b][:, :, :], ALU.add))
                link(tt(gw[b][:, :, :], ex, oh1[b][:, :, :], ALU.mult))
                link(tt(gw[b][:, :, :], gw[b][:, :, :], per_expert(inv), ALU.mult))

            def FH(step, b, e):
                n = nth[step] - 1
                dve.wait_ge(*scores.read(step))
                if n >= 2:
                    dve.wait_ge(*probs.full(("FY", (n - 2) // E, (n - 2) % E)))
                src = relu[n % 2]
                tt(h2[n % 2][:, :, :].rearrange("p c n -> p (c n)"), src, src, ALU.mult).then_inc(done["FH"], 1)

            def accumulate(src, w, acc, t):
                return V_.scalar_tensor_tensor(out=acc[:, t, :], in0=src, scalar=w, in1=acc[:, t, :],
                                               op0=ALU.mult, op1=ALU.add)

            def FY(step, b, e):
                dve.wait_ge(*probs.full(step))
                if e:
                    dve.wait_ge(*probs.read(("FY", b, e - 1)))
                ps = probs_ps[probs.buf(step)]
                for t in range(T):
                    last = accumulate(ps[:, t * P:(t + 1) * P], gw[b][:, t, e:e + 1], X[b], t)
                last.then_inc(probs.read_sem(step), 1)
                if e == E - 1:
                    dve.wait_ge(*probs.read(step))

            def GH(step, b, w):
                n = nth[step] - 1
                dve.wait_ge(*scores.read(step, 0))
                dve.wait_ge(*scores.full(step, 1))
                if b:
                    dve.wait_ge(*probs.full(("SO", 0) if w == 0 else ("RO", 0, T - 1, 1)))
                src = scores_ps[scores.buf(step, 1)][:, :, :].rearrange("p c n -> p (c n)")
                tt(gh[w][:, :, :].rearrange("p c n -> p (c n)"), src, relu[n % 2],
                   ALU.mult).then_inc(scores.read_sem(step, 1), 1)

            def SO(step, b):
                dve.wait_ge(*probs.full(step))
                tt(ACC[b][:, :, :], XN[b][:, :, :], probs_ps[probs.buf(step)][:, :].rearrange("p (t d) -> p t d", t=T),
                   ALU.add).then_inc(probs.read_sem(step), 1)
                dve.wait_ge(*probs.read(step))

            def RO(step, b, t, half):
                dve.wait_ge(*probs.full(step))
                ps = probs_ps[probs.buf(step)]
                for k in range(4):
                    e = 4 * half + k
                    last = accumulate(ps[:, k * P:(k + 1) * P], gw[b][:, t, e:e + 1], ACC[b], t)
                    if k < 3:
                        link(last)
                last.then_inc(probs.read_sem(step), 1)
                dve.wait_ge(*probs.read(step))

            def OUT(step, b):
                dve.wait_ge(*after("NORM", "r2", b))
                link(tt(ACC[b][:, :, :], ACC[b][:, :, :], over_tiles(row["norm2"]), ALU.mult))
                tt(ACC[b][:, :, :], ACC[b][:, :, :], X[b][:, :, :], ALU.add).then_inc(done["OUTV"], 1)

            parts = {"NORM": NORM, "CKV": CKV, "SPLITC": SPLITC, "QP": QP, "SPLITQ": SPLITQ, "KV": KV, "SPLITK": SPLITK,
                     "KT": KT, "QT": QT, "SMAX": SMAX, "MCH": MCH, "PV": PV, "OTR": OTR, "OP": OP, "Z1": Z1, "FIN1": FIN1,
                     "RT": RT, "RTE": RTE, "GT": GT, "GTE": GTE, "FH": FH, "FY": FY, "GH": GH, "SO": SO, "RO": RO,
                     "OUT": OUT}
            dve.wait_ge(loaded["consts"], 16)
            V_.tensor_copy(identb[:, :], ident).then_inc(consts_cast, 1)
            for step in schedule:
                if step[0] in parts:
                    parts[step[0]](step, *step[1:])


def rope_tables():
    inv = (1.0 / np.float32(10000.0) ** (np.arange(0, DH, 2, dtype=np.float32) / np.float32(DH))).astype(np.float32)
    ang = np.arange(N, dtype=np.float32)[:, None] * inv[None, :]
    cos = np.repeat(np.cos(ang), 2, axis=1)
    sin = np.repeat(np.sin(ang), 2, axis=1) * np.tile(np.array([-1.0, 1.0], np.float32), DH // 2)

    def lay(a):
        a = np.tile(a.astype(np.float32), (1, H)).reshape(T, P, P)
        return a.transpose(1, 0, 2).reshape(P, T * P)
    return lay(cos), lay(sin)


def kernel(**inputs):
    import concourse.bacc as bacc
    from concourse.bass_utils import run_bass_kernel_spmd

    a = {k: np.asarray(v) for k, v in inputs.items()}
    f32 = np.float32

    def chunks(w):
        return w.reshape(2, P, -1).transpose(1, 0, 2)

    x = a["x"].reshape(B, T, P, P).transpose(0, 2, 1, 3)
    wa = np.concatenate([a["L0_xattn_Wq"], a["L0_xattn_Wk"], a["L0_xattn_Wv"], a["L0_xattn_Wo"],
                         a["ctx_1024"].reshape(B * C, P).T], axis=1)
    cos, sin = rope_tables()
    consts = np.concatenate([np.eye(P, dtype=f32), cos, sin,
                             np.tile(np.arange(E, 0, -1, dtype=f32), (P, 1)), np.full((P, T), -0.5, f32)], axis=1)
    rows = np.concatenate([a["L0_xattn_bq"], a["L0_xattn_bk"], a["L0_xattn_bv"], a["L0_xattn_bo"],
                           a["L1_xattn_bq"], a["L1_xattn_bk"], a["L1_xattn_bv"], a["L1_xattn_gamma"],
                           a["L1_xattn_beta"], a["L1_ffn_norm1_w"], a["L1_ffn_norm2_w"],
                           a["L1_ffn_group_bias"], a["L1_ffn_expert_bias"], np.zeros(P - 2 - E, f32)])
    f0 = np.concatenate([a["L0_ffn_router_w"].T, a["L0_ffn_w1"].transpose(1, 0, 2).reshape(P, -1)], axis=1)
    f0y = a["L0_ffn_w2"].reshape(E, 2, P, P).transpose(2, 0, 1, 3).reshape(P, -1)
    dc = a["L1_ffn_Wk_c"].shape[1]
    wkvc = np.concatenate([a["L1_ffn_Wk_c"], a["L1_ffn_Wv_c"], np.zeros((P, P - 2 * dc), f32)], axis=1)
    wk2 = np.concatenate([a["L1_ffn_Wk"], np.zeros((P - dc, P), f32)], axis=0)
    wv2 = np.concatenate([np.zeros((dc, P), f32), a["L1_ffn_Wv"], np.zeros((P - 2 * dc, P), f32)], axis=0)
    wb = np.concatenate([a["L1_xattn_Wq"].T, a["L1_xattn_Wk"].T, a["L1_xattn_Wv"].T,
                         a["L1_ffn_Wq"], wkvc, wk2, wv2, a["L1_ffn_Wo"]], axis=1)
    w2x = a["L1_ffn_W2_experts"].reshape(E, 2, P, P).transpose(2, 1, 0, 3).reshape(P, -1)
    f1 = np.concatenate([a["L1_ffn_W_shared_in"], a["L1_ffn_W1_shared"],
                         chunks(a["L1_ffn_W_shared_out"]).reshape(P, -1), w2x,
                         a["L1_ffn_Wg_gate"], a["L1_ffn_We_gate"]], axis=1)

    nc = bacc.Bacc("TRN2", target_bir_lowering=False, num_devices=1)
    arrays, args = {}, []
    for name, arr in (("x", x), ("wa", wa), ("consts", consts), ("rows", rows), ("f0", f0), ("f0y", f0y),
                      ("wb", wb), ("f1", f1)):
        arr = np.ascontiguousarray(arr)
        arrays[f"in_{name}"] = arr
        args.append(nc.dram_tensor(f"in_{name}", arr.shape, F32, kind="ExternalInput").ap())
    out = nc.dram_tensor("out", (B, P, T, P), F32, kind="ExternalOutput").ap()
    build(nc, *args, out)
    r = run_bass_kernel_spmd(nc, [arrays], core_ids=[0])
    got = np.asarray(r.results[0]["out"])
    return got.transpose(0, 2, 1, 3).reshape(B, N, P)
```

```python
from contextlib import ExitStack

import numpy as np

import concourse.bass as bass
from concourse import mybir

F32 = mybir.dt.float32
BF16 = mybir.dt.bfloat16
ALU = mybir.AluOpType
ACT = mybir.ActivationFunctionType
AX = mybir.AxisListType

P = 128
B = 2
T = 4
N = T * P
H = 16
DH = P // H
C = 77
CP = 80
E = 8
HID = 256
GR = 4
HG = H // GR
HP = H // 2
NGRP = B * GR
VW = 32
LN_EPS, RMS_EPS = 1e-5, 1e-6
BIG = 3.0e38
TINY = 1e-30

SLOTS = 6
Q_PART = (0, 0, 1, 1, 0, 2)
K_PART = (0, 1, 0, 1, 2, 0)
HROWS = SLOTS * DH
MROW = 2 * HROWS

ROWS = ("bq0", "bk0", "bv0", "bo0", "bq1", "bk1", "bv1", "gamma", "beta", "norm1", "norm2", "gates")
NKT = (1, 1, T)
AHEAD = (2, 2, T + 1)
SCALE = (DH ** -0.5, 1.0, DH ** -0.5)


ORDER = """
    # Layer 0, cross attention: norm, projections and parts, then the head groups.
    STAT n0 0, CKV 0, NORM n0 0, XT n0 0, STAT n0 1, SPLITC 0, QP 0 0, SPLITQ 0 0, KTC 0 0, NORM n0 1,
    XT n0 1, QT 0 0 0, QT 0 0 1, QP 0 1, SMAX 0 0 0 0, SMAX 0 0 0 1, MCH 0 0, SPLITQ 0 1, SMAX 0 1 0 0,
    MTR 0 0, QT 0 1 1, SMAX 0 1 0 1, MCH 0 1,
    ST 0 0 0 0, KTC 0 1, SMAX 0 2 0 0, ST 0 0 0 1, SMAX 0 2 0 1, QT 0 1 0, MTR 0 1, SMAX 0 3 0 0, MCH 0 2,
    ST 0 1 0 0, ST 0 1 0 1, SMAX 0 3 0 1, OC 0 0, MTR 0 2, PV 0 0 0,
    ST 0 2 0 0, MCH 0 3, SMAX 0 4 0 0, SMAX 0 4 0 1, OTR 0 0, ST 0 2 0 1, MTR 0 3, PV 0 1 0, OC 0 1, MCH 0 4,
    ST 0 3 0 0, SMAX 0 5 0 0, OTR 0 1, SMAX 0 5 0 1, ST 0 3 0 1, MTR 0 4, MCH 0 5, PV 0 2 0, OC 0 2,
    SMAX 0 6 0 0, SMAX 0 6 0 1,
    ST 0 4 0 0, OTR 0 2, ST 0 4 0 1, MTR 0 5, OC 0 3, MCH 0 6, SMAX 0 7 0 0, PV 0 3 0,
    ST 0 5 0 0, OTR 0 3, XT z0 0, OP 0 0, STAT n1 0, SMAX 0 7 0 1, ST 0 5 0 1, OC 0 4, MTR 0 6, MCH 0 7,
    PV 0 4 0, PV 0 5 0, NORM n1 0, OTR 0 4,
    ST 0 6 0 0, ST 0 6 0 1, MTR 0 7, XT n1 0, OC 0 5, RT 0,
    ST 0 7 0 0, RTE 0, FH 0 0, OTR 0 5, OC 0 6, ST 0 7 0 1, OC 0 7, PV 0 6 0, OTR 0 6, PV 0 7 0, OTR 0 7,
    FH 0 1, XT z0 1,
    # Layer 0, experts, beside the last of the attention and the first of the next one.
    FY 0 0, OP 0 1, STAT n1 1, FH 0 2, NORM n1 1,
    FY 0 1, FH 0 3, XT n1 1,
    FY 0 2, FH 0 4,
    FY 0 3, FH 0 5, RT 1,
    FY 0 4, FH 0 6, CKV 1,
    FY 0 5, FH 0 7, SPLITC 1,
    FY 0 6, FH 1 0,
    FY 0 7, FH 1 1, KTC 1 0, RTE 1,
    FY 1 0, FH 1 2, STAT n2 0,
    FY 1 1, NORM n2 0, FH 1 3, KTC 1 1,
    FY 1 2, FH 1 4,
    FY 1 3, XT n2 0,
    FY 1 4, QP 1 0, SPLITQ 1 0, FH 1 5, FH 1 6, QT 1 0 0, QT 1 0 1,
    FY 1 5, SMAX 1 0 0 0, FH 1 7, SMAX 1 0 0 1,
    FY 1 6,
    FY 1 7, STAT n2 1, SMAX 1 1 0 0, MCH 1 0, NORM n2 1, MTR 1 0, SMAX 1 1 0 1, SMAX 1 2 0 0, MCH 1 1,
    # Layer 1, cross attention.
    ST 1 0 0 0, XT n2 1, MTR 1 1, SMAX 1 2 0 1, QP 1 1, ST 1 0 0 1, SPLITQ 1 1, SMAX 1 3 0 0,
    ST 1 1 0 0, ST 1 1 0 1, MCH 1 2, QT 1 1 1, MTR 1 2, SMAX 1 3 0 1, MCH 1 3, PV 1 0 0, OC 1 0,
    ST 1 2 0 0, QT 1 1 0, MTR 1 3, SMAX 1 4 0 0, OTR 1 0, SMAX 1 4 0 1, ST 1 2 0 1, PV 1 1 0, SMAX 1 5 0 0,
    ST 1 3 0 0, MCH 1 4, OC 1 1, SMAX 1 5 0 1, OTR 1 1, MTR 1 4, SMAX 1 6 0 0, MCH 1 5, ST 1 3 0 1, PV 1 2 0,
    OC 1 2, MTR 1 5,
    ST 1 4 0 0, SMAX 1 6 0 1, SMAX 1 7 0 0, OTR 1 2, ST 1 4 0 1, PV 1 3 0, OC 1 3, MCH 1 6, MTR 1 6,
    SMAX 1 7 0 1,
    ST 1 5 0 0, OTR 1 3, Z1 0, STAT n3 0, ST 1 5 0 1, MCH 1 7, PV 1 4 0, OC 1 4,
    ST 1 6 0 0, MTR 1 7, PV 1 5 0, NORM n3 0, FIN1 0, STAT n4 0, ST 1 6 0 1,
    ST 1 7 0 0, ST 1 7 0 1, NORM n4 0, XT n4 0, OC 1 5, OTR 1 5, OTR 1 4, PV 1 6 0, OC 1 6, OTR 1 6, QP 2 0,
    PV 1 7 0, OC 1 7, OTR 1 7, Z1 1, STAT n3 1, KVC 0,
    KV 0, SPLITK 0, SPLITQ 2 0, KT 0 0, NORM n3 1, KT 0 1, FIN1 1, KT 0 2, KT 0 3, QT 2 0 0, QT 2 0 1,
    SMAX 2 0 0 0, SMAX 2 0 0 1, SMAX 2 0 1 0, SMAX 2 0 1 1, SMAX 2 0 2 0, SMAX 2 0 2 1, SMAX 2 0 3 0,
    SMAX 2 0 3 1, MCH 2 0, SMAX 2 1 0 0, SMAX 2 1 0 1, MTR 2 0, SMAX 2 1 1 0,
    # Layer 1, self attention.
    ST 2 0 0 0, STAT n4 1, SMAX 2 1 1 1, ST 2 0 0 1, SMAX 2 1 2 0,
    ST 2 0 1 0, ST 2 0 1 1, PV 2 0 0, NORM n4 1,
    ST 2 0 2 0, SMAX 2 1 2 1, SMAX 2 1 3 0, PV 2 0 1, XT n4 1, ST 2 0 2 1, SMAX 2 1 3 1, MCH 2 1, KVC 1,
    SMAX 2 2 0 0, SMAX 2 2 0 1,
    ST 2 0 3 0, MTR 2 1, ST 2 0 3 1, SMAX 2 2 1 0, OC 2 0, QP 2 1,
    KV 1, PV 2 0 2, PV 2 0 3,
    ST 2 1 0 0, SMAX 2 2 1 1, OTR 2 0, ST 2 1 0 1,
    ST 2 1 1 0, SPLITK 1, SMAX 2 2 2 0, SMAX 2 2 2 1, ST 2 1 1 1, PV 2 1 0,
    ST 2 1 2 0, PV 2 1 1, ST 2 1 2 1, SMAX 2 2 3 0,
    ST 2 1 3 0, SMAX 2 2 3 1, ST 2 1 3 1, MCH 2 2, SMAX 2 3 0 0, PV 2 1 2, MTR 2 2, PV 2 1 3, OC 2 1, KT 1 0,
    ST 2 2 0 0, KT 1 1, SMAX 2 3 0 1, KT 1 2, KT 1 3, ST 2 2 0 1, SMAX 2 3 1 0, SMAX 2 3 1 1, SPLITQ 2 1,
    ST 2 2 1 0, QT 2 1 0, SMAX 2 3 2 0, ST 2 2 1 1, PV 2 2 0, SMAX 2 3 2 1, QT 2 1 1, OTR 2 1,
    ST 2 2 2 0, SMAX 2 3 3 0, ST 2 2 2 1, SMAX 2 3 3 1, PV 2 2 1,
    ST 2 2 3 0, PV 2 2 2, ST 2 2 3 1, MCH 2 3, MTR 2 3, SMAX 2 4 0 0, SMAX 2 4 0 1,
    ST 2 3 0 0, PV 2 2 3, OC 2 2, SMAX 2 4 1 0, ST 2 3 0 1, SMAX 2 4 1 1,
    ST 2 3 1 0, OTR 2 2, SMAX 2 4 2 0, SMAX 2 4 2 1, ST 2 3 1 1, PV 2 3 0,
    ST 2 3 2 0, SMAX 2 4 3 0, SMAX 2 4 3 1, MCH 2 4, ST 2 3 2 1, PV 2 3 1,
    ST 2 3 3 0, ST 2 3 3 1, SMAX 2 5 0 0, MTR 2 4, PV 2 3 2, SMAX 2 5 0 1,
    ST 2 4 0 0, PV 2 3 3, OC 2 3, ST 2 4 0 1, SMAX 2 5 1 0, SMAX 2 5 1 1,
    ST 2 4 1 0, PV 2 4 0, SMAX 2 5 2 0, ST 2 4 1 1, SMAX 2 5 2 1, OTR 2 3,
    ST 2 4 2 0, SMAX 2 5 3 0, SMAX 2 5 3 1, MCH 2 5, ST 2 4 2 1, PV 2 4 1,
    ST 2 4 3 0, SMAX 2 6 0 0, ST 2 4 3 1, MTR 2 5, SMAX 2 6 0 1, PV 2 4 2,
    ST 2 5 0 0, SMAX 2 6 1 0, XT z2 0, SMAX 2 6 1 1, ST 2 5 0 1, PV 2 4 3, SMAX 2 6 2 0, OC 2 4,
    ST 2 5 1 0, SMAX 2 6 2 1, PV 2 5 0, ST 2 5 1 1, SMAX 2 6 3 0, OP 2 0, SMAX 2 6 3 1,
    ST 2 5 2 0, PV 2 5 1, STAT r1 0, MCH 2 6, SMAX 2 7 0 0, ST 2 5 2 1,
    ST 2 5 3 0, OTR 2 4, NORM r1 0, ST 2 5 3 1, MTR 2 6, SMAX 2 7 0 1, PV 2 5 2,
    ST 2 6 0 0, XT fl 0, SMAX 2 7 1 0, SMAX 2 7 1 1, ST 2 6 0 1, PV 2 5 3, OC 2 5,
    ST 2 6 1 0, SMAX 2 7 2 0, SMAX 2 7 2 1, OTR 2 5, ST 2 6 1 1, PV 2 6 0,
    ST 2 6 2 0, SMAX 2 7 3 0, SMAX 2 7 3 1, GT 0, ST 2 6 2 1, PV 2 6 1,
    ST 2 6 3 0, GH 0 0, ST 2 6 3 1, MCH 2 7, PV 2 6 2, PV 2 6 3, MTR 2 7, OC 2 6,
    # Layer 1, shared and routed experts.
    SO 0, GTE 0,
    ST 2 7 0 0, OTR 2 6, ST 2 7 0 1,
    ST 2 7 1 0, GH 0 1, ST 2 7 1 1, PV 2 7 0,
    ST 2 7 2 0, ST 2 7 2 1, PV 2 7 1,
    ST 2 7 3 0, PV 2 7 2, ST 2 7 3 1, OC 2 7, PV 2 7 3, OTR 2 7, RO 0 0 0, XT z2 1, OP 2 1, STAT r1 1,
    RO 0 0 1, NORM r1 1, RO 0 1 0, RO 0 1 1, STAT r2 0, XT fl 1, GH 1 0, NORM r2 0, GT 1, GH 1 1, GTE 1,
    SO 1, RO 1 0 0, RO 1 0 1, RO 1 1 0, OUT 0, RO 1 1 1, STAT r2 1, NORM r2 1, OUT 1
"""

BORROWING = """
    CKV 0, XT n0 0, XT n0 1, QP 0 1, MTR 0 2, MTR 0 3, MTR 0 4, MTR 0 5, OTR 0 3, XT z0 0, MTR 0 6, MTR 0 7,
    XT n1 0, OTR 0 5, XT n1 1, CKV 1, XT n2 0, QP 1 0, MTR 1 0, MTR 1 1, QP 1 1, MTR 1 5, MTR 1 7, XT n4 0,
    QP 2 0, KVC 0, OTR 2 0, OTR 2 4
"""


def steps_of(text):
    rows_ = [line for line in text.splitlines() if not line.strip().startswith("#")]
    entries = [entry.split() for entry in " ".join(rows_).split(",")]
    return [tuple(int(w) if w.isdigit() else w for w in entry) for entry in entries]


BORROW = set(steps_of(BORROWING))


def make_schedule():
    return steps_of(ORDER)


def psum_uses(step):
    kind = step[0]
    if kind == "SMAX":
        return ["scores"]
    if kind == "ST":
        return ["probs"] * (HG // 2)
    if kind in ("QT", "KT", "KTC", "KV", "FH", "RO"):
        return ["scores"]
    if kind == "GH":
        return ["scores"] * 2
    if kind in ("FY", "SO"):
        return ["probs"]
    if kind == "OTR" and step[1] == 1:
        return []
    if kind in ("XT", "QP", "CKV", "OP", "RT", "GT", "KVC", "MTR", "OTR"):
        return ["scores" if step in BORROW else "misc"]
    return []


class Unit:

    def __init__(self, name, buffers, new_sem, schedule):
        self.full_sems = [new_sem(f"{name}{i}_full") for i in range(buffers)]
        self.read_sems = [new_sem(f"{name}{i}_read") for i in range(buffers)]
        self.n = buffers
        self.turn = {}
        for step in schedule:
            for k, unit in enumerate(psum_uses(step)):
                if unit == name:
                    self.turn[step, k] = len(self.turn)

    def buf(self, step, k=0):
        return self.turn[step, k] % self.n

    def reused(self, step, k=0):
        return self.turn[step, k] >= self.n

    def free(self, step, k=0):
        t = self.turn[step, k]
        return self.read_sems[t % self.n], t // self.n

    def full(self, step, k=0):
        t = self.turn[step, k]
        return self.full_sems[t % self.n], t // self.n + 1

    def read(self, step, k=0):
        t = self.turn[step, k]
        return self.read_sems[t % self.n], t // self.n + 1

    def full_sem(self, step, k=0):
        return self.full_sems[self.buf(step, k)]

    def read_sem(self, step, k=0):
        return self.read_sems[self.buf(step, k)]


class Either:

    def __init__(self, misc, scores):
        self.of = lambda step: scores if step in BORROW else misc

    def reused(self, step):
        return self.of(step).reused(step)

    def free(self, step):
        return self.of(step).free(step)

    def full(self, step):
        return self.of(step).full(step)

    def read(self, step):
        return self.of(step).read(step)

    def full_sem(self, step):
        return self.of(step).full_sem(step)

    def read_sem(self, step):
        return self.of(step).read_sem(step)


def build(nc, d_x, d_wa, d_consts, d_rows, d_f0, d_f0y, d_wb, d_f1, d_out):
    schedule = make_schedule()
    ctx = ExitStack()
    with ctx:
        def sb(name, shape, dt=F32):
            return ctx.enter_context(nc.sbuf_tensor(name, shape, dt))

        def psum(name, shape, dt=F32):
            return ctx.enter_context(nc.psum_tensor(name, shape, dt))

        def sem(name):
            return ctx.enter_context(nc.semaphore(name))

        wa = sb("wa", [P, 4 * P + B * C])
        wq0, wkv0, wo0 = wa[:, 0:P], wa[:, P:3 * P], wa[:, 3 * P:4 * P]
        ctxT = wa[:, 4 * P:4 * P + B * C].rearrange("p (b c) -> p b c", b=B)
        consts = sb("consts", [P, P + 2 * T * P + E + T])
        ident = consts[:, 0:P]
        cosf = consts[:, P:P + N]
        sinf = consts[:, P + N:P + 2 * N]
        rev = consts[:, P + 2 * N:P + 2 * N + E]
        minus_half = consts[:, P + 2 * N + E:P + 2 * N + E + T]
        rows = sb("rows", [P, len(ROWS) * P])
        row = {name: rows[:, i * P:(i + 1) * P] for i, name in enumerate(ROWS)}
        f0 = sb("f0", [P, E + E * HID])
        rw = f0[:, 0:E]
        w1 = f0[:, E:E + E * HID].rearrange("p (e c h) -> p e c h", e=E, c=2)
        f0y = sb("f0y", [P, E * 2 * P])
        w2 = f0y[:, :].rearrange("p (e c d) -> p e c d", e=E, c=2)
        wb = sb("wb", [P, 8 * P])
        wq1, wkv1 = wb[:, 0:P], wb[:, P:3 * P]
        wq2, wkvc, wkv2, wo2 = wb[:, 3 * P:4 * P], wb[:, 4 * P:5 * P], wb[:, 5 * P:7 * P], wb[:, 7 * P:8 * P]
        GW = 2 + E
        f1 = sb("f1", [P, 2 * 2 * HID + 2 * P + 2 * E * P + GW])
        win = f1[:, 0:4 * HID].rearrange("p (w m h) -> p w m h", w=2, m=4)
        wso = f1[:, 4 * HID:4 * HID + 2 * P].rearrange("p (c d) -> p c d", c=2)
        w2x = f1[:, 4 * HID + 2 * P:4 * HID + 2 * P + 2 * E * P].rearrange("p (c f n) -> p c f n", c=2, f=2)
        wgate = f1[:, 4 * HID + 2 * P + 2 * E * P:]
        wq = (wq0, wq1, wq2)
        wkvx = (wkv0, wkv1)
        identb = sb("identb", [P, P], BF16)

        def pair(name, shape, dt=F32):
            return [sb(f"{name}{b}", shape, dt) for b in range(B)]

        X = pair("X", [P, T, P])
        XN = pair("XN", [P, T, P])
        XT = pair("XT", [P, N])
        Z = pair("Z", [P, T, P])
        ACC = pair("ACC", [P, T, P])
        QF = [ACC[b][:, :, :].rearrange("p t d -> p (t d)") for b in range(B)]
        KF = [f0[:, E + b * N:E + (b + 1) * N] for b in range(B)]
        RS = [Z[b][:, :, :].rearrange("p t d -> p (t d)") for b in range(B)]
        RSP = f0[:, E + B * N:E + (B + 1) * N]
        qcat = pair("qcat", [P, T, HP, P], BF16)
        qT = pair("qT", [P, HP, N], BF16)
        kcat = sb("kcat", [P, T, H, P], BF16)
        kT = pair("kT", [P, H, N], BF16)
        kTc = [pair(f"kTc{l}", [P, H, CP], BF16) for l in range(2)]
        V = pair("V", [P, T, H, VW])
        Vc = [pair(f"Vc{l}", [P, H, VW]) for l in range(2)]
        mx = [sb(f"mx{i}", [P, T, HG]) for i in range(2)]
        mrs = [sb(f"mrs{i}", [P, T, HG]) for i in range(2)]
        mcat = [sb(f"mcat{i}", [P, T, 2, P], BF16) for i in range(2)]
        pT = [sb(f"pT{i}", [P, HG, N]) for i in range(2)]
        oT = [sb(f"oT{i}", [P, N]) for i in range(2)]
        kf = oT[0][:, 0:B * P].rearrange("p (b d) -> p b d", b=B)
        rinv = [sb(f"rinv{i}", [P, T, HG]) for i in range(2)]
        kflat = [kT[b][:, :, :].bitcast(F32).rearrange("p h n -> p (h n)") for b in range(B)]
        relu = [kflat[0][:, 2 * N * (2 + i):2 * N * (3 + i)] for i in range(2)]
        h2 = [kflat[0][:, 2 * N * i:2 * N * (i + 1)].rearrange("p (c n) -> p c n", c=2) for i in range(2)]
        gh = h2
        kvc = [kflat[1][:, N * b:N * (b + 1)] for b in range(B)]
        bn = pair("bn", [P, T, 6])
        mv = pair("mv", [P, T, 2])
        var = pair("var", [P, T])
        rstd = pair("rstd", [P, T])
        gl = pair("gl", [P, T, GW])
        gx = pair("gx", [P, T, GW])
        gex = pair("gex", [P, T, GW])
        g1 = pair("g1", [P, T, E])
        g2 = pair("g2", [P, T, E])
        oh1 = pair("oh1", [P, T, E])
        oh2 = pair("oh2", [P, T, E])
        gv = pair("gv", [P, 8, T])
        gw = pair("gw", [P, T, E])

        scores_ps = [psum(f"scores_ps{i}", [P, 2, 512]) for i in range(2)]
        probs_ps = [psum(f"probs_ps{i}", [P, 512]) for i in range(2)]
        misc_ps = psum("misc_ps", [P, 512])
        out_ps = psum("out_ps", [P, 512])
        scores = Unit("scores", 2, sem, schedule)
        probs = Unit("probs", 2, sem, schedule)
        misc = Either(Unit("misc", 1, sem, schedule), scores)

        def small_ps(step):
            return scores_ps[scores.buf(step)][:, 0, :] if step in BORROW else misc_ps[:, :]


        kinds = {"NORM": "normed", "SPLITQ": "query_parts", "SPLITC": "context_parts", "SPLITK": "key_parts",
                 "MCH": "max_parts", "FH": "hidden", "RT": "router_diffs", "RTE": "router_exps",
                 "GT": "gate_diffs", "GTE": "gate_exps", "OP": "projected", "KV": "values",
                 "FIN1": "cross_attended", "PV": "pv", "NORMSTATS": "stats", "RSTD": "rstds",
                 "OUTV": "out_rows", "GUARD": "guarded", "OC": "out_ps_read", "QP": "rotated_queries"}
        done = {k: sem(f"{n}_done") for k, n in kinds.items()}
        base = {"NORMSTATS": "STAT", "RSTD": "STAT", "OUTV": "OUT"}
        seen, nth = {}, {}
        for step in schedule:
            seen[step[0]] = seen.get(step[0], 0) + 1
            nth[step] = seen[step[0]]

        def after(kind, *args):
            return done[kind], nth[(base.get(kind, kind),) + args]

        loaded = {n: sem(f"{n}_loaded") for n in ("x0", "x1", "wa", "consts", "rows", "f0", "f0y", "wb", "f1")}
        stored = [sem(f"stored{b}") for b in range(B)]
        zeroed = sem("zeroed")
        consts_cast = sem("consts_cast")
        dve_chain = sem("dve_chain")
        pool_chain = sem("pool_chain")
        ZERO = {"Vc": 1, "qcat0": 2, "mcat": 3, "qcat1": 4, "pT": 5, "V": 6}

        source = {"n0": XN, "n1": XN, "n2": XN, "n4": XN, "fl": XN, "z0": Z, "z2": Z}

        def slot(cat, first, pairs, s, parts=P):
            wide = 2 * P if cat is kcat else P
            step = P + HROWS if cat is kcat else HROWS
            size = int(np.prod(cat.shape[1:]))
            return bass.AP(cat, first * wide + DH * s, [[size, parts], [wide, pairs], [step, 2], [1, DH]])

        def flat_heads(t, parts=P):
            return t.rearrange("p (n e d) -> p n e d", e=2, d=DH)

        def flat(t):
            return t[:, :, :].rearrange("p t d -> p (t d)")

        def over_tiles(r, n=T):
            return r.unsqueeze(1).broadcast_to([P, n, r.shape[1]])

        block = ctx.enter_context(nc.Block())

        @block.sync
        def _(sp):
            sp.dma_start(X[0][:, :, :], d_x[0]).then_inc(loaded["x0"], 16)
            sp.dma_start(wa[:, :], d_wa).then_inc(loaded["wa"], 16)
            sp.dma_start(X[1][:, :, :], d_x[1]).then_inc(loaded["x1"], 16)
            sp.dma_start(f0[:, :], d_f0).then_inc(loaded["f0"], 16)
            sp.dma_start(f0y[:, :], d_f0y).then_inc(loaded["f0y"], 16)
            sp.dma_start(wb[:, :], d_wb).then_inc(loaded["wb"], 16)
            sp.dma_start(f1[:, :], d_f1).then_inc(loaded["f1"], 16)
            for b in range(B):
                sp.wait_ge(*after("OUTV", b))
                sp.dma_start(d_out[b], ACC[b][:, :, :]).then_inc(stored[b], 16)
            for b in range(B):
                sp.wait_ge(stored[b], 16)

        @block.gpsimd
        def _(pool):
            U32 = mybir.dt.uint32
            for l in range(2):
                for b in range(B):
                    last = pool.memset(Vc[l][b][:, :, :], 0.0)
            last.then_inc(zeroed, 1)
            pool.memset(qcat[0][:, :, :, :].bitcast(U32), 0).then_inc(zeroed, 1)
            pool.wait_ge(loaded["consts"], 16)

            def background(n):
                if n == 0:
                    pool.memset(mcat[0][:, :, :, :].bitcast(U32), 0)
                    pool.memset(mcat[1][:, :, :, :].bitcast(U32), 0).then_inc(zeroed, 1)
                elif n == 1:
                    pool.memset(pT[0][:, :, :], 0.0)
                    pool.memset(qcat[1][:, :, :, :].bitcast(U32), 0).then_inc(zeroed, 1)
                    pool.memset(pT[1][:, :, :], 0.0).then_inc(zeroed, 1)
                    pool.memset(V[0][:, :, :, :], 0.0)
                    pool.memset(V[1][:, :, :, :], 0.0).then_inc(zeroed, 1)

            def STAT(step, kind, b):
                pool.wait_ge(*after("NORMSTATS", kind, b))
                pool.tensor_tensor(rstd[b][:, :], var[b][:, :], minus_half, ALU.pow).then_inc(done["RSTD"], 1)

            chain = [0]

            def link(ins):
                chain[0] += 1
                ins.then_inc(pool_chain, 1)
                pool.wait_ge(pool_chain, chain[0])

            def tt(out, a, c, op):
                return pool.tensor_tensor(out, a, c, op)

            def FIN1(step, b):
                if b == 0:
                    return
                pool.wait_ge(*after("NORM", "n3", b))
                link(tt(ACC[b][:, :, :], ACC[b][:, :, :], over_tiles(row["gamma"]), ALU.mult))
                link(tt(ACC[b][:, :, :], ACC[b][:, :, :], over_tiles(row["beta"]), ALU.add))
                tt(X[b][:, :, :], X[b][:, :, :], ACC[b][:, :, :], ALU.add).then_inc(done["FIN1"], 1)

            def ST(step, layer, i, kt, half):
                if layer != 1:
                    return
                n = (nth[step] - 1) // 2
                pool.wait_ge(*probs.read(step, 0))
                pool.wait_ge(*probs.read(step, 1))
                heads = pT[n % 2][0:C, 2 * half:2 * half + 2, :]
                pool.tensor_scalar(heads, heads, 0.0, None, ALU.max).then_inc(done["GUARD"], 1)

            def SPLITQ(step, layer, b):
                if (layer, b) != (2, B - 1):
                    return
                pool.wait_ge(done["QP"], B)
                def dst(s):
                    return slot(qcat[b], 0, T * HP, s)
                def copy(out, src):
                    return pool.tensor_scalar(out, src, 1.0, None, ALU.mult)
                values, rest = flat_heads(QF[b]), flat_heads(RSP)
                s0, s1, s2 = (Q_PART.index(k) for k in range(3))
                link(copy(dst(s0), values))
                link(tt(rest, values, dst(s0), ALU.subtract))
                link(copy(dst(s1), rest))
                for s, k in enumerate(Q_PART):
                    if k < 2 and s != (s0, s1)[k]:
                        copy(dst(s), dst((s0, s1)[k]))
                tt(dst(s2), rest, dst(s1), ALU.subtract).then_inc(done["SPLITQ"], 1)

            parts = {"STAT": STAT, "FIN1": FIN1, "ST": ST, "SPLITQ": SPLITQ}
            stats = 0
            for step in schedule:
                if step[0] in parts:
                    parts[step[0]](step, *step[1:])
                if step[0] == "STAT":
                    background(stats)
                    stats += 1

        @block.tensor
        def _(pe):
            def mm(out, lhsT, rhs, start=True, stop=True):
                return nc.tensor.matmul(out, lhsT, rhs, start=start, stop=stop)

            def wait_free(unit, step):
                if unit.reused(step):
                    pe.wait_ge(*unit.free(step))

            def XTstep(step, kind, b):
                if kind[0] == "z":
                    pe.wait_ge(*misc.read(("OTR", int(kind[1]), b * GR + GR - 1)))
                else:
                    pe.wait_ge(*after("NORM", {"fl": "r1"}.get(kind, kind), b))
                wait_free(misc, step)
                for t in range(T):
                    last = nc.tensor.transpose(small_ps(step)[:, t * P:(t + 1) * P], source[kind][b][:, t, :], ident)
                last.then_inc(misc.full_sem(step), 1)

            def project(step, b, w, width, xt_step):
                pe.wait_ge(*misc.read(xt_step))
                wait_free(misc, step)
                for t in range(T):
                    last = mm(small_ps(step)[:, t * width:(t + 1) * width], XT[b][:, t * P:(t + 1) * P], w)
                last.then_inc(misc.full_sem(step), 1)

            def QP(step, layer, b):
                if layer:
                    pe.wait_ge(loaded["wb"], 16)
                else:
                    pe.wait_ge(loaded["wa"], 16)
                project(step, b, wq[layer], P, ("XT", ("n0", "n2", "n4")[layer], b))

            def OP(step, layer, b):
                project(step, b, wo0 if layer == 0 else wo2, P, ("XT", "z0" if layer == 0 else "z2", b))

            def RT(step, b):
                if b == 0:
                    pe.wait_ge(loaded["f0"], 16)
                project(step, b, rw, E, ("XT", "n1", b))

            def GT(step, b):
                if b == 0:
                    pe.wait_ge(loaded["f1"], 16)
                project(step, b, wgate, GW, ("XT", "fl", b))

            def CKV(step, layer):
                pe.wait_ge(loaded["wb" if layer else "wa"], 16)
                wait_free(misc, step)
                for b in range(B):
                    last = mm(small_ps(step)[0:C, b * 2 * P:(b + 1) * 2 * P], ctxT[:, b, :], wkvx[layer])
                last.then_inc(misc.full_sem(step), 1)

            def KVC(step, b):
                pe.wait_ge(*misc.read(("XT", "n4", b)))
                wait_free(misc, step)
                mm(small_ps(step), wkvc, XT[b][:, :]).then_inc(misc.full_sem(step), 1)

            def KV(step, b):
                pe.wait_ge(*misc.read(("KVC", b)))
                wait_free(scores, step)
                ps = scores_ps[scores.buf(step)]
                for t in range(T):
                    last = mm(ps[:, t // 2, (t % 2) * 256:(t % 2) * 256 + 256], kvc[b][:, t * P:(t + 1) * P], wkv2)
                last.then_inc(scores.full_sem(step), 1)

            def KTC(step, layer, b):
                pe.wait_ge(*after("SPLITC", layer))
                wait_free(scores, step)
                ps = scores_ps[scores.buf(step)][:, :, :].bitcast(BF16)
                for h in range(H):
                    o = (h % 8) * CP
                    last = nc.tensor.transpose(ps[:, h // 8, o:o + C], kcat[0:C, 2 * layer + b, h, :], identb[0:C, 0:C])
                last.then_inc(scores.full_sem(step), 1)

            def KT(step, b, t):
                pe.wait_ge(*after("SPLITK", b))
                wait_free(scores, step)
                ps = scores_ps[scores.buf(step)][:, :, :].bitcast(BF16)
                for h in range(H):
                    o = (h % 8) * P
                    last = nc.tensor.transpose(ps[:, h // 8, o:o + P], kcat[:, t, h, :], identb[:, :])
                last.then_inc(scores.full_sem(step), 1)

            def QT(step, layer, b, u):
                pe.wait_ge(*after("SPLITQ", layer, b))
                wait_free(scores, step)
                ps = scores_ps[scores.buf(step)][:, :, :].bitcast(BF16)
                for t in range(2):
                    for p in range(HP):
                        last = nc.tensor.transpose(ps[:, t, p * P:(p + 1) * P], qcat[b][:, 2 * u + t, p, :], identb[:, :])
                last.then_inc(scores.full_sem(step), 1)

            def SMAX(step, layer, i, part, u):
                b, g = divmod(i, GR)
                if i % GR == 0 and part == 0 and u == 0:
                    for k in range(2):
                        pe.wait_ge(*scores.read(("QT", layer, b, k)))
                    for k in range(T if layer == 2 else 1):
                        pe.wait_ge(*scores.read(("KT", b, k) if layer == 2 else ("KTC", layer, b)))
                wait_free(scores, step)
                ps = scores_ps[scores.buf(step)]
                for k in range(2):
                    if layer == 2:
                        pr = 2 * g + u
                        last = mm(ps[:, k, :], qT[b][:, pr, part * P:(part + 1) * P], kT[b][:, 2 * pr + k, :])
                    else:
                        t = 2 * u + k
                        for pr in range(2):
                            a = 2 * g + pr
                            last = mm(ps[:, k, pr * 2 * C:(pr + 1) * 2 * C], qT[b][:, a, t * P:(t + 1) * P],
                                      kTc[layer][b][:, 2 * a:2 * a + 2, 0:C])
                last.then_inc(scores.full_sem(step), 1)

            def MTR(step, layer, i):
                pe.wait_ge(*after("MCH", layer, i))
                wait_free(misc, step)
                ps = small_ps(step).bitcast(BF16)
                for pr in range(2):
                    for t in range(T):
                        o = (pr * T + t) * P
                        last = nc.tensor.transpose(ps[:, o:o + P], mcat[i % 2][:, t, pr, :], identb[:, :])
                last.then_inc(misc.full_sem(step), 1)

            def ST(step, layer, i, kt, half):
                b, g = divmod(i, GR)
                if kt == 0 and half == 0:
                    pe.wait_ge(*misc.read(("MTR", layer, i)))
                for k in range(2):
                    h = HG * g + 2 * half + k
                    if probs.reused(step, k):
                        pe.wait_ge(*probs.free(step, k))
                    ps = probs_ps[probs.buf(step, k)]
                    if layer == 2:
                        out, keys = ps[:, :], kT[b][:, h, kt * P:(kt + 1) * P]
                    else:
                        out, keys = ps[0:C, :], kTc[layer][b][:, h, 0:C]
                    mm(out, keys, qT[b][:, h // 2, :]).then_inc(probs.full_sem(step, k), 1)

            def PV(step, layer, i, kt):
                b, g = divmod(i, GR)
                if layer == 2 and i % GR == 0 and kt == 0:
                    pe.wait_ge(*after("KV", b))
                if kt == 0 and (layer or i):
                    pe.wait_ge(done["OC"], layer * NGRP + i)
                for j in range(HG):
                    if layer == 1:
                        pe.wait_ge(done["GUARD"], 2 * i + j // 2 + 1)
                    else:
                        pe.wait_ge(*probs.read(("ST", layer, i, kt, j // 2), j % 2))
                    h = HG * g + j
                    vals = V[b][:, kt, h, :] if layer == 2 else Vc[layer][b][:, h, :]
                    last = mm(out_ps[j * VW:(j + 1) * VW, :], vals, pT[(nth[step] - 1) % 2][:, j, :],
                              start=(kt == 0), stop=(kt == NKT[layer] - 1))
                last.then_inc(done["PV"], 1)

            def OTR(step, layer, i):
                if layer == 1:
                    return
                pe.wait_ge(*after("OC", layer, i))
                wait_free(misc, step)
                for t in range(T):
                    last = nc.tensor.transpose(small_ps(step)[:, t * P:(t + 1) * P], oT[i % 2][:, t * P:(t + 1) * P], ident)
                last.then_inc(misc.full_sem(step), 1)

            def FH(step, b, e):
                if e == 0:
                    pe.wait_ge(*misc.read(("XT", "n1", b)))
                wait_free(scores, step)
                ps = scores_ps[scores.buf(step)]
                for c in range(2):
                    last = mm(ps[:, c, :], w1[:, e, c, :], XT[b][:, :])
                last.then_inc(scores.full_sem(step), 1)

            def FY(step, b, e):
                if b == 0 and e == 0:
                    pe.wait_ge(loaded["f0y"], 16)
                pe.wait_ge(*after("FH", b, e))
                pe.wait_ge(*probs.free(step))
                ps = probs_ps[probs.buf(step)]
                for t in range(T):
                    for c in range(2):
                        last = mm(ps[:, t * P:(t + 1) * P], h2[e % 2][:, c, t * P:(t + 1) * P], w2[:, e, c, :],
                                  start=(c == 0), stop=(c == 1))
                last.then_inc(probs.full_sem(step), 1)

            def GH(step, b, w):
                if w == 0:
                    pe.wait_ge(*misc.read(("XT", "fl", b)))
                for half in range(2):
                    pe.wait_ge(*scores.free(step, half))
                    ps = scores_ps[scores.buf(step, half)]
                    for c in range(2):
                        last = mm(ps[:, c, :], win[:, w, 2 * half + c, :], XT[b][:, :])
                    last.then_inc(scores.full_sem(step, half), 1)

            def SO(step, b):
                pe.wait_ge(*scores.read(("GH", b, 0), 1))
                pe.wait_ge(*probs.free(step))
                ps = probs_ps[probs.buf(step)]
                for t in range(T):
                    for c in range(2):
                        last = mm(ps[:, t * P:(t + 1) * P], gh[0][:, c, t * P:(t + 1) * P], wso[:, c, :],
                                  start=(c == 0), stop=(c == 1))
                last.then_inc(probs.full_sem(step), 1)

            def RO(step, b, pr, half):
                if pr == 0 and half == 0:
                    pe.wait_ge(*scores.read(("GH", b, 1), 1))
                wait_free(scores, step)
                ps = scores_ps[scores.buf(step)]
                for u in range(2):
                    t = 2 * pr + u
                    for c in range(2):
                        last = mm(ps[:, u, :], gh[1][:, c, t * P:(t + 1) * P], w2x[:, c, half, :],
                                  start=(c == 0), stop=(c == 1))
                last.then_inc(scores.full_sem(step), 1)

            parts = {"XT": XTstep, "QP": QP, "OP": OP, "RT": RT, "GT": GT, "CKV": CKV, "KVC": KVC, "KV": KV,
                     "KTC": KTC, "KT": KT, "QT": QT, "SMAX": SMAX, "MTR": MTR, "ST": ST, "PV": PV, "OTR": OTR,
                     "FH": FH, "FY": FY, "GH": GH, "SO": SO, "RO": RO}
            pe.wait_ge(loaded["consts"], 16)
            pe.wait_ge(consts_cast, 1)
            for step in schedule:
                if step[0] in parts:
                    parts[step[0]](step, *step[1:])

        @block.scalar
        def _(act):
            act.dma_start(consts[:, :], d_consts).then_inc(loaded["consts"], 16)
            act.dma_start(rows[:, :], d_rows.partition_broadcast(P)).then_inc(loaded["rows"], 16)

            def XTstep(step, kind, b):
                act.wait_ge(*misc.full(step))
                nc.scalar.copy(XT[b][:, :], small_ps(step)).then_inc(misc.read_sem(step), 1)

            def KVC(step, b):
                act.wait_ge(*misc.full(step))
                nc.scalar.copy(kvc[b], small_ps(step)).then_inc(misc.read_sem(step), 1)

            def KTC(step, layer, b):
                act.wait_ge(*scores.full(step))
                src = scores_ps[scores.buf(step)][:, :, :].bitcast(BF16)[:, :, 0:8 * CP]
                src = src.rearrange("p a (h c) -> p a h c", c=CP)[:, :, :, 0:C]
                dst = kTc[layer][b][:, :, :].rearrange("p (a h) c -> p a h c", a=2)[:, :, :, 0:C]
                nc.scalar.copy(dst, src).then_inc(scores.read_sem(step), 1)

            def KT(step, b, t):
                if t % 2:
                    return
                act.wait_ge(*scores.full(step))
                src = scores_ps[scores.buf(step)][:, :, :].bitcast(BF16)
                src = src.rearrange("p a (h c) -> p (a h) c", c=P)
                nc.scalar.copy(kT[b][:, :, t * P:(t + 1) * P], src).then_inc(scores.read_sem(step), 1)

            def QT(step, layer, b, u):
                if u:
                    return
                act.wait_ge(*scores.full(step))
                src = scores_ps[scores.buf(step)][:, :, :].bitcast(BF16).rearrange("p t (a c) -> p t a c", c=P)
                dst = qT[b][:, :, 2 * u * P:2 * (u + 1) * P].rearrange("p a (t c) -> p t a c", t=2)
                nc.scalar.copy(dst, src).then_inc(scores.read_sem(step), 1)

            def MTR(step, layer, i):
                if layer < 2:
                    return
                b, g = divmod(i, GR)
                act.wait_ge(*misc.full(step))
                src = small_ps(step)[MROW:MROW + 6, :].bitcast(BF16).rearrange("p (a n) -> p a n", a=2)
                nc.scalar.copy(qT[b][MROW:MROW + 6, 2 * g:2 * g + 2, :], src).then_inc(misc.read_sem(step), 1)

            def ST(step, layer, i, kt, half):
                parts_ = P if layer == 2 else C
                n = (nth[step] - 1) // 2
                if n == 0 and half == 0:
                    act.wait_ge(zeroed, ZERO["pT"])
                if n >= 2 and half == 0:
                    act.wait_ge(done["PV"], n - 1)
                for k in range(2):
                    act.wait_ge(*probs.full(step, k))
                    nc.scalar.activation(pT[n % 2][0:parts_, 2 * half + k, :], probs_ps[probs.buf(step, k)][0:parts_, :],
                                         ACT.Exp, scale=SCALE[layer]).then_inc(probs.read_sem(step, k), 1)

            def OC(step, layer, i):
                if layer == 1:
                    return
                act.wait_ge(*after("PV", layer, i, NKT[layer] - 1))
                if i >= 2:
                    act.wait_ge(*misc.full(("OTR", layer, i - 2)))
                nc.scalar.copy(oT[i % 2][:, :], out_ps[:, :]).then_inc(done["OC"], 1)

            def RTE(step, b):
                act.wait_ge(*after("RT", b))
                nc.scalar.activation(gex[b][:, :, 0:1], gx[b][:, :, 0:1], ACT.Exp).then_inc(done["RTE"], 1)

            def GTE(step, b):
                act.wait_ge(*after("GT", b))
                nc.scalar.activation(gex[b][:, :, :], gx[b][:, :, :], ACT.Exp).then_inc(done["GTE"], 1)

            def FH(step, b, e):
                n = nth[step] - 1
                if n >= 2:
                    act.wait_ge(done["FH"], n - 1)
                act.wait_ge(*scores.full(step))
                src = scores_ps[scores.buf(step)][:, :, :].rearrange("p c n -> p (c n)")
                nc.scalar.activation(relu[n % 2], src, ACT.Relu).then_inc(scores.read_sem(step), 1)

            def GH(step, b, w):
                n = nth[step] - 1
                if n >= 2:
                    prev = [s for s in schedule if s[0] == "GH"][n - 2]
                    act.wait_ge(*scores.read(prev, 1))
                act.wait_ge(*scores.full(step, 0))
                src = scores_ps[scores.buf(step, 0)][:, :, :].rearrange("p c n -> p (c n)")
                nc.scalar.activation(relu[n % 2], src, ACT.Silu).then_inc(scores.read_sem(step, 0), 1)

            parts = {"XT": XTstep, "KVC": KVC, "KTC": KTC, "KT": KT, "QT": QT, "MTR": MTR, "ST": ST, "OC": OC,
                     "RTE": RTE, "GTE": GTE, "FH": FH, "GH": GH}
            for step in schedule:
                if step[0] in parts:
                    parts[step[0]](step, *step[1:])

        @block.vector
        def _(dve):
            V_ = nc.vector
            chain = [0]

            def link(ins):
                chain[0] += 1
                ins.then_inc(dve_chain, 1)
                dve.wait_ge(dve_chain, chain[0])

            def tt(out, a, c, op):
                return V_.tensor_tensor(out, a, c, op)

            NORMS = {"n0": (X, XN), "n1": (X, XN), "n2": (X, XN), "n4": (X, XN), "n3": (ACC, ACC),
                     "r1": (ACC, XN), "r2": (ACC, ACC)}

            def STAT(step, kind, b):
                src = NORMS[kind][0]
                if kind == "n0":
                    dve.wait_ge(loaded[f"x{b}"], 16)
                if kind == "n4":
                    dve.wait_ge(*after("FIN1", b))
                if kind != "r2":
                    for t in range(T):
                        ins = V_.bn_stats(bn[b][:, t, :], src[b][:, t, :])
                    link(ins)
                for t in range(T):
                    ins = V_.bn_aggr(mv[b][:, t, :], bn[b][:, t, :])
                link(ins)
                mean, v = mv[b][:, :, 0], mv[b][:, :, 1]
                if kind[0] == "n":
                    V_.tensor_scalar(var[b][:, :], v, LN_EPS, None, ALU.add).then_inc(done["NORMSTATS"], 1)
                else:
                    link(tt(var[b][:, :], mean, mean, ALU.mult))
                    V_.scalar_tensor_tensor(out=var[b][:, :], in0=var[b][:, :], scalar=RMS_EPS, in1=v,
                                            op0=ALU.add, op1=ALU.add).then_inc(done["NORMSTATS"], 1)

            def NORM(step, kind, b):
                src, dst = NORMS[kind]
                dve.wait_ge(*after("RSTD", kind, b))
                for t in range(T):
                    if kind[0] == "n":
                        ins = V_.tensor_scalar(dst[b][:, t, :], src[b][:, t, :], mv[b][:, t, 0:1],
                                               rstd[b][:, t:t + 1], ALU.subtract, ALU.mult)
                    elif kind == "r1":
                        ins = V_.scalar_tensor_tensor(out=dst[b][:, t, :], in0=src[b][:, t, :], scalar=rstd[b][:, t:t + 1],
                                                      in1=row["norm1"], op0=ALU.mult, op1=ALU.mult)
                    else:
                        ins = V_.scalar_tensor_tensor(out=dst[b][:, t, :], in0=src[b][:, t, :], scalar=rstd[b][:, t:t + 1],
                                                      in1=row["norm2"], op0=ALU.mult, op1=ALU.mult)
                ins.then_inc(done["NORM"], 1)

            def CKV(step, layer):
                dve.wait_ge(*misc.full(step))
                if layer == 0:
                    dve.wait_ge(loaded["rows"], 16)
                    dve.wait_ge(zeroed, ZERO["Vc"])
                src = small_ps(step)[0:C, :].rearrange("p (b w d) -> p b w d", b=B, w=2)
                bk, bv = row[f"bk{layer}"][0:C, :], row[f"bv{layer}"][0:C, :]
                for b in range(B):
                    v = Vc[layer][b]
                    V_.memset(v[0:C, :, DH:DH + 1], 1.0)
                    tt(v[0:C, :, 0:DH], src[:, b, 1, :].rearrange("p (h d) -> p h d", d=DH),
                       bv.rearrange("p (h d) -> p h d", d=DH), ALU.add)
                    last = tt(kf[0:C, b, :], src[:, b, 0, :], bk, ALU.add)
                    if layer == 1:
                        link(last)
                        pos = oT[1][0:C, b * P:(b + 1) * P].rearrange("p (h d) -> p h d", d=DH)
                        link(V_.tensor_scalar(pos, v[0:C, :, 0:DH], 0.0, None, ALU.max))
                        last = V_.scalar_tensor_tensor(out=v[0:C, :, 0:DH], in0=v[0:C, :, 0:DH], scalar=0.0, in1=pos,
                                                       op0=ALU.min, op1=ALU.add)
                last.then_inc(misc.read_sem(step), 1)

            def split(cat, first, pairs, values, rest, part_of, parts=P):
                def dst(s):
                    return slot(cat, first, pairs, s, parts)
                s0, s1, s2 = (part_of.index(k) for k in range(3))
                link(V_.tensor_copy(dst(s0), flat_heads(values)))
                link(tt(flat_heads(rest), flat_heads(values), dst(s0), ALU.subtract))
                link(V_.tensor_copy(dst(s1), flat_heads(rest)))
                for s, k in enumerate(part_of):
                    if k < 2 and s != (s0, s1)[k]:
                        V_.tensor_copy(dst(s), dst((s0, s1)[k]))
                return tt(dst(s2), flat_heads(rest), dst(s1), ALU.subtract)

            def SPLITC(step, layer):
                dve.wait_ge(*misc.read(("CKV", layer)))
                if layer == 0:
                    for e in range(2):
                        heads = kcat[:, :, :, :].rearrange("p t (a e) c -> p (t a) e c", e=2)
                        V_.memset(heads[:, :, e, MROW + 3 * e:MROW + 3 * e + 3], 1.0)
                flatk = oT[0][0:C, 0:B * P]
                flatr = oT[1][0:C, 0:B * P]
                split(kcat, 2 * layer * HP, B * HP, flatk, flatr, K_PART, C).then_inc(done["SPLITC"], 1)

            def rotate(src, out, tmp):
                sv = src.rearrange("p t (i two) -> p t i two", two=2)
                tv = tmp.rearrange("p (t i two) -> p t i two", t=T, two=2)
                nv = sinf.rearrange("p (t i two) -> p t i two", t=T, two=2)
                tt(out.rearrange("p (t d) -> p t d", t=T), src, cosf.rearrange("p (t d) -> p t d", t=T), ALU.mult)
                tt(tv[:, :, :, 0], sv[:, :, :, 1], nv[:, :, :, 0], ALU.mult)
                return tt(tv[:, :, :, 1], sv[:, :, :, 0], nv[:, :, :, 1], ALU.mult)

            def QP(step, layer, b):
                dve.wait_ge(*misc.full(step))
                src = small_ps(step).rearrange("p (t d) -> p t d", t=T)
                if layer < 2:
                    tt(QF[b].rearrange("p (t d) -> p t d", t=T), src, over_tiles(row[f"bq{layer}"]),
                       ALU.add).then_inc(misc.read_sem(step), 1)
                    dve.wait_ge(*misc.read(step))
                else:
                    rotate(src, QF[b], RS[b]).then_inc(misc.read_sem(step), 1)
                    dve.wait_ge(*misc.read(step))
                    tt(QF[b], QF[b], RS[b], ALU.add).then_inc(done["QP"], 1)
                    dve.wait_ge(done["QP"], b + 1)

            def SPLITQ(step, layer, b):
                if (layer, b) == (2, B - 1):
                    return
                if layer == 0:
                    dve.wait_ge(zeroed, ZERO[f"qcat{b}"])
                split(qcat[b], 0, T * HP, QF[b], RS[b], Q_PART).then_inc(done["SPLITQ"], 1)

            def KV(step, b):
                dve.wait_ge(*scores.full(step))
                if b == 0:
                    dve.wait_ge(zeroed, ZERO["V"])
                src = scores_ps[scores.buf(step)][:, :, :].rearrange("p a (t w d) -> p (a t) w d", t=2, w=2)
                V_.memset(V[b][:, :, :, DH:DH + 1], 1.0)
                V_.tensor_copy(V[b][:, :, :, 0:DH], src[:, :, 1, :].rearrange("p t (h d) -> p t h d", d=DH)
                               ).then_inc(done["KV"], 1)
                rotate(src[:, :, 0, :], KF[b], RS[b]).then_inc(scores.read_sem(step), 1)
                dve.wait_ge(*scores.read(step))
                link(tt(KF[b], KF[b], RS[b], ALU.add))

            def SPLITK(step, b):
                if b:
                    for t in range(T):
                        dve.wait_ge(*scores.full(("KT", 0, t)))
                split(kcat, 0, T * HP, KF[b], RS[b], K_PART).then_inc(done["SPLITK"], 1)

            def KT(step, b, t):
                if t % 2 == 0:
                    return
                dve.wait_ge(*scores.full(step))
                src = scores_ps[scores.buf(step)][:, :, :].bitcast(BF16).rearrange("p a (h c) -> p (a h) c", c=P)
                V_.tensor_copy(kT[b][:, :, t * P:(t + 1) * P], src).then_inc(scores.read_sem(step), 1)

            def QT(step, layer, b, u):
                if u == 0:
                    return
                dve.wait_ge(*scores.full(step))
                src = scores_ps[scores.buf(step)][:, :, :].bitcast(BF16).rearrange("p t (a c) -> p t a c", c=P)
                dst = qT[b][:, :, 2 * u * P:2 * (u + 1) * P].rearrange("p a (t c) -> p t a c", t=2)
                V_.tensor_copy(dst, src).then_inc(scores.read_sem(step), 1)

            def SMAX(step, layer, i, part, u):
                dve.wait_ge(*scores.full(step))
                ps = scores_ps[scores.buf(step)]
                if layer == 2:
                    src, dst = ps[:, :, :], mx[i % 2][:, part, 2 * u:2 * u + 2]
                else:
                    src = ps[:, :, 0:HG * C].rearrange("p t (h c) -> p t h c", c=C)
                    dst = mx[i % 2][:, 2 * u:2 * u + 2, :]
                V_.tensor_reduce(dst, src, AX.X, ALU.max).then_inc(scores.read_sem(step), 1)

            def MCH(step, layer, i):
                k = i % 2
                if layer == 0 and i == 0:
                    dve.wait_ge(zeroed, ZERO["mcat"])
                if layer or i >= 2:
                    old = ("MTR", layer, i - 2) if i >= 2 else ("MTR", layer - 1, NGRP - 2 + i)
                    dve.wait_ge(*misc.full(old))
                for u in range(2):
                    dve.wait_ge(*scores.read(("SMAX", layer, i, NKT[layer] - 1, u)))
                m = mx[k][:, :, :].rearrange("p t (a e) -> p (t a) e", e=2)
                r = mrs[k][:, :, :].rearrange("p t (a e) -> p (t a) e", e=2)
                c = mcat[k][:, :, :, MROW:MROW + 6].rearrange("p t a (e r) -> p (t a) e r", e=2)
                link(V_.tensor_scalar(c[:, :, :, 0], m, -1.0, None, ALU.mult))
                V_.scalar_tensor_tensor(out=r, in0=m, scalar=-1.0, in1=c[:, :, :, 0], op0=ALU.mult, op1=ALU.subtract)
                link(V_.scalar_tensor_tensor(out=c[:, :, :, 1], in0=m, scalar=-1.0, in1=c[:, :, :, 0],
                                             op0=ALU.mult, op1=ALU.subtract))
                tt(c[:, :, :, 2], r, c[:, :, :, 1], ALU.subtract).then_inc(done["MCH"], 1)

            def MTR(step, layer, i):
                if layer == 2:
                    return
                b, g = divmod(i, GR)
                dve.wait_ge(*misc.full(step))
                src = small_ps(step)[MROW:MROW + 6, :].bitcast(BF16).rearrange("p (a n) -> p a n", a=2)
                V_.tensor_copy(qT[b][MROW:MROW + 6, 2 * g:2 * g + 2, :], src).then_inc(misc.read_sem(step), 1)

            def OC(step, layer, i):
                if layer != 1:
                    return
                dve.wait_ge(*after("PV", layer, i, 0))
                V_.transpose(oT[i % 2][:, :].rearrange("p (c r) -> p c r", c=N // VW),
                             out_ps[:, :].rearrange("p (m c) -> p c m", c=N // VW)).then_inc(done["OC"], 1)

            def OTR(step, layer, i):
                b, g = divmod(i, GR)
                if layer == 1:
                    dve.wait_ge(*after("OC", layer, i))
                    src = oT[i % 2][:, :].rearrange("p (c r) -> p c r", c=N // VW)
                    inv = rinv[i % 2][:, :, :].rearrange("p t j -> p (t j)")
                    link(V_.tensor_scalar(inv, src[:, :, DH], TINY, None, ALU.max))
                    link(V_.reciprocal(inv, inv))
                    dst = Z[b][:, g, :].rearrange("p (c d) -> p c d", d=DH)
                    link(tt(dst, src[:, :, 0:DH], inv.unsqueeze(2).broadcast_to([P, N // VW, DH]), ALU.mult))
                    return
                dve.wait_ge(*misc.full(step))
                src = small_ps(step).rearrange("p (t j c) -> p t j c", t=T, j=HG)
                link(V_.reciprocal(rinv[i % 2][:, :, :], src[:, :, :, DH]))
                dst = Z[b][:, :, g * HG * DH:(g + 1) * HG * DH].rearrange("p t (j d) -> p t j d", d=DH)
                tt(dst, src[:, :, :, 0:DH], rinv[i % 2][:, :, :].unsqueeze(3).broadcast_to([P, T, HG, DH]),
                   ALU.mult).then_inc(misc.read_sem(step), 1)

            def OP(step, layer, b):
                dve.wait_ge(*misc.full(step))
                src = small_ps(step).rearrange("p (t d) -> p t d", t=T)
                if layer == 0:
                    tt(X[b][:, :, :], X[b][:, :, :], src, ALU.add).then_inc(misc.read_sem(step), 1)
                    dve.wait_ge(*misc.read(step))
                    link(tt(X[b][:, :, :], X[b][:, :, :], over_tiles(row["bo0"]), ALU.add))
                else:
                    tt(ACC[b][:, :, :], XN[b][:, :, :], src, ALU.add).then_inc(misc.read_sem(step), 1)
                    dve.wait_ge(*misc.read(step))

            def Z1(step, b):
                link(tt(ACC[b][:, :, :], Z[b][:, :, :], XN[b][:, :, :], ALU.add))

            def FIN1(step, b):
                if b:
                    return
                dve.wait_ge(*after("NORM", "n3", b))
                link(tt(ACC[b][:, :, :], ACC[b][:, :, :], over_tiles(row["gamma"]), ALU.mult))
                link(tt(ACC[b][:, :, :], ACC[b][:, :, :], over_tiles(row["beta"]), ALU.add))
                tt(X[b][:, :, :], X[b][:, :, :], ACC[b][:, :, :], ALU.add).then_inc(done["FIN1"], 1)

            def first_max(b, src, oh, top, k):
                eq, best = g2[b], gv[b][:, k, :]
                link(V_.tensor_reduce(top, src, AX.X, ALU.max))
                link(tt(eq[:, :, :], src, top.unsqueeze(2).broadcast_to([P, T, E]), ALU.is_equal))
                link(tt(eq[:, :, :], eq[:, :, :], over_tiles(rev), ALU.mult))
                link(V_.tensor_reduce(best, eq[:, :, :], AX.X, ALU.max))
                link(tt(oh[:, :, :], over_tiles(rev), best.unsqueeze(2).broadcast_to([P, T, E]), ALU.is_equal))

            def per_expert(v):
                return v.unsqueeze(2).broadcast_to([P, T, E])

            def RT(step, b):
                dve.wait_ge(*misc.full(step))
                lg = gl[b][:, :, 0:E]
                V_.tensor_copy(lg, small_ps(step)[:, 0:T * E].rearrange("p (t e) -> p t e", t=T)).then_inc(misc.read_sem(step), 1)
                dve.wait_ge(*misc.read(step))
                first_max(b, lg, oh1[b], gv[b][:, 0, :], 7)
                link(V_.scalar_tensor_tensor(out=g1[b][:, :, :], in0=oh1[b][:, :, :], scalar=-BIG, in1=lg,
                                             op0=ALU.mult, op1=ALU.add))
                first_max(b, g1[b][:, :, :], oh2[b], gv[b][:, 1, :], 6)
                tt(gx[b][:, :, 0], gv[b][:, 1, :], gv[b][:, 0, :], ALU.subtract).then_inc(done["RT"], 1)

            def RTE(step, b):
                dve.wait_ge(*after("RTE", b))
                e2, w1_, w2_ = gex[b][:, :, 0], gv[b][:, 2, :], gv[b][:, 3, :]
                link(V_.tensor_scalar(w2_, e2, 1.0, None, ALU.add))
                link(V_.reciprocal(w1_, w2_))
                link(tt(w2_, e2, w1_, ALU.mult))
                tt(oh1[b][:, :, :], oh1[b][:, :, :], per_expert(w1_), ALU.mult)
                link(tt(oh2[b][:, :, :], oh2[b][:, :, :], per_expert(w2_), ALU.mult))
                link(tt(gw[b][:, :, :], oh1[b][:, :, :], oh2[b][:, :, :], ALU.add))

            def GT(step, b):
                dve.wait_ge(*misc.full(step))
                tt(gl[b][:, :, :], small_ps(step)[:, 0:T * GW].rearrange("p (t e) -> p t e", t=T),
                   over_tiles(row["gates"][:, 0:GW]), ALU.add).then_inc(misc.read_sem(step), 1)
                dve.wait_ge(*misc.read(step))
                lg = gl[b][:, :, 2:GW].rearrange("p t (g e) -> p t g e", g=2)
                gmax, emax = gv[b][:, 0, :], g1[b][:, :, 0:2]
                V_.tensor_reduce(gmax, gl[b][:, :, 0:2], AX.X, ALU.max)
                link(V_.tensor_reduce(emax, lg, AX.X, ALU.max))
                tt(gx[b][:, :, 0:2], gl[b][:, :, 0:2], gmax.unsqueeze(2).broadcast_to([P, T, 2]), ALU.subtract)
                tt(gx[b][:, :, 2:GW].rearrange("p t (g e) -> p t g e", g=2), lg,
                   emax.unsqueeze(3).broadcast_to([P, T, 2, E // 2]), ALU.subtract).then_inc(done["GT"], 1)

            def GTE(step, b):
                dve.wait_ge(*after("GTE", b))
                eg = gex[b][:, :, 0:2]
                sel, ex = g1[b][:, :, 0:2], gex[b][:, :, 2:GW]
                gsum, esum, inv = gv[b][:, 1, :], gv[b][:, 2, :], gv[b][:, 3, :]
                V_.tensor_reduce(gsum, eg, AX.X, ALU.add)
                tt(sel[:, :, 1], eg[:, :, 1], eg[:, :, 0], ALU.is_gt)
                link(tt(sel[:, :, 0], eg[:, :, 0], eg[:, :, 1], ALU.is_ge))
                ex4 = ex.rearrange("p t (g e) -> p t g e", g=2)
                link(tt(ex4, ex4, sel.unsqueeze(3).broadcast_to([P, T, 2, E // 2]), ALU.mult))
                link(V_.tensor_reduce(esum, ex, AX.X, ALU.add))
                link(tt(inv, gsum, esum, ALU.mult))
                link(V_.reciprocal(inv, inv))
                first_max(b, ex, oh1[b], gv[b][:, 4, :], 7)
                link(V_.scalar_tensor_tensor(out=g1[b][:, :, :], in0=oh1[b][:, :, :], scalar=-BIG, in1=ex,
                                             op0=ALU.mult, op1=ALU.add))
                first_max(b, g1[b][:, :, :], oh2[b], gv[b][:, 5, :], 6)
                link(tt(oh1[b][:, :, :], oh1[b][:, :, :], oh2[b][:, :, :], ALU.add))
                link(tt(gw[b][:, :, :], ex, oh1[b][:, :, :], ALU.mult))
                link(tt(gw[b][:, :, :], gw[b][:, :, :], per_expert(inv), ALU.mult))

            def FH(step, b, e):
                n = nth[step] - 1
                dve.wait_ge(*scores.read(step))
                if n >= 2:
                    dve.wait_ge(*probs.full(("FY", (n - 2) // E, (n - 2) % E)))
                src = relu[n % 2]
                tt(h2[n % 2][:, :, :].rearrange("p c n -> p (c n)"), src, src, ALU.mult).then_inc(done["FH"], 1)

            def accumulate(src, w, acc, t):
                return V_.scalar_tensor_tensor(out=acc[:, t, :], in0=src, scalar=w, in1=acc[:, t, :],
                                               op0=ALU.mult, op1=ALU.add)

            def FY(step, b, e):
                dve.wait_ge(*probs.full(step))
                if e:
                    dve.wait_ge(*probs.read(("FY", b, e - 1)))
                ps = probs_ps[probs.buf(step)]
                for t in range(T):
                    last = accumulate(ps[:, t * P:(t + 1) * P], gw[b][:, t, e:e + 1], X[b], t)
                last.then_inc(probs.read_sem(step), 1)
                if e == E - 1:
                    dve.wait_ge(*probs.read(step))

            def GH(step, b, w):
                n = nth[step] - 1
                dve.wait_ge(*scores.read(step, 0))
                dve.wait_ge(*scores.full(step, 1))
                if b:
                    dve.wait_ge(*(scores.full(("RO", 0, 1, 1)) if w else probs.full(("SO", 0))))
                src = scores_ps[scores.buf(step, 1)][:, :, :].rearrange("p c n -> p (c n)")
                tt(gh[w][:, :, :].rearrange("p c n -> p (c n)"), src, relu[n % 2],
                   ALU.mult).then_inc(scores.read_sem(step, 1), 1)

            def SO(step, b):
                dve.wait_ge(*probs.full(step))
                tt(ACC[b][:, :, :], XN[b][:, :, :], probs_ps[probs.buf(step)][:, :].rearrange("p (t d) -> p t d", t=T),
                   ALU.add).then_inc(probs.read_sem(step), 1)
                dve.wait_ge(*probs.read(step))

            def RO(step, b, pr, half):
                dve.wait_ge(*scores.full(step))
                ps = scores_ps[scores.buf(step)]
                for k in range(E // 2):
                    e = E // 2 * half + k
                    for u in range(2):
                        t = 2 * pr + u
                        last = accumulate(ps[:, u, k * P:(k + 1) * P], gw[b][:, t, e:e + 1], ACC[b], t)
                    if k < E // 2 - 1:
                        link(last)
                last.then_inc(scores.read_sem(step), 1)
                dve.wait_ge(*scores.read(step))
                if half == 1:
                    for t in (2 * pr, 2 * pr + 1):
                        last = V_.bn_stats(bn[b][:, t, :], ACC[b][:, t, :])
                    link(last)

            def OUT(step, b):
                dve.wait_ge(*after("NORM", "r2", b))
                tt(ACC[b][:, :, :], ACC[b][:, :, :], X[b][:, :, :], ALU.add).then_inc(done["OUTV"], 1)

            parts = {"STAT": STAT, "NORM": NORM, "CKV": CKV, "SPLITC": SPLITC, "QP": QP, "SPLITQ": SPLITQ, "KV": KV, "SPLITK": SPLITK,
                     "KT": KT, "QT": QT, "SMAX": SMAX, "MCH": MCH, "MTR": MTR, "OC": OC, "OTR": OTR,
                     "OP": OP, "Z1": Z1, "FIN1": FIN1,
                     "RT": RT, "RTE": RTE, "GT": GT, "GTE": GTE, "FH": FH, "FY": FY, "GH": GH, "SO": SO, "RO": RO,
                     "OUT": OUT}
            link(V_.memset(kcat[:, :, :, :].bitcast(mybir.dt.uint32), 0))
            dve.wait_ge(loaded["consts"], 16)
            V_.tensor_copy(identb[:, :], ident).then_inc(consts_cast, 1)
            for step in schedule:
                if step[0] in parts:
                    parts[step[0]](step, *step[1:])


def rope_tables():
    inv = (1.0 / np.float32(10000.0) ** (np.arange(0, DH, 2, dtype=np.float32) / np.float32(DH))).astype(np.float32)
    ang = np.arange(N, dtype=np.float32)[:, None] * inv[None, :]
    cos = np.repeat(np.cos(ang), 2, axis=1)
    sin = np.repeat(np.sin(ang), 2, axis=1) * np.tile(np.array([-1.0, 1.0], np.float32), DH // 2)

    def lay(a):
        a = np.tile(a.astype(np.float32), (1, H)).reshape(T, P, P)
        return a.transpose(1, 0, 2).reshape(P, T * P)
    return lay(cos), lay(sin)


def kernel(**inputs):
    import concourse.bacc as bacc
    from concourse.bass_utils import run_bass_kernel_spmd

    a = {k: np.asarray(v) for k, v in inputs.items()}
    f32 = np.float32

    def chunks(w):
        return w.reshape(2, P, -1).transpose(1, 0, 2)

    x = a["x"].reshape(B, T, P, P).transpose(0, 2, 1, 3)
    wa = np.concatenate([a["L0_xattn_Wq"], a["L0_xattn_Wk"], a["L0_xattn_Wv"], a["L0_xattn_Wo"],
                         a["ctx_1024"].reshape(B * C, P).T], axis=1)
    cos, sin = rope_tables()
    consts = np.concatenate([np.eye(P, dtype=f32), cos, sin,
                             np.tile(np.arange(E, 0, -1, dtype=f32), (P, 1)), np.full((P, T), -0.5, f32)], axis=1)
    rows = np.concatenate([a["L0_xattn_bq"], a["L0_xattn_bk"], a["L0_xattn_bv"], a["L0_xattn_bo"],
                           a["L1_xattn_bq"], a["L1_xattn_bk"], a["L1_xattn_bv"], a["L1_xattn_gamma"],
                           a["L1_xattn_beta"], a["L1_ffn_norm1_w"], a["L1_ffn_norm2_w"],
                           a["L1_ffn_group_bias"], a["L1_ffn_expert_bias"], np.zeros(P - 2 - E, f32)])
    f0 = np.concatenate([a["L0_ffn_router_w"].T, a["L0_ffn_w1"].transpose(1, 0, 2).reshape(P, -1)], axis=1)
    f0y = a["L0_ffn_w2"].reshape(E, 2, P, P).transpose(2, 0, 1, 3).reshape(P, -1)
    dc = a["L1_ffn_Wk_c"].shape[1]
    wkvc = np.concatenate([a["L1_ffn_Wk_c"], a["L1_ffn_Wv_c"], np.zeros((P, P - 2 * dc), f32)], axis=1)
    wk2 = np.concatenate([a["L1_ffn_Wk"], np.zeros((P - dc, P), f32)], axis=0)
    wv2 = np.concatenate([np.zeros((dc, P), f32), a["L1_ffn_Wv"], np.zeros((P - 2 * dc, P), f32)], axis=0)
    wb = np.concatenate([a["L1_xattn_Wq"].T, a["L1_xattn_Wk"].T, a["L1_xattn_Wv"].T,
                         a["L1_ffn_Wq"], wkvc, wk2, wv2, a["L1_ffn_Wo"]], axis=1)
    w2x = a["L1_ffn_W2_experts"].reshape(E, 2, P, P).transpose(2, 1, 0, 3).reshape(P, -1)
    f1 = np.concatenate([a["L1_ffn_W_shared_in"], a["L1_ffn_W1_shared"],
                         chunks(a["L1_ffn_W_shared_out"]).reshape(P, -1), w2x,
                         a["L1_ffn_Wg_gate"], a["L1_ffn_We_gate"]], axis=1)

    nc = bacc.Bacc("TRN2", target_bir_lowering=False, num_devices=1)
    arrays, args = {}, []
    for name, arr in (("x", x), ("wa", wa), ("consts", consts), ("rows", rows), ("f0", f0), ("f0y", f0y),
                      ("wb", wb), ("f1", f1)):
        arr = np.ascontiguousarray(arr)
        arrays[f"in_{name}"] = arr
        args.append(nc.dram_tensor(f"in_{name}", arr.shape, F32, kind="ExternalInput").ap())
    out = nc.dram_tensor("out", (B, P, T, P), F32, kind="ExternalOutput").ap()
    build(nc, *args, out)
    r = run_bass_kernel_spmd(nc, [arrays], core_ids=[0])
    got = np.asarray(r.results[0]["out"])
    return got.transpose(0, 2, 1, 3).reshape(B, N, P)
```

```python
from contextlib import ExitStack

import numpy as np

import concourse.bass as bass
from concourse import mybir

F32 = mybir.dt.float32
BF16 = mybir.dt.bfloat16
ALU = mybir.AluOpType
ACT = mybir.ActivationFunctionType
AX = mybir.AxisListType

P = 128
B = 2
T = 4
N = T * P
H = 16
DH = P // H
C = 77
CP = 80
E = 8
HID = 256
GR = 4
HG = H // GR
HP = H // 2
NGRP = B * GR
VW = 32
LN_EPS, RMS_EPS = 1e-5, 1e-6
BIG = 3.0e38
TINY = 1e-30

SLOTS = 6
Q_PART = (0, 0, 1, 1, 0, 2)
K_PART = (0, 1, 0, 1, 2, 0)
HROWS = SLOTS * DH
MROW = 2 * HROWS

ROWS = ("bq0", "bk0", "bv0", "bo0", "bq1", "bk1", "bv1", "gamma", "beta", "norm1", "norm2", "gates")
NKT = (1, 1, T)
POOL_SPLITS = {(2, 0), (2, 1)}
SCALE = (DH ** -0.5, 1.0, DH ** -0.5)


ORDER = """
    # Layer 0, cross attention: norm, projections and parts, then the head groups.
    STAT n0 0, CKV 0, NORM n0 0, XT n0 0, STAT n0 1, SPLITC 0, NORM n0 1, QP 0 0, SPLITQ 0 0, XT n0 1,
    QP 0 1, KTC 0 0, QT 0 0 0, SPLITQ 0 1, QT 0 0 1, SMAX 0 0 0 0, KTC 0 1, SMAX 0 0 0 1, MCH 0 0,
    SMAX 0 1 0 0, MTR 0 0, SMAX 0 1 0 1, QT 0 1 1,
    ST 0 0 0 0, MCH 0 1, SMAX 0 2 0 0, MTR 0 1, SMAX 0 2 0 1, MCH 0 2, ST 0 0 0 1, SMAX 0 3 0 0,
    ST 0 1 0 0, QT 0 1 0, SMAX 0 3 0 1, ST 0 1 0 1, MCH 0 3, MTR 0 2, OC 0 0, PV 0 0 0,
    ST 0 2 0 0, SMAX 0 4 0 0, SMAX 0 4 0 1, OTR 0 0, ST 0 2 0 1, PV 0 1 0, OC 0 1, OC 0 2, SMAX 0 5 0 0,
    MTR 0 3, PV 0 2 0, MCH 0 4,
    ST 0 3 0 0, SMAX 0 5 0 1, MTR 0 4, SMAX 0 6 0 0, MCH 0 5, ST 0 3 0 1, OTR 0 1, OC 0 3, PV 0 3 0,
    ST 0 4 0 0, OTR 0 3, OTR 0 2, MTR 0 5, XT z0 0, ST 0 4 0 1, SMAX 0 6 0 1, SMAX 0 7 0 0, OP 0 0,
    STAT n1 0, PV 0 4 0, SMAX 0 7 0 1, OC 0 4, MCH 0 6,
    ST 0 5 0 0, MCH 0 7, ST 0 5 0 1, PV 0 5 0, MTR 0 6, NORM n1 0, MTR 0 7, OTR 0 4,
    ST 0 6 0 0, XT n1 0, OC 0 5, ST 0 6 0 1, RT 0, FH 0 0, OTR 0 5,
    ST 0 7 0 0, OC 0 6, PV 0 6 0, ST 0 7 0 1, PV 0 7 0, OTR 0 6, RTE 0, OC 0 7, OTR 0 7, FH 0 1, XT z0 1,
    # Layer 0, experts, beside the last of the attention and the first of the next one.
    FY 0 0, OP 0 1, STAT n1 1, FH 0 2,
    FY 0 1, NORM n1 1, CKV 1, FH 0 3,
    FY 0 2, FH 0 4,
    FY 0 3, XT n1 1, FH 0 5, RT 1,
    FY 0 4, FH 0 6,
    FY 0 5, FH 0 7, SPLITC 1,
    FY 0 6, FH 1 0,
    FY 0 7, STAT n2 0, FH 1 1, RTE 1,
    FY 1 0, FH 1 2, KTC 1 0, NORM n2 0,
    FY 1 1, FH 1 3,
    FY 1 2, XT n2 0, FH 1 4, QP 1 0, SPLITQ 1 0,
    FY 1 3, FH 1 5,
    FY 1 4, QT 1 0 0, FH 1 6,
    FY 1 5, FH 1 7, QT 1 0 1,
    FY 1 6,
    FY 1 7, STAT n2 1, KTC 1 1, SMAX 1 0 0 0, SMAX 1 0 0 1, MCH 1 0, NORM n2 1, SMAX 1 1 0 0, MTR 1 0,
    SMAX 1 1 0 1, XT n2 1, MCH 1 1,
    # Layer 1, cross attention.
    ST 1 0 0 0, QP 1 1, ST 1 0 0 1, SPLITQ 1 1, SMAX 1 2 0 0, SMAX 1 2 0 1, MTR 1 1,
    ST 1 1 0 0, ST 1 1 0 1, QT 1 1 0, PV 1 0 0, MCH 1 2, MTR 1 2, SMAX 1 3 0 0, SMAX 1 3 0 1,
    ST 1 2 0 0, MCH 1 3, QT 1 1 1, OC 1 0, OTR 1 0, ST 1 2 0 1, SMAX 1 4 0 0, SMAX 1 4 0 1, OC 1 1, MTR 1 3,
    PV 1 1 0,
    ST 1 3 0 0, MCH 1 4, ST 1 3 0 1, SMAX 1 5 0 0, OTR 1 1, SMAX 1 5 0 1, MCH 1 5, PV 1 2 0, MTR 1 4, OC 1 2,
    SMAX 1 6 0 0,
    ST 1 4 0 0, SMAX 1 6 0 1, MTR 1 5, PV 1 3 0, OTR 1 2, MCH 1 6, ST 1 4 0 1, SMAX 1 7 0 0, SMAX 1 7 0 1,
    MTR 1 6, OC 1 3,
    ST 1 5 0 0, OTR 1 3, PV 1 4 0, Z1 0, MCH 1 7, STAT n3 0, MTR 1 7, ST 1 5 0 1, NORM n3 0, OC 1 4,
    ST 1 6 0 0, FIN1 0, STAT n4 0, ST 1 6 0 1, OTR 1 4, PV 1 5 0,
    ST 1 7 0 0, NORM n4 0, ST 1 7 0 1, XT n4 0, PV 1 6 0, KVC 0, OC 1 5, OTR 1 5, OC 1 6, OTR 1 6, QP 2 0,
    KV 0, SPLITK 0, PV 1 7 0, SPLITQ 2 0, KT 0 0, OC 1 7, OTR 1 7, Z1 1, KT 0 1, KT 0 2, STAT n3 1, KT 0 3,
    QT 2 0 0, QT 2 0 1, SMAX 2 0 0 0, SMAX 2 0 0 1, SMAX 2 0 1 0, SMAX 2 0 1 1, SMAX 2 0 2 0, SMAX 2 0 2 1,
    SMAX 2 0 3 0, SMAX 2 0 3 1, MCH 2 0, SMAX 2 1 0 0, NORM n3 1, SMAX 2 1 0 1, FIN1 1, MTR 2 0,
    SMAX 2 1 1 0, STAT n4 1,
    # Layer 1, self attention.
    ST 2 0 0 0, SMAX 2 1 1 1, ST 2 0 0 1,
    ST 2 0 1 0, SMAX 2 1 2 0, ST 2 0 1 1, NORM n4 1, PV 2 0 0, SMAX 2 1 2 1, SMAX 2 1 3 0,
    ST 2 0 2 0, XT n4 1, SMAX 2 1 3 1, PV 2 0 1, SMAX 2 2 0 0, ST 2 0 2 1, KVC 1, MCH 2 1, SMAX 2 2 0 1,
    ST 2 0 3 0, MTR 2 1, PV 2 0 2, SMAX 2 2 1 0, SMAX 2 2 1 1, ST 2 0 3 1, OC 2 0, QP 2 1, PV 2 0 3,
    KV 1, OTR 2 0,
    ST 2 1 0 0, ST 2 1 0 1, PV 2 1 0,
    ST 2 1 1 0, SPLITK 1, SMAX 2 2 2 0, ST 2 1 1 1, SMAX 2 2 2 1,
    ST 2 1 2 0, PV 2 1 1, ST 2 1 2 1, SMAX 2 2 3 0,
    ST 2 1 3 0, KT 1 0, SMAX 2 2 3 1, ST 2 1 3 1, MCH 2 2, PV 2 1 2, SMAX 2 3 0 0, MTR 2 2, OC 2 1,
    SMAX 2 3 0 1, PV 2 1 3, KT 1 1,
    ST 2 2 0 0, KT 1 2, ST 2 2 0 1, SMAX 2 3 1 0, SMAX 2 3 1 1, SPLITQ 2 1, KT 1 3,
    ST 2 2 1 0, QT 2 1 0, SMAX 2 3 2 0, PV 2 2 0, ST 2 2 1 1, SMAX 2 3 2 1, QT 2 1 1,
    ST 2 2 2 0, OTR 2 1, SMAX 2 3 3 0, ST 2 2 2 1, SMAX 2 3 3 1, PV 2 2 1,
    ST 2 2 3 0, MCH 2 3, PV 2 2 2, ST 2 2 3 1, MTR 2 3, SMAX 2 4 0 0, SMAX 2 4 0 1,
    ST 2 3 0 0, OC 2 2, SMAX 2 4 1 0, PV 2 2 3, ST 2 3 0 1, SMAX 2 4 1 1, OTR 2 2,
    ST 2 3 1 0, SMAX 2 4 2 0, SMAX 2 4 2 1, ST 2 3 1 1, PV 2 3 0,
    ST 2 3 2 0, SMAX 2 4 3 0, SMAX 2 4 3 1, ST 2 3 2 1, PV 2 3 1,
    ST 2 3 3 0, MCH 2 4, SMAX 2 5 0 0, ST 2 3 3 1, MTR 2 4, SMAX 2 5 0 1, PV 2 3 2,
    ST 2 4 0 0, PV 2 3 3, OC 2 3, ST 2 4 0 1, SMAX 2 5 1 0, SMAX 2 5 1 1,
    ST 2 4 1 0, PV 2 4 0, SMAX 2 5 2 0, ST 2 4 1 1, SMAX 2 5 2 1, OTR 2 3,
    ST 2 4 2 0, SMAX 2 5 3 0, SMAX 2 5 3 1, ST 2 4 2 1, MCH 2 5, PV 2 4 1,
    ST 2 4 3 0, SMAX 2 6 0 0, ST 2 4 3 1, SMAX 2 6 0 1, MTR 2 5, PV 2 4 2, SMAX 2 6 1 0,
    ST 2 5 0 0, SMAX 2 6 1 1, XT z2 0, OC 2 4, PV 2 4 3, SMAX 2 6 2 0, ST 2 5 0 1, SMAX 2 6 2 1, PV 2 5 0,
    ST 2 5 1 0, SMAX 2 6 3 0, SMAX 2 6 3 1, ST 2 5 1 1, OP 2 0,
    ST 2 5 2 0, MCH 2 6, PV 2 5 1, ST 2 5 2 1, STAT r1 0, OTR 2 4,
    ST 2 5 3 0, SMAX 2 7 0 0, MTR 2 6, NORM r1 0, ST 2 5 3 1, PV 2 5 2, SMAX 2 7 0 1,
    ST 2 6 0 0, SMAX 2 7 1 0, XT fl 0, ST 2 6 0 1, SMAX 2 7 1 1, PV 2 5 3, OC 2 5,
    ST 2 6 1 0, SMAX 2 7 2 0, SMAX 2 7 2 1, GT 0, ST 2 6 1 1, PV 2 6 0,
    ST 2 6 2 0, SMAX 2 7 3 0, SMAX 2 7 3 1, MCH 2 7, ST 2 6 2 1, PV 2 6 1,
    ST 2 6 3 0, GH 0 0, ST 2 6 3 1, OC 2 6, PV 2 6 2, PV 2 6 3, MTR 2 7,
    # Layer 1, shared and routed experts.
    SO 0, OTR 2 5,
    ST 2 7 0 0, ST 2 7 0 1, GTE 0,
    ST 2 7 1 0, GH 0 1, ST 2 7 1 1, PV 2 7 0,
    ST 2 7 2 0, ST 2 7 2 1, PV 2 7 1,
    ST 2 7 3 0, PV 2 7 2, ST 2 7 3 1, PV 2 7 3, OTR 2 6, OC 2 7, OTR 2 7, RO 0 0 0, XT z2 1, OP 2 1,
    STAT r1 1, RO 0 0 1, NORM r1 1, RO 0 1 0, RO 0 1 1, STAT r2 0, XT fl 1, GH 1 0, GT 1, NORM r2 0, GH 1 1,
    GTE 1, SO 1, RO 1 0 0, RO 1 0 1, RO 1 1 0, OUT 0, RO 1 1 1, STAT r2 1, NORM r2 1, OUT 1
"""

BORROWING = """
    XT n0 1, OTR 0 1, OTR 0 3, OTR 0 2, XT z0 0, MTR 0 6, OTR 0 4, XT n1 0, OTR 0 6, XT n1 1, XT n2 0,
    QP 1 0, XT n2 1, QP 1 1, MTR 1 4, MTR 1 7, KVC 0, QP 2 0, OTR 2 0, OTR 2 4, OTR 2 6
"""


def steps_of(text):
    rows_ = [line for line in text.splitlines() if not line.strip().startswith("#")]
    entries = [entry.split() for entry in " ".join(rows_).split(",")]
    return [tuple(int(w) if w.isdigit() else w for w in entry) for entry in entries]


BORROW = set(steps_of(BORROWING))


def make_schedule():
    return steps_of(ORDER)


def psum_uses(step):
    kind = step[0]
    if kind == "SMAX":
        return ["scores"]
    if kind == "ST":
        return ["probs"] * (HG // 2)
    if kind in ("QT", "KT", "KTC", "KV", "FH", "RO"):
        return ["scores"]
    if kind == "GH":
        return ["scores"] * 2
    if kind in ("FY", "SO"):
        return ["probs"]
    if kind == "OTR" and step[1] == 1:
        return []
    if kind in ("XT", "QP", "CKV", "OP", "RT", "GT", "KVC", "MTR", "OTR"):
        return ["scores" if step in BORROW else "misc"]
    return []


class Unit:

    def __init__(self, name, buffers, new_sem, schedule):
        self.full_sems = [new_sem(f"{name}{i}_full") for i in range(buffers)]
        self.read_sems = [new_sem(f"{name}{i}_read") for i in range(buffers)]
        self.n = buffers
        self.turn = {}
        for step in schedule:
            for k, unit in enumerate(psum_uses(step)):
                if unit == name:
                    self.turn[step, k] = len(self.turn)

    def buf(self, step, k=0):
        return self.turn[step, k] % self.n

    def reused(self, step, k=0):
        return self.turn[step, k] >= self.n

    def free(self, step, k=0):
        t = self.turn[step, k]
        return self.read_sems[t % self.n], t // self.n

    def full(self, step, k=0):
        t = self.turn[step, k]
        return self.full_sems[t % self.n], t // self.n + 1

    def read(self, step, k=0):
        t = self.turn[step, k]
        return self.read_sems[t % self.n], t // self.n + 1

    def full_sem(self, step, k=0):
        return self.full_sems[self.buf(step, k)]

    def read_sem(self, step, k=0):
        return self.read_sems[self.buf(step, k)]


class Either:

    def __init__(self, misc, scores):
        self.of = lambda step: scores if step in BORROW else misc

    def reused(self, step):
        return self.of(step).reused(step)

    def free(self, step):
        return self.of(step).free(step)

    def full(self, step):
        return self.of(step).full(step)

    def read(self, step):
        return self.of(step).read(step)

    def full_sem(self, step):
        return self.of(step).full_sem(step)

    def read_sem(self, step):
        return self.of(step).read_sem(step)


def build(nc, d_x, d_wa, d_consts, d_rows, d_f0, d_f0y, d_wb, d_f1, d_out):
    schedule = make_schedule()
    ctx = ExitStack()
    with ctx:
        def sb(name, shape, dt=F32):
            return ctx.enter_context(nc.sbuf_tensor(name, shape, dt))

        def psum(name, shape, dt=F32):
            return ctx.enter_context(nc.psum_tensor(name, shape, dt))

        def sem(name):
            return ctx.enter_context(nc.semaphore(name))

        wa = sb("wa", [P, 4 * P + B * C])
        wq0, wkv0, wo0 = wa[:, 0:P], wa[:, P:3 * P], wa[:, 3 * P:4 * P]
        ctxT = wa[:, 4 * P:4 * P + B * C].rearrange("p (b c) -> p b c", b=B)
        consts = sb("consts", [P, P + 2 * T * P + E + T])
        ident = consts[:, 0:P]
        cosf = consts[:, P:P + N]
        sinf = consts[:, P + N:P + 2 * N]
        rev = consts[:, P + 2 * N:P + 2 * N + E]
        minus_half = consts[:, P + 2 * N + E:P + 2 * N + E + T]
        rows = sb("rows", [P, len(ROWS) * P])
        row = {name: rows[:, i * P:(i + 1) * P] for i, name in enumerate(ROWS)}
        f0 = sb("f0", [P, E + E * HID])
        rw = f0[:, 0:E]
        w1 = f0[:, E:E + E * HID].rearrange("p (e c h) -> p e c h", e=E, c=2)
        f0y = sb("f0y", [P, E * 2 * P])
        w2 = f0y[:, :].rearrange("p (e c d) -> p e c d", e=E, c=2)
        wb = sb("wb", [P, 8 * P])
        wq1, wkv1 = wb[:, 0:P], wb[:, P:3 * P]
        wq2, wkvc, wkv2, wo2 = wb[:, 3 * P:4 * P], wb[:, 4 * P:5 * P], wb[:, 5 * P:7 * P], wb[:, 7 * P:8 * P]
        GW = 2 + E
        f1 = sb("f1", [P, 2 * 2 * HID + 2 * P + 2 * E * P + GW])
        win = f1[:, 0:4 * HID].rearrange("p (w m h) -> p w m h", w=2, m=4)
        wso = f1[:, 4 * HID:4 * HID + 2 * P].rearrange("p (c d) -> p c d", c=2)
        w2x = f1[:, 4 * HID + 2 * P:4 * HID + 2 * P + 2 * E * P].rearrange("p (c f n) -> p c f n", c=2, f=2)
        wgate = f1[:, 4 * HID + 2 * P + 2 * E * P:]
        wq = (wq0, wq1, wq2)
        wkvx = (wkv0, wkv1)
        identb = sb("identb", [P, P], BF16)

        def pair(name, shape, dt=F32):
            return [sb(f"{name}{b}", shape, dt) for b in range(B)]

        X = pair("X", [P, T, P])
        XN = pair("XN", [P, T, P])
        XT = pair("XT", [P, N])
        Z = pair("Z", [P, T, P])
        ACC = pair("ACC", [P, T, P])
        QF = [ACC[b][:, :, :].rearrange("p t d -> p (t d)") for b in range(B)]
        KF = [f0[:, E + b * N:E + (b + 1) * N] for b in range(B)]
        RS = [Z[b][:, :, :].rearrange("p t d -> p (t d)") for b in range(B)]
        RSP = [f0[:, E + (B + b) * N:E + (B + b + 1) * N] for b in range(B)]
        qcat = pair("qcat", [P, T, HP, P], BF16)
        qT = pair("qT", [P, HP, N], BF16)
        kcat = sb("kcat", [P, T, H, P], BF16)
        kT = pair("kT", [P, H, N], BF16)
        kTc = [pair(f"kTc{l}", [P, H, CP], BF16) for l in range(2)]
        V = pair("V", [P, T, H, VW])
        Vc = [pair(f"Vc{l}", [P, H, VW]) for l in range(2)]
        mx = [sb(f"mx{i}", [P, T, HG]) for i in range(2)]
        mrs = [sb(f"mrs{i}", [P, T, HG]) for i in range(2)]
        mcat = [sb(f"mcat{i}", [P, T, 2, P // 2], BF16) for i in range(2)]
        pT = [sb(f"pT{i}", [P, HG, N]) for i in range(2)]
        oT = [sb(f"oT{i}", [P, N]) for i in range(2)]
        kf = oT[0][:, 0:B * P].rearrange("p (b d) -> p b d", b=B)
        rinv = [sb(f"rinv{i}", [P, T, HG]) for i in range(GR)]
        kflat = [kT[b][:, :, :].bitcast(F32).rearrange("p h n -> p (h n)") for b in range(B)]
        relu = [kflat[0][:, 2 * N * (2 + i):2 * N * (3 + i)] for i in range(2)]
        h2 = [kflat[0][:, 2 * N * i:2 * N * (i + 1)].rearrange("p (c n) -> p c n", c=2) for i in range(2)]
        gh = h2
        kvc = [kflat[1][:, N * b:N * (b + 1)] for b in range(B)]
        bn = pair("bn", [P, T, 6])
        mv = pair("mv", [P, T, 2])
        var = pair("var", [P, T])
        rstd = pair("rstd", [P, T])
        nmean = pair("nmean", [P, T])
        shift = pair("shift", [P, T])
        gl = pair("gl", [P, T, GW])
        gx = pair("gx", [P, T, GW])
        gex = pair("gex", [P, T, GW])
        g1 = pair("g1", [P, T, E])
        g2 = pair("g2", [P, T, E])
        oh1 = pair("oh1", [P, T, E])
        oh2 = pair("oh2", [P, T, E])
        gv = pair("gv", [P, 8, T])
        gw = pair("gw", [P, T, E])

        scores_ps = [psum(f"scores_ps{i}", [P, 2, 512]) for i in range(2)]
        probs_ps = [psum(f"probs_ps{i}", [P, 512]) for i in range(2)]
        misc_ps = psum("misc_ps", [P, 512])
        out_ps = psum("out_ps", [P, 512])
        scores = Unit("scores", 2, sem, schedule)
        probs = Unit("probs", 2, sem, schedule)
        misc = Either(Unit("misc", 1, sem, schedule), scores)

        def small_ps(step):
            return scores_ps[scores.buf(step)][:, 0, :] if step in BORROW else misc_ps[:, :]

        kinds = {"NORM": "normed", "NORMR": "scaled",
                 "SPLITQ": "query_parts", "SPLITQ_POOL": "pool_query_parts", "SPLITC": "context_parts", "SPLITK": "key_parts",
                 "MCH": "max_parts", "FH": "hidden", "RT": "router_diffs", "RTE": "router_exps",
                 "GT": "gate_diffs", "GTE": "gate_exps", "KV": "values",
                 "FIN1": "cross_attended", "PV": "pv", "NORMSTATS": "stats", "RSTD": "rstds",
                 "OUTV": "out_rows", "GUARD": "guarded", "OC": "out_ps_read", "QP": "rotated_queries"}
        done = {k: sem(f"{n}_done") for k, n in kinds.items()}
        base = {"NORMSTATS": "STAT", "RSTD": "STAT", "OUTV": "OUT"}
        seen, nth = {}, {}
        for step in schedule:
            seen[step[0]] = seen.get(step[0], 0) + 1
            nth[step] = seen[step[0]]

        def after(kind, *args):
            if kind in ("NORM", "NORMR"):
                same = [s for s in schedule if s[0] == "NORM" and (s[1][0] == "n") == (kind == "NORM")]
                return done[kind], same.index(("NORM",) + args) + 1
            if kind == "QROT":
                return done["QP"], [s for s in schedule if s[:2] == ("QP", 2)].index(("QP", 2) + args) + 1
            if kind in ("SPLITQ", "SPLITQ_POOL"):
                same = [s for s in schedule if s[0] == "SPLITQ" and (s[1:] in POOL_SPLITS) == (kind == "SPLITQ_POOL")]
                return done[kind], same.index(("SPLITQ",) + args) + 1
            return done[kind], nth[(base.get(kind, kind),) + args]

        loaded = {n: sem(f"{n}_loaded") for n in ("x0", "x1", "wa", "consts", "rows", "f0", "f0y", "wb", "f1")}
        stored = [sem(f"stored{b}") for b in range(B)]
        zeroed = sem("zeroed")
        shifted = [sem(f"residual{b}_shifted") for b in range(B)]
        consts_cast = sem("consts_cast")
        dve_chain = sem("dve_chain")
        pool_chain = sem("pool_chain")
        ZERO = {"Vc": 1, "qcat0": 2, "mcat": 3, "qcat1": 4, "pT": 5, "V": 6}

        source = {"n0": XN, "n1": XN, "n2": XN, "n4": XN, "fl": XN, "z0": Z, "z2": Z}

        NORMS = {"n0": (X, XN), "n1": (X, XN), "n2": (X, XN), "n4": (X, XN), "n3": (ACC, ACC),
                 "r1": (ACC, XN), "r2": (ACC, ACC)}

        def slot(cat, first, pairs, s, parts=P):
            wide = 2 * P if cat is kcat else P
            step = P + HROWS if cat is kcat else HROWS
            size = int(np.prod(cat.shape[1:]))
            return bass.AP(cat, first * wide + DH * s, [[size, parts], [wide, pairs], [step, 2], [1, DH]])

        def flat_heads(t):
            return t.rearrange("p (n e d) -> p n e d", e=2, d=DH)

        def over_tiles(r):
            return r.unsqueeze(1).broadcast_to([P, T, r.shape[1]])

        block = ctx.enter_context(nc.Block())

        @block.sync
        def _(sp):
            sp.dma_start(X[0][:, :, :], d_x[0]).then_inc(loaded["x0"], 16)
            sp.dma_start(wa[:, :], d_wa).then_inc(loaded["wa"], 16)
            sp.dma_start(X[1][:, :, :], d_x[1]).then_inc(loaded["x1"], 16)
            sp.dma_start(f0[:, :], d_f0).then_inc(loaded["f0"], 16)
            sp.dma_start(f0y[:, :], d_f0y).then_inc(loaded["f0y"], 16)
            sp.dma_start(wb[:, :], d_wb).then_inc(loaded["wb"], 16)
            sp.dma_start(f1[:, :], d_f1).then_inc(loaded["f1"], 16)
            for b in range(B):
                sp.wait_ge(*after("OUTV", b))
                sp.dma_start(d_out[b], ACC[b][:, :, :]).then_inc(stored[b], 16)
            for b in range(B):
                sp.wait_ge(stored[b], 16)

        @block.gpsimd
        def _(pool):
            U32 = mybir.dt.uint32
            for l in range(2):
                for b in range(B):
                    last = pool.memset(Vc[l][b][:, :, :], 0.0)
            last.then_inc(zeroed, 1)
            pool.memset(qcat[0][:, :, :, :].bitcast(U32), 0).then_inc(zeroed, 1)
            pool.wait_ge(loaded["consts"], 16)

            def background(n):
                if n == 0:
                    pool.memset(mcat[0][:, :, :, :].bitcast(U32), 0)
                    pool.memset(mcat[1][:, :, :, :].bitcast(U32), 0).then_inc(zeroed, 1)
                elif n == 1:
                    pool.memset(pT[0][:, :, :], 0.0)
                    pool.memset(qcat[1][:, :, :, :].bitcast(U32), 0).then_inc(zeroed, 1)
                    pool.memset(pT[1][:, :, :], 0.0).then_inc(zeroed, 1)
                    pool.memset(V[0][:, :, :, :], 0.0)
                    pool.memset(V[1][:, :, :, :], 0.0).then_inc(zeroed, 1)

            def STAT(step, kind, b):
                pool.wait_ge(*after("NORMSTATS", kind, b))
                power = tt(rstd[b][:, :], var[b][:, :], minus_half, ALU.pow)
                if kind[0] == "n":
                    link(power)
                    power = tt(shift[b][:, :], nmean[b][:, :], rstd[b][:, :], ALU.mult)
                power.then_inc(done["RSTD"], 1)

            chain = [0]

            def link(ins):
                chain[0] += 1
                ins.then_inc(pool_chain, 1)
                pool.wait_ge(pool_chain, chain[0])

            def tt(out, a, c, op):
                return pool.tensor_tensor(out, a, c, op)

            def FIN1(step, b):
                if b == 0:
                    return
                pool.wait_ge(*after("NORM", "n3", b))
                link(tt(ACC[b][:, :, :], ACC[b][:, :, :], over_tiles(row["gamma"]), ALU.mult))
                tt(X[b][:, :, :], X[b][:, :, :], ACC[b][:, :, :], ALU.add).then_inc(done["FIN1"], 1)

            def NORM(step, kind, b):
                if kind not in ("n0", "n2"):
                    return
                if step == ("NORM", "n0", 0):
                    pool.wait_ge(loaded["rows"], 16)
                pool.wait_ge(*after("NORM", kind, b))
                tt(X[b][:, :, :], X[b][:, :, :], over_tiles(row["bo0" if kind == "n0" else "beta"]),
                   ALU.add).then_inc(shifted[b], 1)

            def ST(step, layer, i, kt, half):
                if layer != 1:
                    return
                n = (nth[step] - 1) // 2
                pool.wait_ge(*probs.read(step, 0))
                pool.wait_ge(*probs.read(step, 1))
                heads = pT[n % 2][0:C, 2 * half:2 * half + 2, :]
                pool.tensor_scalar(heads, heads, 0.0, None, ALU.max).then_inc(done["GUARD"], 1)

            def SPLITQ(step, layer, b):
                if (layer, b) not in POOL_SPLITS:
                    return
                if layer == 2:
                    pool.wait_ge(*after("QROT", b))
                else:
                    pool.wait_ge(*misc.read(("QP", layer, b)))
                def dst(s):
                    return slot(qcat[b], 0, T * HP, s)
                def copy(out, src):
                    return pool.tensor_scalar(out, src, 1.0, None, ALU.mult)
                values, rest = flat_heads(QF[b]), flat_heads(RSP[b] if layer == 2 else RS[b])
                s0, s1, s2 = (Q_PART.index(k) for k in range(3))
                link(copy(dst(s0), values))
                link(tt(rest, values, dst(s0), ALU.subtract))
                link(copy(dst(s1), rest))
                for s, k in enumerate(Q_PART):
                    if k < 2 and s != (s0, s1)[k]:
                        copy(dst(s), dst((s0, s1)[k]))
                tt(dst(s2), rest, dst(s1), ALU.subtract).then_inc(done["SPLITQ_POOL"], 1)

            parts = {"STAT": STAT, "NORM": NORM, "FIN1": FIN1, "ST": ST, "SPLITQ": SPLITQ}
            stats = 0
            for step in schedule:
                if step[0] in parts:
                    parts[step[0]](step, *step[1:])
                if step[0] == "STAT":
                    background(stats)
                    stats += 1

        @block.tensor
        def _(pe):
            def mm(out, lhsT, rhs, start=True, stop=True):
                return nc.tensor.matmul(out, lhsT, rhs, start=start, stop=stop)

            def wait_free(unit, step):
                if unit.reused(step):
                    pe.wait_ge(*unit.free(step))

            def XTstep(step, kind, b):
                if kind[0] == "z":
                    heads = [s for s in schedule if s[0] == "OTR" and s[1] == int(kind[1]) and s[2] // GR == b]
                    pe.wait_ge(*misc.read(heads[-1]))
                else:
                    pe.wait_ge(*(after("NORMR", "r1", b) if kind == "fl" else after("NORM", kind, b)))
                wait_free(misc, step)
                for t in range(T):
                    last = nc.tensor.transpose(small_ps(step)[:, t * P:(t + 1) * P], source[kind][b][:, t, :], ident)
                last.then_inc(misc.full_sem(step), 1)

            def project(step, b, w, width, xt_step):
                pe.wait_ge(*misc.read(xt_step))
                wait_free(misc, step)
                for t in range(T):
                    last = mm(small_ps(step)[:, t * width:(t + 1) * width], XT[b][:, t * P:(t + 1) * P], w)
                last.then_inc(misc.full_sem(step), 1)

            def QP(step, layer, b):
                if layer:
                    pe.wait_ge(loaded["wb"], 16)
                else:
                    pe.wait_ge(loaded["wa"], 16)
                project(step, b, wq[layer], P, ("XT", ("n0", "n2", "n4")[layer], b))

            def OP(step, layer, b):
                project(step, b, wo0 if layer == 0 else wo2, P, ("XT", "z0" if layer == 0 else "z2", b))

            def RT(step, b):
                if b == 0:
                    pe.wait_ge(loaded["f0"], 16)
                project(step, b, rw, E, ("XT", "n1", b))

            def GT(step, b):
                if b == 0:
                    pe.wait_ge(loaded["f1"], 16)
                project(step, b, wgate, GW, ("XT", "fl", b))

            def CKV(step, layer):
                pe.wait_ge(loaded["wb" if layer else "wa"], 16)
                wait_free(misc, step)
                for b in range(B):
                    last = mm(small_ps(step)[0:C, b * 2 * P:(b + 1) * 2 * P], ctxT[:, b, :], wkvx[layer])
                last.then_inc(misc.full_sem(step), 1)

            def KVC(step, b):
                pe.wait_ge(*misc.read(("XT", "n4", b)))
                wait_free(misc, step)
                mm(small_ps(step), wkvc, XT[b][:, :]).then_inc(misc.full_sem(step), 1)

            def KV(step, b):
                pe.wait_ge(*misc.read(("KVC", b)))
                wait_free(scores, step)
                ps = scores_ps[scores.buf(step)]
                for t in range(T):
                    last = mm(ps[:, t // 2, (t % 2) * 256:(t % 2) * 256 + 256], kvc[b][:, t * P:(t + 1) * P], wkv2)
                last.then_inc(scores.full_sem(step), 1)

            def KTC(step, layer, b):
                pe.wait_ge(*after("SPLITC", layer))
                wait_free(scores, step)
                ps = scores_ps[scores.buf(step)][:, :, :].bitcast(BF16)
                for h in range(H):
                    o = (h % 8) * CP
                    last = nc.tensor.transpose(ps[:, h // 8, o:o + C], kcat[0:C, 2 * layer + b, h, :], identb[0:C, 0:C])
                last.then_inc(scores.full_sem(step), 1)

            def KT(step, b, t):
                pe.wait_ge(*after("SPLITK", b))
                wait_free(scores, step)
                ps = scores_ps[scores.buf(step)][:, :, :].bitcast(BF16)
                for h in range(H):
                    o = (h % 8) * P
                    last = nc.tensor.transpose(ps[:, h // 8, o:o + P], kcat[:, t, h, :], identb[:, :])
                last.then_inc(scores.full_sem(step), 1)

            def QT(step, layer, b, u):
                pe.wait_ge(*after("SPLITQ_POOL" if (layer, b) in POOL_SPLITS else "SPLITQ", layer, b))
                wait_free(scores, step)
                ps = scores_ps[scores.buf(step)][:, :, :].bitcast(BF16)
                for t in range(2):
                    for p in range(HP):
                        last = nc.tensor.transpose(ps[:, t, p * P:(p + 1) * P], qcat[b][:, 2 * u + t, p, :], identb[:, :])
                last.then_inc(scores.full_sem(step), 1)

            def SMAX(step, layer, i, part, u):
                b, g = divmod(i, GR)
                if i % GR == 0 and part == 0 and u == 0:
                    for k in range(2):
                        pe.wait_ge(*scores.read(("QT", layer, b, k)))
                    for k in range(T if layer == 2 else 1):
                        pe.wait_ge(*scores.read(("KT", b, k) if layer == 2 else ("KTC", layer, b)))
                wait_free(scores, step)
                ps = scores_ps[scores.buf(step)]
                for k in range(2):
                    if layer == 2:
                        pr = 2 * g + u
                        last = mm(ps[:, k, :], qT[b][:, pr, part * P:(part + 1) * P], kT[b][:, 2 * pr + k, :])
                    else:
                        t = 2 * u + k
                        for pr in range(2):
                            a = 2 * g + pr
                            last = mm(ps[:, k, pr * 2 * C:(pr + 1) * 2 * C], qT[b][:, a, t * P:(t + 1) * P],
                                      kTc[layer][b][:, 2 * a:2 * a + 2, 0:C])
                last.then_inc(scores.full_sem(step), 1)

            def MTR(step, layer, i):
                pe.wait_ge(*after("MCH", layer, i))
                wait_free(misc, step)
                ps = small_ps(step).bitcast(BF16)
                for t in range(T):
                    last = nc.tensor.transpose(ps[:, t * P:(t + 1) * P],
                                               mcat[i % 2][:, t, :, :].rearrange("p a c -> p (a c)"), identb[:, :])
                last.then_inc(misc.full_sem(step), 1)

            def ST(step, layer, i, kt, half):
                b, g = divmod(i, GR)
                if kt == 0 and half == 0:
                    pe.wait_ge(*misc.read(("MTR", layer, i)))
                for k in range(2):
                    h = HG * g + 2 * half + k
                    if probs.reused(step, k):
                        pe.wait_ge(*probs.free(step, k))
                    ps = probs_ps[probs.buf(step, k)]
                    if layer == 2:
                        out, keys = ps[:, :], kT[b][:, h, kt * P:(kt + 1) * P]
                    else:
                        out, keys = ps[0:C, :], kTc[layer][b][:, h, 0:C]
                    mm(out, keys, qT[b][:, h // 2, :]).then_inc(probs.full_sem(step, k), 1)

            def PV(step, layer, i, kt):
                b, g = divmod(i, GR)
                if layer == 2 and i % GR == 0 and kt == 0:
                    pe.wait_ge(*after("KV", b))
                    pe.wait_ge(*scores.read(("KV", b)))
                if kt == 0 and (layer or i):
                    pe.wait_ge(done["OC"], layer * NGRP + i)
                for j in range(HG):
                    if layer == 1:
                        pe.wait_ge(done["GUARD"], 2 * i + j // 2 + 1)
                    else:
                        pe.wait_ge(*probs.read(("ST", layer, i, kt, j // 2), j % 2))
                    h = HG * g + j
                    vals = V[b][:, kt, h, :] if layer == 2 else Vc[layer][b][:, h, :]
                    last = mm(out_ps[j * VW:(j + 1) * VW, :], vals, pT[(nth[step] - 1) % 2][:, j, :],
                              start=(kt == 0), stop=(kt == NKT[layer] - 1))
                last.then_inc(done["PV"], 1)

            def OTR(step, layer, i):
                if layer == 1:
                    return
                pe.wait_ge(*after("OC", layer, i))
                wait_free(misc, step)
                for t in range(T):
                    last = nc.tensor.transpose(small_ps(step)[:, t * P:(t + 1) * P], oT[i % 2][:, t * P:(t + 1) * P], ident)
                last.then_inc(misc.full_sem(step), 1)

            def FH(step, b, e):
                if e == 0:
                    pe.wait_ge(*misc.read(("XT", "n1", b)))
                wait_free(scores, step)
                ps = scores_ps[scores.buf(step)]
                for c in range(2):
                    last = mm(ps[:, c, :], w1[:, e, c, :], XT[b][:, :])
                last.then_inc(scores.full_sem(step), 1)

            def FY(step, b, e):
                if b == 0 and e == 0:
                    pe.wait_ge(loaded["f0y"], 16)
                pe.wait_ge(*after("FH", b, e))
                pe.wait_ge(*probs.free(step))
                ps = probs_ps[probs.buf(step)]
                for t in range(T):
                    for c in range(2):
                        last = mm(ps[:, t * P:(t + 1) * P], h2[e % 2][:, c, t * P:(t + 1) * P], w2[:, e, c, :],
                                  start=(c == 0), stop=(c == 1))
                last.then_inc(probs.full_sem(step), 1)

            def GH(step, b, w):
                if w == 0:
                    pe.wait_ge(*misc.read(("XT", "fl", b)))
                for half in range(2):
                    pe.wait_ge(*scores.free(step, half))
                    ps = scores_ps[scores.buf(step, half)]
                    for c in range(2):
                        last = mm(ps[:, c, :], win[:, w, 2 * half + c, :], XT[b][:, :])
                    last.then_inc(scores.full_sem(step, half), 1)

            def SO(step, b):
                pe.wait_ge(*scores.read(("GH", b, 0), 1))
                pe.wait_ge(*probs.free(step))
                ps = probs_ps[probs.buf(step)]
                for t in range(T):
                    for c in range(2):
                        last = mm(ps[:, t * P:(t + 1) * P], gh[0][:, c, t * P:(t + 1) * P], wso[:, c, :],
                                  start=(c == 0), stop=(c == 1))
                last.then_inc(probs.full_sem(step), 1)

            def RO(step, b, pr, half):
                if pr == 0 and half == 0:
                    pe.wait_ge(*scores.read(("GH", b, 1), 1))
                wait_free(scores, step)
                ps = scores_ps[scores.buf(step)]
                for u in range(2):
                    t = 2 * pr + u
                    for c in range(2):
                        last = mm(ps[:, u, :], gh[1][:, c, t * P:(t + 1) * P], w2x[:, c, half, :],
                                  start=(c == 0), stop=(c == 1))
                last.then_inc(scores.full_sem(step), 1)

            parts = {"XT": XTstep, "QP": QP, "OP": OP, "RT": RT, "GT": GT, "CKV": CKV, "KVC": KVC, "KV": KV,
                     "KTC": KTC, "KT": KT, "QT": QT, "SMAX": SMAX, "MTR": MTR, "ST": ST, "PV": PV, "OTR": OTR,
                     "FH": FH, "FY": FY, "GH": GH, "SO": SO, "RO": RO}
            pe.wait_ge(loaded["consts"], 16)
            pe.wait_ge(consts_cast, 1)
            for step in schedule:
                if step[0] in parts:
                    parts[step[0]](step, *step[1:])

        @block.scalar
        def _(act):
            act.dma_start(consts[:, :], d_consts).then_inc(loaded["consts"], 16)
            act.dma_start(rows[:, :], d_rows.partition_broadcast(P)).then_inc(loaded["rows"], 16)

            def XTstep(step, kind, b):
                act.wait_ge(*misc.full(step))
                nc.scalar.copy(XT[b][:, :], small_ps(step)).then_inc(misc.read_sem(step), 1)

            def NORM(step, kind, b):
                if kind[0] != "n":
                    return
                src, dst = NORMS[kind]
                act.wait_ge(*after("RSTD", kind, b))
                for t in range(T):
                    ins = nc.scalar.activation(dst[b][:, t, :], src[b][:, t, :], ACT.Identity,
                                               bias=shift[b][:, t:t + 1], scale=rstd[b][:, t:t + 1])
                ins.then_inc(done["NORM"], 1)

            def KV(step, b):
                act.wait_ge(*scores.full(step))
                if b == 0:
                    act.wait_ge(zeroed, ZERO["V"])
                src = scores_ps[scores.buf(step)][:, :, :].rearrange("p a (t w d) -> p (a t) w d", t=2, w=2)
                nc.scalar.copy(V[b][:, :, :, 0:DH], src[:, :, 1, :].rearrange("p t (h d) -> p t h d", d=DH)
                               ).then_inc(done["KV"], 1)

            def KVC(step, b):
                act.wait_ge(*misc.full(step))
                nc.scalar.copy(kvc[b], small_ps(step)).then_inc(misc.read_sem(step), 1)

            def KTC(step, layer, b):
                act.wait_ge(*scores.full(step))
                src = scores_ps[scores.buf(step)][:, :, :].bitcast(BF16)[:, :, 0:8 * CP]
                src = src.rearrange("p a (h c) -> p a h c", c=CP)[:, :, :, 0:C]
                dst = kTc[layer][b][:, :, :].rearrange("p (a h) c -> p a h c", a=2)[:, :, :, 0:C]
                nc.scalar.copy(dst, src).then_inc(scores.read_sem(step), 1)

            def KT(step, b, t):
                if t % 2:
                    return
                act.wait_ge(*scores.full(step))
                src = scores_ps[scores.buf(step)][:, :, :].bitcast(BF16)
                src = src.rearrange("p a (h c) -> p (a h) c", c=P)
                nc.scalar.copy(kT[b][:, :, t * P:(t + 1) * P], src).then_inc(scores.read_sem(step), 1)

            def QT(step, layer, b, u):
                if u:
                    return
                act.wait_ge(*scores.full(step))
                src = scores_ps[scores.buf(step)][:, :, :].bitcast(BF16).rearrange("p t (a c) -> p t a c", c=P)
                dst = qT[b][:, :, 2 * u * P:2 * (u + 1) * P].rearrange("p a (t c) -> p t a c", t=2)
                nc.scalar.copy(dst, src).then_inc(scores.read_sem(step), 1)

            def MTR(step, layer, i):
                if layer == 0:
                    return
                b, g = divmod(i, GR)
                act.wait_ge(*misc.full(step))
                for a in range(2):
                    src = small_ps(step)[64 * a + 32:64 * a + 38, 0:N // 2].bitcast(BF16)
                    last = nc.scalar.copy(qT[b][MROW:MROW + 6, 2 * g + a, :], src)
                last.then_inc(misc.read_sem(step), 1)

            def ST(step, layer, i, kt, half):
                parts_ = P if layer == 2 else C
                n = (nth[step] - 1) // 2
                if n == 0 and half == 0:
                    act.wait_ge(zeroed, ZERO["pT"])
                if n >= 2 and half == 0:
                    act.wait_ge(done["PV"], n - 1)
                for k in range(2):
                    act.wait_ge(*probs.full(step, k))
                    nc.scalar.activation(pT[n % 2][0:parts_, 2 * half + k, :], probs_ps[probs.buf(step, k)][0:parts_, :],
                                         ACT.Exp, scale=SCALE[layer]).then_inc(probs.read_sem(step, k), 1)

            def OC(step, layer, i):
                if layer == 1:
                    return
                act.wait_ge(*after("PV", layer, i, NKT[layer] - 1))
                if i >= 2:
                    act.wait_ge(*misc.full(("OTR", layer, i - 2)))
                nc.scalar.copy(oT[i % 2][:, :], out_ps[:, :]).then_inc(done["OC"], 1)

            def RTE(step, b):
                act.wait_ge(*after("RT", b))
                nc.scalar.activation(gex[b][:, :, 0:1], gx[b][:, :, 0:1], ACT.Exp).then_inc(done["RTE"], 1)

            def GTE(step, b):
                act.wait_ge(*after("GT", b))
                nc.scalar.activation(gex[b][:, :, :], gx[b][:, :, :], ACT.Exp).then_inc(done["GTE"], 1)

            def FH(step, b, e):
                n = nth[step] - 1
                if n >= 2:
                    act.wait_ge(done["FH"], n - 1)
                act.wait_ge(*scores.full(step))
                src = scores_ps[scores.buf(step)][:, :, :].rearrange("p c n -> p (c n)")
                nc.scalar.activation(relu[n % 2], src, ACT.Relu).then_inc(scores.read_sem(step), 1)

            def GH(step, b, w):
                n = nth[step] - 1
                if n >= 2:
                    prev = [s for s in schedule if s[0] == "GH"][n - 2]
                    act.wait_ge(*scores.read(prev, 1))
                act.wait_ge(*scores.full(step, 0))
                src = scores_ps[scores.buf(step, 0)][:, :, :].rearrange("p c n -> p (c n)")
                nc.scalar.activation(relu[n % 2], src, ACT.Silu).then_inc(scores.read_sem(step, 0), 1)

            parts = {"XT": XTstep, "NORM": NORM, "KVC": KVC, "KV": KV, "KTC": KTC, "KT": KT, "QT": QT, "MTR": MTR, "ST": ST, "OC": OC,
                     "RTE": RTE, "GTE": GTE, "FH": FH, "GH": GH}
            for step in schedule:
                if step[0] in parts:
                    parts[step[0]](step, *step[1:])

        @block.vector
        def _(dve):
            V_ = nc.vector
            chain = [0]

            def link(ins):
                chain[0] += 1
                ins.then_inc(dve_chain, 1)
                dve.wait_ge(dve_chain, chain[0])

            def tt(out, a, c, op):
                return V_.tensor_tensor(out, a, c, op)

            def STAT(step, kind, b):
                src = NORMS[kind][0]
                if kind == "n0":
                    dve.wait_ge(loaded[f"x{b}"], 16)
                if kind == "n4":
                    dve.wait_ge(*after("FIN1", b))
                if kind != "r2":
                    for t in range(T):
                        ins = V_.bn_stats(bn[b][:, t, :], src[b][:, t, :])
                    link(ins)
                for t in range(T):
                    ins = V_.bn_aggr(mv[b][:, t, :], bn[b][:, t, :])
                link(ins)
                mean, v = mv[b][:, :, 0], mv[b][:, :, 1]
                if kind[0] == "n":
                    V_.tensor_scalar(nmean[b][:, :], mean, -1.0, None, ALU.mult)
                    V_.tensor_scalar(var[b][:, :], v, LN_EPS, None, ALU.add).then_inc(done["NORMSTATS"], 1)
                else:
                    link(tt(var[b][:, :], mean, mean, ALU.mult))
                    V_.scalar_tensor_tensor(out=var[b][:, :], in0=var[b][:, :], scalar=RMS_EPS, in1=v,
                                            op0=ALU.add, op1=ALU.add).then_inc(done["NORMSTATS"], 1)

            def NORM(step, kind, b):
                if kind[0] == "n":
                    return
                src, dst = NORMS[kind]
                dve.wait_ge(*after("RSTD", kind, b))
                for t in range(T):
                    ins = V_.scalar_tensor_tensor(out=dst[b][:, t, :], in0=src[b][:, t, :], scalar=rstd[b][:, t:t + 1],
                                                  in1=row["norm1" if kind == "r1" else "norm2"], op0=ALU.mult, op1=ALU.mult)
                ins.then_inc(done["NORMR"], 1)

            def CKV(step, layer):
                dve.wait_ge(*misc.full(step))
                if layer == 0:
                    dve.wait_ge(loaded["rows"], 16)
                    dve.wait_ge(zeroed, ZERO["Vc"])
                src = small_ps(step)[0:C, :].rearrange("p (b w d) -> p b w d", b=B, w=2)
                bk, bv = row[f"bk{layer}"][0:C, :], row[f"bv{layer}"][0:C, :]
                for b in range(B):
                    v = Vc[layer][b]
                    V_.memset(v[0:C, :, DH:DH + 1], 1.0)
                    tt(v[0:C, :, 0:DH], src[:, b, 1, :].rearrange("p (h d) -> p h d", d=DH),
                       bv.rearrange("p (h d) -> p h d", d=DH), ALU.add)
                    last = tt(kf[0:C, b, :], src[:, b, 0, :], bk, ALU.add)
                    if layer == 1:
                        link(last)
                        pos = oT[1][0:C, b * P:(b + 1) * P].rearrange("p (h d) -> p h d", d=DH)
                        link(V_.tensor_scalar(pos, v[0:C, :, 0:DH], 0.0, None, ALU.max))
                        last = V_.scalar_tensor_tensor(out=v[0:C, :, 0:DH], in0=v[0:C, :, 0:DH], scalar=0.0, in1=pos,
                                                       op0=ALU.min, op1=ALU.add)
                last.then_inc(misc.read_sem(step), 1)

            def split(cat, first, pairs, values, rest, part_of, parts=P):
                def dst(s):
                    return slot(cat, first, pairs, s, parts)
                s0, s1, s2 = (part_of.index(k) for k in range(3))
                link(V_.tensor_copy(dst(s0), flat_heads(values)))
                link(tt(flat_heads(rest), flat_heads(values), dst(s0), ALU.subtract))
                link(V_.tensor_copy(dst(s1), flat_heads(rest)))
                for s, k in enumerate(part_of):
                    if k < 2 and s != (s0, s1)[k]:
                        V_.tensor_copy(dst(s), dst((s0, s1)[k]))
                return tt(dst(s2), flat_heads(rest), dst(s1), ALU.subtract)

            def SPLITC(step, layer):
                dve.wait_ge(*misc.read(("CKV", layer)))
                if layer == 0:
                    for e in range(2):
                        heads = kcat[:, :, :, :].rearrange("p t (a e) c -> p (t a) e c", e=2)
                        V_.memset(heads[:, :, e, MROW + 3 * e:MROW + 3 * e + 3], 1.0)
                flatk = oT[0][0:C, 0:B * P]
                flatr = oT[1][0:C, 0:B * P]
                split(kcat, 2 * layer * HP, B * HP, flatk, flatr, K_PART, C).then_inc(done["SPLITC"], 1)

            def rotate(src, out, tmp):
                sv = src.rearrange("p t (i two) -> p t i two", two=2)
                tv = tmp.rearrange("p (t i two) -> p t i two", t=T, two=2)
                nv = sinf.rearrange("p (t i two) -> p t i two", t=T, two=2)
                tt(out.rearrange("p (t d) -> p t d", t=T), src, cosf.rearrange("p (t d) -> p t d", t=T), ALU.mult)
                tt(tv[:, :, :, 0], sv[:, :, :, 1], nv[:, :, :, 0], ALU.mult)
                return tt(tv[:, :, :, 1], sv[:, :, :, 0], nv[:, :, :, 1], ALU.mult)

            def QP(step, layer, b):
                dve.wait_ge(*misc.full(step))
                src = small_ps(step).rearrange("p (t d) -> p t d", t=T)
                if layer < 2:
                    tt(QF[b].rearrange("p (t d) -> p t d", t=T), src, over_tiles(row[f"bq{layer}"]),
                       ALU.add).then_inc(misc.read_sem(step), 1)
                    dve.wait_ge(*misc.read(step))
                else:
                    rotate(src, QF[b], RS[b]).then_inc(misc.read_sem(step), 1)
                    dve.wait_ge(*misc.read(step))
                    tt(QF[b], QF[b], RS[b], ALU.add).then_inc(done["QP"], 1)

            def SPLITQ(step, layer, b):
                if (layer, b) in POOL_SPLITS:
                    return
                if layer == 0:
                    dve.wait_ge(zeroed, ZERO[f"qcat{b}"])
                if layer == 2:
                    dve.wait_ge(*after("QROT", b))
                split(qcat[b], 0, T * HP, QF[b], RS[b], Q_PART).then_inc(done["SPLITQ"], 1)

            def KV(step, b):
                dve.wait_ge(*scores.full(step))
                if b == 0:
                    dve.wait_ge(zeroed, ZERO["V"])
                src = scores_ps[scores.buf(step)][:, :, :].rearrange("p a (t w d) -> p (a t) w d", t=2, w=2)
                V_.memset(V[b][:, :, :, DH:DH + 1], 1.0)
                dve.wait_ge(*after("KV", b))
                dve.wait_ge(*after("QROT", b))
                rotate(src[:, :, 0, :], KF[b], RS[b]).then_inc(scores.read_sem(step), 1)
                dve.wait_ge(*scores.read(step))
                link(tt(KF[b], KF[b], RS[b], ALU.add))

            def SPLITK(step, b):
                if b:
                    for t in range(T):
                        dve.wait_ge(*scores.full(("KT", 0, t)))
                split(kcat, 0, T * HP, KF[b], RS[b], K_PART).then_inc(done["SPLITK"], 1)

            def KT(step, b, t):
                if t % 2 == 0:
                    return
                dve.wait_ge(*scores.full(step))
                src = scores_ps[scores.buf(step)][:, :, :].bitcast(BF16).rearrange("p a (h c) -> p (a h) c", c=P)
                V_.tensor_copy(kT[b][:, :, t * P:(t + 1) * P], src).then_inc(scores.read_sem(step), 1)

            def QT(step, layer, b, u):
                if u == 0:
                    return
                dve.wait_ge(*scores.full(step))
                src = scores_ps[scores.buf(step)][:, :, :].bitcast(BF16).rearrange("p t (a c) -> p t a c", c=P)
                dst = qT[b][:, :, 2 * u * P:2 * (u + 1) * P].rearrange("p a (t c) -> p t a c", t=2)
                V_.tensor_copy(dst, src).then_inc(scores.read_sem(step), 1)

            def SMAX(step, layer, i, part, u):
                dve.wait_ge(*scores.full(step))
                ps = scores_ps[scores.buf(step)]
                if layer == 2:
                    src, dst = ps[:, :, :], mx[i % 2][:, part, 2 * u:2 * u + 2]
                else:
                    src = ps[:, :, 0:HG * C].rearrange("p t (h c) -> p t h c", c=C)
                    dst = mx[i % 2][:, 2 * u:2 * u + 2, :]
                V_.tensor_reduce(dst, src, AX.X, ALU.max).then_inc(scores.read_sem(step), 1)

            def MCH(step, layer, i):
                k = i % 2
                if layer == 0 and i == 0:
                    dve.wait_ge(zeroed, ZERO["mcat"])
                if layer or i >= 2:
                    old = ("MTR", layer, i - 2) if i >= 2 else ("MTR", layer - 1, NGRP - 2 + i)
                    dve.wait_ge(*misc.full(old))
                for u in range(2):
                    dve.wait_ge(*scores.read(("SMAX", layer, i, NKT[layer] - 1, u)))
                m = mx[k][:, :, :].rearrange("p t (a e) -> p (t a) e", e=2)
                r = mrs[k][:, :, :].rearrange("p t (a e) -> p (t a) e", e=2)
                c = mcat[k][:, :, :, 32:38].rearrange("p t a (e r) -> p (t a) e r", e=2)
                link(V_.tensor_scalar(c[:, :, :, 0], m, -1.0, None, ALU.mult))
                V_.scalar_tensor_tensor(out=r, in0=m, scalar=-1.0, in1=c[:, :, :, 0], op0=ALU.mult, op1=ALU.subtract)
                link(V_.scalar_tensor_tensor(out=c[:, :, :, 1], in0=m, scalar=-1.0, in1=c[:, :, :, 0],
                                             op0=ALU.mult, op1=ALU.subtract))
                tt(c[:, :, :, 2], r, c[:, :, :, 1], ALU.subtract).then_inc(done["MCH"], 1)

            def MTR(step, layer, i):
                if layer:
                    return
                b, g = divmod(i, GR)
                dve.wait_ge(*misc.full(step))
                for a in range(2):
                    src = small_ps(step)[64 * a + 32:64 * a + 38, 0:N // 2].bitcast(BF16)
                    last = V_.tensor_copy(qT[b][MROW:MROW + 6, 2 * g + a, :], src)
                last.then_inc(misc.read_sem(step), 1)

            def OC(step, layer, i):
                if layer != 1:
                    return
                dve.wait_ge(*after("PV", layer, i, 0))
                V_.transpose(oT[i % 2][:, :].rearrange("p (c r) -> p c r", c=N // VW),
                             out_ps[:, :].rearrange("p (m c) -> p c m", c=N // VW)).then_inc(done["OC"], 1)

            def OTR(step, layer, i):
                b, g = divmod(i, GR)
                if layer == 1:
                    dve.wait_ge(*after("OC", layer, i))
                    src = oT[i % 2][:, :].rearrange("p (c r) -> p c r", c=N // VW)
                    inv = rinv[i % GR][:, :, :].rearrange("p t j -> p (t j)")
                    link(V_.tensor_scalar(inv, src[:, :, DH], TINY, None, ALU.max))
                    link(V_.reciprocal(inv, inv))
                    dst = Z[b][:, g, :].rearrange("p (c d) -> p c d", d=DH)
                    link(tt(dst, src[:, :, 0:DH], inv.unsqueeze(2).broadcast_to([P, N // VW, DH]), ALU.mult))
                    return
                dve.wait_ge(*misc.full(step))
                src = small_ps(step).rearrange("p (t j c) -> p t j c", t=T, j=HG)
                link(V_.reciprocal(rinv[i % GR][:, :, :], src[:, :, :, DH]))
                dst = Z[b][:, :, g * HG * DH:(g + 1) * HG * DH].rearrange("p t (j d) -> p t j d", d=DH)
                tt(dst, src[:, :, :, 0:DH], rinv[i % GR][:, :, :].unsqueeze(3).broadcast_to([P, T, HG, DH]),
                   ALU.mult).then_inc(misc.read_sem(step), 1)

            def OP(step, layer, b):
                dve.wait_ge(*misc.full(step))
                src = small_ps(step).rearrange("p (t d) -> p t d", t=T)
                if layer == 0:
                    dve.wait_ge(shifted[b], 1)
                    tt(X[b][:, :, :], X[b][:, :, :], src, ALU.add).then_inc(misc.read_sem(step), 1)
                    dve.wait_ge(*misc.read(step))
                else:
                    dve.wait_ge(*after("NORM", "n4", b))
                    tt(ACC[b][:, :, :], XN[b][:, :, :], src, ALU.add).then_inc(misc.read_sem(step), 1)
                    dve.wait_ge(*misc.read(step))

            def Z1(step, b):
                dve.wait_ge(*after("NORM", "n2", b))
                link(tt(ACC[b][:, :, :], Z[b][:, :, :], XN[b][:, :, :], ALU.add))

            def FIN1(step, b):
                if b:
                    return
                dve.wait_ge(*after("NORM", "n3", b))
                link(tt(ACC[b][:, :, :], ACC[b][:, :, :], over_tiles(row["gamma"]), ALU.mult))
                dve.wait_ge(shifted[b], 2)
                tt(X[b][:, :, :], X[b][:, :, :], ACC[b][:, :, :], ALU.add).then_inc(done["FIN1"], 1)

            def first_max(b, src, oh, top, k):
                eq, best = g2[b], gv[b][:, k, :]
                link(V_.tensor_reduce(top, src, AX.X, ALU.max))
                link(tt(eq[:, :, :], src, top.unsqueeze(2).broadcast_to([P, T, E]), ALU.is_equal))
                link(tt(eq[:, :, :], eq[:, :, :], over_tiles(rev), ALU.mult))
                link(V_.tensor_reduce(best, eq[:, :, :], AX.X, ALU.max))
                link(tt(oh[:, :, :], over_tiles(rev), best.unsqueeze(2).broadcast_to([P, T, E]), ALU.is_equal))

            def per_expert(v):
                return v.unsqueeze(2).broadcast_to([P, T, E])

            def RT(step, b):
                dve.wait_ge(*misc.full(step))
                lg = gl[b][:, :, 0:E]
                V_.tensor_copy(lg, small_ps(step)[:, 0:T * E].rearrange("p (t e) -> p t e", t=T)).then_inc(misc.read_sem(step), 1)
                dve.wait_ge(*misc.read(step))
                first_max(b, lg, oh1[b], gv[b][:, 0, :], 7)
                link(V_.scalar_tensor_tensor(out=g1[b][:, :, :], in0=oh1[b][:, :, :], scalar=-BIG, in1=lg,
                                             op0=ALU.mult, op1=ALU.add))
                first_max(b, g1[b][:, :, :], oh2[b], gv[b][:, 1, :], 6)
                tt(gx[b][:, :, 0], gv[b][:, 1, :], gv[b][:, 0, :], ALU.subtract).then_inc(done["RT"], 1)

            def RTE(step, b):
                dve.wait_ge(*after("RTE", b))
                e2, w1_, w2_ = gex[b][:, :, 0], gv[b][:, 2, :], gv[b][:, 3, :]
                link(V_.tensor_scalar(w2_, e2, 1.0, None, ALU.add))
                link(V_.reciprocal(w1_, w2_))
                link(tt(w2_, e2, w1_, ALU.mult))
                tt(oh1[b][:, :, :], oh1[b][:, :, :], per_expert(w1_), ALU.mult)
                link(tt(oh2[b][:, :, :], oh2[b][:, :, :], per_expert(w2_), ALU.mult))
                link(tt(gw[b][:, :, :], oh1[b][:, :, :], oh2[b][:, :, :], ALU.add))

            def GT(step, b):
                dve.wait_ge(*misc.full(step))
                tt(gl[b][:, :, :], small_ps(step)[:, 0:T * GW].rearrange("p (t e) -> p t e", t=T),
                   over_tiles(row["gates"][:, 0:GW]), ALU.add).then_inc(misc.read_sem(step), 1)
                dve.wait_ge(*misc.read(step))
                lg = gl[b][:, :, 2:GW].rearrange("p t (g e) -> p t g e", g=2)
                gmax, emax = gv[b][:, 0, :], g1[b][:, :, 0:2]
                V_.tensor_reduce(gmax, gl[b][:, :, 0:2], AX.X, ALU.max)
                link(V_.tensor_reduce(emax, lg, AX.X, ALU.max))
                tt(gx[b][:, :, 0:2], gl[b][:, :, 0:2], gmax.unsqueeze(2).broadcast_to([P, T, 2]), ALU.subtract)
                tt(gx[b][:, :, 2:GW].rearrange("p t (g e) -> p t g e", g=2), lg,
                   emax.unsqueeze(3).broadcast_to([P, T, 2, E // 2]), ALU.subtract).then_inc(done["GT"], 1)

            def GTE(step, b):
                dve.wait_ge(*after("GTE", b))
                eg = gex[b][:, :, 0:2]
                sel, ex = g1[b][:, :, 0:2], gex[b][:, :, 2:GW]
                gsum, esum, inv = gv[b][:, 1, :], gv[b][:, 2, :], gv[b][:, 3, :]
                V_.tensor_reduce(gsum, eg, AX.X, ALU.add)
                tt(sel[:, :, 1], eg[:, :, 1], eg[:, :, 0], ALU.is_gt)
                link(tt(sel[:, :, 0], eg[:, :, 0], eg[:, :, 1], ALU.is_ge))
                ex4 = ex.rearrange("p t (g e) -> p t g e", g=2)
                link(tt(ex4, ex4, sel.unsqueeze(3).broadcast_to([P, T, 2, E // 2]), ALU.mult))
                link(V_.tensor_reduce(esum, ex, AX.X, ALU.add))
                link(tt(inv, gsum, esum, ALU.mult))
                link(V_.reciprocal(inv, inv))
                first_max(b, ex, oh1[b], gv[b][:, 4, :], 7)
                link(V_.scalar_tensor_tensor(out=g1[b][:, :, :], in0=oh1[b][:, :, :], scalar=-BIG, in1=ex,
                                             op0=ALU.mult, op1=ALU.add))
                first_max(b, g1[b][:, :, :], oh2[b], gv[b][:, 5, :], 6)
                link(tt(oh1[b][:, :, :], oh1[b][:, :, :], oh2[b][:, :, :], ALU.add))
                link(tt(gw[b][:, :, :], ex, oh1[b][:, :, :], ALU.mult))
                link(tt(gw[b][:, :, :], gw[b][:, :, :], per_expert(inv), ALU.mult))

            def FH(step, b, e):
                n = nth[step] - 1
                dve.wait_ge(*scores.read(step))
                if n >= 2:
                    dve.wait_ge(*probs.full(("FY", (n - 2) // E, (n - 2) % E)))
                src = relu[n % 2]
                tt(h2[n % 2][:, :, :].rearrange("p c n -> p (c n)"), src, src, ALU.mult).then_inc(done["FH"], 1)

            def accumulate(src, w, acc, t):
                return V_.scalar_tensor_tensor(out=acc[:, t, :], in0=src, scalar=w, in1=acc[:, t, :],
                                               op0=ALU.mult, op1=ALU.add)

            def FY(step, b, e):
                dve.wait_ge(*probs.full(step))
                if e:
                    dve.wait_ge(*probs.read(("FY", b, e - 1)))
                ps = probs_ps[probs.buf(step)]
                for t in range(T):
                    last = accumulate(ps[:, t * P:(t + 1) * P], gw[b][:, t, e:e + 1], X[b], t)
                last.then_inc(probs.read_sem(step), 1)
                if e == E - 1:
                    dve.wait_ge(*probs.read(step))

            def GH(step, b, w):
                n = nth[step] - 1
                dve.wait_ge(*scores.read(step, 0))
                dve.wait_ge(*scores.full(step, 1))
                if b:
                    dve.wait_ge(*(scores.full(("RO", 0, 1, 1)) if w else probs.full(("SO", 0))))
                src = scores_ps[scores.buf(step, 1)][:, :, :].rearrange("p c n -> p (c n)")
                tt(gh[w][:, :, :].rearrange("p c n -> p (c n)"), src, relu[n % 2],
                   ALU.mult).then_inc(scores.read_sem(step, 1), 1)

            def SO(step, b):
                dve.wait_ge(*probs.full(step))
                tt(ACC[b][:, :, :], XN[b][:, :, :], probs_ps[probs.buf(step)][:, :].rearrange("p (t d) -> p t d", t=T),
                   ALU.add).then_inc(probs.read_sem(step), 1)
                dve.wait_ge(*probs.read(step))

            def RO(step, b, pr, half):
                dve.wait_ge(*scores.full(step))
                ps = scores_ps[scores.buf(step)]
                for k in range(E // 2):
                    e = E // 2 * half + k
                    for u in range(2):
                        t = 2 * pr + u
                        last = accumulate(ps[:, u, k * P:(k + 1) * P], gw[b][:, t, e:e + 1], ACC[b], t)
                    if k < E // 2 - 1:
                        link(last)
                last.then_inc(scores.read_sem(step), 1)
                dve.wait_ge(*scores.read(step))
                if half == 1:
                    for t in (2 * pr, 2 * pr + 1):
                        last = V_.bn_stats(bn[b][:, t, :], ACC[b][:, t, :])
                    link(last)

            def OUT(step, b):
                dve.wait_ge(*after("NORMR", "r2", b))
                tt(ACC[b][:, :, :], ACC[b][:, :, :], X[b][:, :, :], ALU.add).then_inc(done["OUTV"], 1)

            parts = {"STAT": STAT, "NORM": NORM, "CKV": CKV, "SPLITC": SPLITC, "QP": QP, "SPLITQ": SPLITQ, "KV": KV, "SPLITK": SPLITK,
                     "KT": KT, "QT": QT, "SMAX": SMAX, "MCH": MCH, "MTR": MTR, "OC": OC, "OTR": OTR,
                     "OP": OP, "Z1": Z1, "FIN1": FIN1,
                     "RT": RT, "RTE": RTE, "GT": GT, "GTE": GTE, "FH": FH, "FY": FY, "GH": GH, "SO": SO, "RO": RO,
                     "OUT": OUT}
            link(V_.memset(kcat[:, :, :, :].bitcast(mybir.dt.uint32), 0))
            dve.wait_ge(loaded["consts"], 16)
            V_.tensor_copy(identb[:, :], ident).then_inc(consts_cast, 1)
            for step in schedule:
                if step[0] in parts:
                    parts[step[0]](step, *step[1:])


def rope_tables():
    inv = (1.0 / np.float32(10000.0) ** (np.arange(0, DH, 2, dtype=np.float32) / np.float32(DH))).astype(np.float32)
    ang = np.arange(N, dtype=np.float32)[:, None] * inv[None, :]
    cos = np.repeat(np.cos(ang), 2, axis=1)
    sin = np.repeat(np.sin(ang), 2, axis=1) * np.tile(np.array([-1.0, 1.0], np.float32), DH // 2)

    def lay(a):
        a = np.tile(a.astype(np.float32), (1, H)).reshape(T, P, P)
        return a.transpose(1, 0, 2).reshape(P, T * P)
    return lay(cos), lay(sin)


def kernel(**inputs):
    import concourse.bacc as bacc
    from concourse.bass_utils import run_bass_kernel_spmd

    a = {k: np.asarray(v) for k, v in inputs.items()}
    f32 = np.float32

    def chunks(w):
        return w.reshape(2, P, -1).transpose(1, 0, 2)

    x = a["x"].reshape(B, T, P, P).transpose(0, 2, 1, 3)
    wa = np.concatenate([a["L0_xattn_Wq"], a["L0_xattn_Wk"], a["L0_xattn_Wv"], a["L0_xattn_Wo"],
                         a["ctx_1024"].reshape(B * C, P).T], axis=1)
    cos, sin = rope_tables()
    consts = np.concatenate([np.eye(P, dtype=f32), cos, sin,
                             np.tile(np.arange(E, 0, -1, dtype=f32), (P, 1)), np.full((P, T), -0.5, f32)], axis=1)
    rows = np.concatenate([a["L0_xattn_bq"], a["L0_xattn_bk"], a["L0_xattn_bv"], a["L0_xattn_bo"],
                           a["L1_xattn_bq"], a["L1_xattn_bk"], a["L1_xattn_bv"], a["L1_xattn_gamma"],
                           a["L1_xattn_beta"], a["L1_ffn_norm1_w"], a["L1_ffn_norm2_w"],
                           a["L1_ffn_group_bias"], a["L1_ffn_expert_bias"], np.zeros(P - 2 - E, f32)])
    f0 = np.concatenate([a["L0_ffn_router_w"].T, a["L0_ffn_w1"].transpose(1, 0, 2).reshape(P, -1)], axis=1)
    f0y = a["L0_ffn_w2"].reshape(E, 2, P, P).transpose(2, 0, 1, 3).reshape(P, -1)
    dc = a["L1_ffn_Wk_c"].shape[1]
    wkvc = np.concatenate([a["L1_ffn_Wk_c"], a["L1_ffn_Wv_c"], np.zeros((P, P - 2 * dc), f32)], axis=1)
    wk2 = np.concatenate([a["L1_ffn_Wk"], np.zeros((P - dc, P), f32)], axis=0)
    wv2 = np.concatenate([np.zeros((dc, P), f32), a["L1_ffn_Wv"], np.zeros((P - 2 * dc, P), f32)], axis=0)
    wb = np.concatenate([a["L1_xattn_Wq"].T, a["L1_xattn_Wk"].T, a["L1_xattn_Wv"].T,
                         a["L1_ffn_Wq"], wkvc, wk2, wv2, a["L1_ffn_Wo"]], axis=1)
    w2x = a["L1_ffn_W2_experts"].reshape(E, 2, P, P).transpose(2, 1, 0, 3).reshape(P, -1)
    f1 = np.concatenate([a["L1_ffn_W_shared_in"], a["L1_ffn_W1_shared"],
                         chunks(a["L1_ffn_W_shared_out"]).reshape(P, -1), w2x,
                         a["L1_ffn_Wg_gate"], a["L1_ffn_We_gate"]], axis=1)

    nc = bacc.Bacc("TRN2", target_bir_lowering=False, num_devices=1)
    arrays, args = {}, []
    for name, arr in (("x", x), ("wa", wa), ("consts", consts), ("rows", rows), ("f0", f0), ("f0y", f0y),
                      ("wb", wb), ("f1", f1)):
        arr = np.ascontiguousarray(arr)
        arrays[f"in_{name}"] = arr
        args.append(nc.dram_tensor(f"in_{name}", arr.shape, F32, kind="ExternalInput").ap())
    out = nc.dram_tensor("out", (B, P, T, P), F32, kind="ExternalOutput").ap()
    build(nc, *args, out)
    r = run_bass_kernel_spmd(nc, [arrays], core_ids=[0])
    got = np.asarray(r.results[0]["out"])
    return got.transpose(0, 2, 1, 3).reshape(B, N, P)
```
